# Optimizing a Trainium2 kernel written in Bass

```python
import numpy as np
import jax
import jax.numpy as jnp

def _softmax(x, axis=-1):
    return jax.nn.softmax(x, axis=axis)

def _gelu(x):
    return jax.nn.gelu(x, approximate=True)

def _silu(x):
    return jax.nn.silu(x)

def _sigmoid(x):
    return jax.nn.sigmoid(x)

def _layernorm(x, axis=-1, eps=1e-05):
    m = jnp.mean(x, axis=axis, keepdims=True)
    v = jnp.var(x, axis=axis, keepdims=True)
    return (x - m) / jnp.sqrt(v + eps)

def _scatter_add(tgt, idx, src, axis=0):
    return tgt.at[idx].add(src)

def _segment_sum(src, seg, n):
    return jax.ops.segment_sum(src, seg, n)
kernel_name = 'mk_conv_preact_d4_conv_nchw128_r4_c3ca42'

def setup_inputs(seed: int=0):
    np.random.seed(seed)
    _w = jnp.asarray

    def _rec_inputs():
        import jax
        import jax.numpy as jnp
        _gk = jax.random.key(seed)
        x = -0.0005207 + 1.001 * jax.random.normal(jax.random.fold_in(_gk, 1), (4, 32, 16, 16), jnp.float32)
        return x
    x = _rec_inputs()

    def _L0_conv_setup():
        import jax, jax.numpy as jnp
        import numpy as np
        K = 7
        PAD = (K - 1) // 2
        EPS = 1e-05

        def _gen_kernel(x, w1, b1, bn_gamma, bn_beta, bn_mean, bn_var, w2, b2):
            f = jnp.einsum('oc,bchw->bohw', w1, x) + b1[None, :, None, None]
            scale = bn_gamma / jnp.sqrt(bn_var + EPS)
            f = f * scale[None, :, None, None] + (bn_beta - bn_mean * scale)[None, :, None, None]
            f = jax.nn.relu(f)
            return jnp.einsum('oc,bchw->bohw', w2, f) + b2[None, :, None, None]
        key = jax.random.key(seed)
        ks = jax.random.split(key, 5)
        B, C, H, W = (4, 32, 16, 16)
        Cr = C // 4
        x = jax.random.normal(ks[0], (B, C, H, W), dtype=jnp.float32)
        w1 = jax.random.normal(ks[1], (Cr, C), dtype=jnp.float32) * (1.0 / np.sqrt(C))
        b1 = jax.random.normal(ks[2], (Cr,), dtype=jnp.float32) * 0.01
        bn_gamma = jnp.ones((Cr,), dtype=jnp.float32)
        bn_beta = jnp.zeros((Cr,), dtype=jnp.float32)
        bn_mean = jnp.zeros((Cr,), dtype=jnp.float32)
        bn_var = jnp.ones((Cr,), dtype=jnp.float32)
        w2 = jax.random.normal(ks[3], (K * K, Cr), dtype=jnp.float32) * (1.0 / np.sqrt(Cr))
        b2 = jax.random.normal(ks[4], (K * K,), dtype=jnp.float32) * 0.01
        return {'x': x, 'w1': w1, 'b1': b1, 'bn_gamma': bn_gamma, 'bn_beta': bn_beta, 'bn_mean': bn_mean, 'bn_var': bn_var, 'w2': w2, 'b2': b2}
    _L0_conv_all = _L0_conv_setup()
    _L0_conv_in = {k: v for k, v in _L0_conv_all.items() if k in ('w1', 'b1', 'bn_gamma', 'bn_beta', 'bn_mean', 'bn_var', 'w2', 'b2')}
    del _L0_conv_all

    def _L1_conv_setup():
        import jax, jax.numpy as jnp
        import numpy as np
        B, C, H, W = (8, 32, 16, 16)
        KH = KW = 3
        K = KH * KW
        PAD = 1
        EPS = 1e-05

        def conv2d(x, w, b, stride=1, pad=1):
            y = jax.lax.conv_general_dilated(x, w, window_strides=(stride, stride), padding=[(pad, pad), (pad, pad)], dimension_numbers=('NCHW', 'OIHW', 'NCHW'))
            return y + b[None, :, None, None]

        def batchnorm(x, g, be, m, v):
            inv = jax.lax.rsqrt(v + EPS)
            return (x - m[None, :, None, None]) * (g * inv)[None, :, None, None] + be[None, :, None, None]

        def bilinear_gather(img, py, px):
            Bs, Cs, Hs, Ws = img.shape
            img_flat = img.reshape(Bs, Cs, Hs * Ws)
            y0 = jnp.floor(py)
            x0 = jnp.floor(px)
            wy = py - y0
            wx = px - x0

            def corner(yc, xc):
                valid = (yc >= 0) & (yc <= Hs - 1) & (xc >= 0) & (xc <= Ws - 1)
                yi = jnp.clip(yc, 0, Hs - 1).astype(jnp.int32)
                xi = jnp.clip(xc, 0, Ws - 1).astype(jnp.int32)
                flat = (yi * Ws + xi).reshape(Bs, 1, -1)
                g = jnp.take_along_axis(img_flat, flat, axis=2)
                g = g.reshape(Bs, Cs, *py.shape[1:])
                return g * valid[:, None].astype(img.dtype)
            v00 = corner(y0, x0)
            v01 = corner(y0, x0 + 1)
            v10 = corner(y0 + 1, x0)
            v11 = corner(y0 + 1, x0 + 1)
            w00 = ((1 - wy) * (1 - wx))[:, None]
            w01 = ((1 - wy) * wx)[:, None]
            w10 = (wy * (1 - wx))[:, None]
            w11 = (wy * wx)[:, None]
            return v00 * w00 + v01 * w01 + v10 * w10 + v11 * w11

        def deform_conv(x, offset, w, b):
            Bs, Cs, Hs, Ws = x.shape
            off = offset.reshape(Bs, K, 2, Hs, Ws)
            ky, kx = jnp.meshgrid(jnp.arange(KH), jnp.arange(KW), indexing='ij')
            ky = ky.reshape(K).astype(x.dtype)
            kx = kx.reshape(K).astype(x.dtype)
            oy = (jnp.arange(Hs) - PAD).astype(x.dtype)
            ox = (jnp.arange(Ws) - PAD).astype(x.dtype)
            py = off[:, :, 0] + ky[None, :, None, None] + oy[None, None, :, None]
            px = off[:, :, 1] + kx[None, :, None, None] + ox[None, None, None, :]
            sampled = bilinear_gather(x, py, px)
            out = jnp.einsum('bckhw,ock->bohw', sampled, w.reshape(w.shape[0], Cs, K))
            return out + b[None, :, None, None]
        key = jax.random.key(seed)
        ks = jax.random.split(key, 18)
        s = 1.0 / np.sqrt(C * K)
        return {'x': jax.random.normal(ks[0], (B, C, H, W), jnp.float32), 'conv1_w': jax.random.normal(ks[1], (C, C, 3, 3), jnp.float32) * s, 'conv1_b': jax.random.normal(ks[2], (C,), jnp.float32) * 0.01, 'bn1_g': 1.0 + 0.1 * jax.random.normal(ks[3], (C,), jnp.float32), 'bn1_b': 0.1 * jax.random.normal(ks[4], (C,), jnp.float32), 'bn1_m': 0.1 * jax.random.normal(ks[5], (C,), jnp.float32), 'bn1_v': jax.random.uniform(ks[6], (C,), jnp.float32, 0.5, 1.5), 'off_w': jax.random.normal(ks[7], (2 * K, C, 3, 3), jnp.float32) * (0.1 * s), 'off_b': jnp.zeros((2 * K,), jnp.float32), 'dconv_w': jax.random.normal(ks[8], (C, C, 3, 3), jnp.float32) * s, 'dconv_b': jax.random.normal(ks[9], (C,), jnp.float32) * 0.01, 'bn2_g': 1.0 + 0.1 * jax.random.normal(ks[10], (C,), jnp.float32), 'bn2_b': 0.1 * jax.random.normal(ks[11], (C,), jnp.float32), 'bn2_m': 0.1 * jax.random.normal(ks[12], (C,), jnp.float32), 'bn2_v': jax.random.uniform(ks[13], (C,), jnp.float32, 0.5, 1.5)}
    _L1_conv_all = _L1_conv_setup()
    _L1_conv_in = {k: v for k, v in _L1_conv_all.items() if k in ('conv1_w', 'conv1_b', 'bn1_g', 'bn1_b', 'bn1_m', 'bn1_v', 'off_w', 'off_b', 'dconv_w', 'dconv_b', 'bn2_g', 'bn2_b', 'bn2_m', 'bn2_v')}
    del _L1_conv_all

    def _L2_conv_setup():
        import jax, jax.numpy as jnp
        import numpy as np
        from jax import lax
        ITER = 5
        ALPHA = 2.0
        B, C, H, W = (16, 32, 16, 40)
        WSCALE = 0.02

        def _conv(x, w, pad_h, pad_w):
            return lax.conv_general_dilated(x, w, window_strides=(1, 1), padding=((pad_h, pad_h), (pad_w, pad_w)), dimension_numbers=('NCHW', 'OIHW', 'NCHW'))
        key = jax.random.key(seed)
        k0, k1, k2, k3, k4 = jax.random.split(key, 5)
        x = jax.random.normal(k0, (B, C, H, W), dtype=jnp.float32)
        w_d = jax.random.normal(k1, (ITER, C, C, 1, 9), dtype=jnp.float32) * WSCALE
        w_u = jax.random.normal(k2, (ITER, C, C, 1, 9), dtype=jnp.float32) * WSCALE
        w_r = jax.random.normal(k3, (ITER, C, C, 9, 1), dtype=jnp.float32) * WSCALE
        w_l = jax.random.normal(k4, (ITER, C, C, 9, 1), dtype=jnp.float32) * WSCALE
        return {'x': x, 'w_d': w_d, 'w_u': w_u, 'w_r': w_r, 'w_l': w_l}
    _L2_conv_all = _L2_conv_setup()
    _L2_conv_in = {k: v for k, v in _L2_conv_all.items() if k in ('w_d', 'w_u', 'w_r', 'w_l')}
    del _L2_conv_all

    def _L3_conv_setup():
        import jax, jax.numpy as jnp
        import numpy as np
        from jax import lax
        EPS_NORM = 1e-12
        KS = 3
        K2 = KS * KS
        MIN_CONN, MAX_CONN = (1, 8)
        NUM_GROUPS = 16
        GN_EPS = 1e-05

        def _unfold3x3_reflect(x):
            B, C, H, W = x.shape
            p = jnp.pad(x, ((0, 0), (0, 0), (1, 1), (1, 1)), mode='reflect')
            pats = [p[:, :, dy:dy + H, dx:dx + W] for dy in range(KS) for dx in range(KS)]
            return jnp.stack(pats, axis=2)

        def _df_counts(x):
            B = x.shape[0]
            avg = jnp.mean(x, axis=1, keepdims=True)
            kern = jnp.array([[0.0, -1.0, 0.0], [-1.0, 4.0, -1.0], [0.0, -1.0, 0.0]], dtype=x.dtype).reshape(1, 1, 3, 3)
            df = jnp.abs(lax.conv_general_dilated(avg, kern, window_strides=(1, 1), padding=((1, 1), (1, 1)), dimension_numbers=('NCHW', 'OIHW', 'NCHW')))
            dmin = df.reshape(B, -1).min(axis=1).reshape(B, 1, 1, 1)
            dmax = df.reshape(B, -1).max(axis=1).reshape(B, 1, 1, 1)
            dn = (df - dmin) / (dmax - dmin + 1e-08)
            return MIN_CONN + jnp.round(dn * (MAX_CONN - MIN_CONN))

        def _group_norm(x, w, b):
            B, C, H, W = x.shape
            g = x.reshape(B, NUM_GROUPS, -1)
            mu = g.mean(-1, keepdims=True)
            var = g.var(-1, keepdims=True)
            g = (g - mu) * lax.rsqrt(var + GN_EPS)
            return g.reshape(B, C, H, W) * w[None, :, None, None] + b[None, :, None, None]
        key = jax.random.key(seed)
        ks = jax.random.split(key, 7)
        B, C, H, W = (8, 32, 24, 24)
        return {'x': jax.random.normal(ks[0], (B, C, H, W), jnp.float32), 'gn_weight': jax.random.uniform(ks[1], (C,), jnp.float32, 0.5, 1.5), 'gn_bias': jax.random.normal(ks[2], (C,), jnp.float32) * 0.1, 'w1': jax.random.normal(ks[3], (2 * C, C), jnp.float32) * 0.02, 'b1': jax.random.normal(ks[4], (2 * C,), jnp.float32) * 0.02, 'w2': jax.random.normal(ks[5], (C, 2 * C), jnp.float32) * 0.02, 'b2': jax.random.normal(ks[6], (C,), jnp.float32) * 0.02}
    _L3_conv_all = _L3_conv_setup()
    _L3_conv_in = {k: v for k, v in _L3_conv_all.items() if k in ('gn_weight', 'gn_bias', 'w1', 'b1', 'w2', 'b2')}
    del _L3_conv_all
    return {'x': x, 'L0_conv_w1': _L0_conv_in['w1'], 'L0_conv_b1': _L0_conv_in['b1'], 'L0_conv_bn_gamma': _L0_conv_in['bn_gamma'], 'L0_conv_bn_beta': _L0_conv_in['bn_beta'], 'L0_conv_bn_mean': _L0_conv_in['bn_mean'], 'L0_conv_bn_var': _L0_conv_in['bn_var'], 'L0_conv_w2': _L0_conv_in['w2'], 'L0_conv_b2': _L0_conv_in['b2'], 'L1_conv_conv1_w': _L1_conv_in['conv1_w'], 'L1_conv_conv1_b': _L1_conv_in['conv1_b'], 'L1_conv_bn1_g': _L1_conv_in['bn1_g'], 'L1_conv_bn1_b': _L1_conv_in['bn1_b'], 'L1_conv_bn1_m': _L1_conv_in['bn1_m'], 'L1_conv_bn1_v': _L1_conv_in['bn1_v'], 'L1_conv_off_w': _L1_conv_in['off_w'], 'L1_conv_off_b': _L1_conv_in['off_b'], 'L1_conv_dconv_w': _L1_conv_in['dconv_w'], 'L1_conv_dconv_b': _L1_conv_in['dconv_b'], 'L1_conv_bn2_g': _L1_conv_in['bn2_g'], 'L1_conv_bn2_b': _L1_conv_in['bn2_b'], 'L1_conv_bn2_m': _L1_conv_in['bn2_m'], 'L1_conv_bn2_v': _L1_conv_in['bn2_v'], 'L2_conv_w_d': _L2_conv_in['w_d'], 'L2_conv_w_u': _L2_conv_in['w_u'], 'L2_conv_w_r': _L2_conv_in['w_r'], 'L2_conv_w_l': _L2_conv_in['w_l'], 'L3_conv_gn_weight': _L3_conv_in['gn_weight'], 'L3_conv_gn_bias': _L3_conv_in['gn_bias'], 'L3_conv_w1': _L3_conv_in['w1'], 'L3_conv_b1': _L3_conv_in['b1'], 'L3_conv_w2': _L3_conv_in['w2'], 'L3_conv_b2': _L3_conv_in['b2']}

def reference(x, L0_conv_w1, L0_conv_b1, L0_conv_bn_gamma, L0_conv_bn_beta, L0_conv_bn_mean, L0_conv_bn_var, L0_conv_w2, L0_conv_b2, L1_conv_conv1_w, L1_conv_conv1_b, L1_conv_bn1_g, L1_conv_bn1_b, L1_conv_bn1_m, L1_conv_bn1_v, L1_conv_off_w, L1_conv_off_b, L1_conv_dconv_w, L1_conv_dconv_b, L1_conv_bn2_g, L1_conv_bn2_b, L1_conv_bn2_m, L1_conv_bn2_v, L2_conv_w_d, L2_conv_w_u, L2_conv_w_r, L2_conv_w_l, L3_conv_gn_weight, L3_conv_gn_bias, L3_conv_w1, L3_conv_b1, L3_conv_w2, L3_conv_b2):
    import jax
    import jax.numpy as jnp

    def _L0_conv_ref(x, w1, b1, bn_gamma, bn_beta, bn_mean, bn_var, w2, b2):
        import jax, jax.numpy as jnp
        import numpy as np
        K = 7
        PAD = (K - 1) // 2
        EPS = 1e-05

        def _gen_kernel(x, w1, b1, bn_gamma, bn_beta, bn_mean, bn_var, w2, b2):
            f = jnp.einsum('oc,bchw->bohw', w1, x) + b1[None, :, None, None]
            scale = bn_gamma / jnp.sqrt(bn_var + EPS)
            f = f * scale[None, :, None, None] + (bn_beta - bn_mean * scale)[None, :, None, None]
            f = jax.nn.relu(f)
            return jnp.einsum('oc,bchw->bohw', w2, f) + b2[None, :, None, None]
        B, C, H, W = x.shape
        kernel = _gen_kernel(x, w1, b1, bn_gamma, bn_beta, bn_mean, bn_var, w2, b2)
        xp = jnp.pad(x, ((0, 0), (0, 0), (PAD, PAD), (PAD, PAD)))
        out = jnp.zeros_like(x)
        for i in range(K):
            for j in range(K):
                idx = i * K + j
                out = out + kernel[:, idx:idx + 1] * xp[:, :, i:i + H, j:j + W]
        return out

    def _L1_conv_ref(x, conv1_w, conv1_b, bn1_g, bn1_b, bn1_m, bn1_v, off_w, off_b, dconv_w, dconv_b, bn2_g, bn2_b, bn2_m, bn2_v):
        import jax, jax.numpy as jnp
        import numpy as np
        B, C, H, W = (8, 32, 16, 16)
        KH = KW = 3
        K = KH * KW
        PAD = 1
        EPS = 1e-05

        def conv2d(x, w, b, stride=1, pad=1):
            y = jax.lax.conv_general_dilated(x, w, window_strides=(stride, stride), padding=[(pad, pad), (pad, pad)], dimension_numbers=('NCHW', 'OIHW', 'NCHW'))
            return y + b[None, :, None, None]

        def batchnorm(x, g, be, m, v):
            inv = jax.lax.rsqrt(v + EPS)
            return (x - m[None, :, None, None]) * (g * inv)[None, :, None, None] + be[None, :, None, None]

        def bilinear_gather(img, py, px):
            Bs, Cs, Hs, Ws = img.shape
            img_flat = img.reshape(Bs, Cs, Hs * Ws)
            y0 = jnp.floor(py)
            x0 = jnp.floor(px)
            wy = py - y0
            wx = px - x0

            def corner(yc, xc):
                valid = (yc >= 0) & (yc <= Hs - 1) & (xc >= 0) & (xc <= Ws - 1)
                yi = jnp.clip(yc, 0, Hs - 1).astype(jnp.int32)
                xi = jnp.clip(xc, 0, Ws - 1).astype(jnp.int32)
                flat = (yi * Ws + xi).reshape(Bs, 1, -1)
                g = jnp.take_along_axis(img_flat, flat, axis=2)
                g = g.reshape(Bs, Cs, *py.shape[1:])
                return g * valid[:, None].astype(img.dtype)
            v00 = corner(y0, x0)
            v01 = corner(y0, x0 + 1)
            v10 = corner(y0 + 1, x0)
            v11 = corner(y0 + 1, x0 + 1)
            w00 = ((1 - wy) * (1 - wx))[:, None]
            w01 = ((1 - wy) * wx)[:, None]
            w10 = (wy * (1 - wx))[:, None]
            w11 = (wy * wx)[:, None]
            return v00 * w00 + v01 * w01 + v10 * w10 + v11 * w11

        def deform_conv(x, offset, w, b):
            Bs, Cs, Hs, Ws = x.shape
            off = offset.reshape(Bs, K, 2, Hs, Ws)
            ky, kx = jnp.meshgrid(jnp.arange(KH), jnp.arange(KW), indexing='ij')
            ky = ky.reshape(K).astype(x.dtype)
            kx = kx.reshape(K).astype(x.dtype)
            oy = (jnp.arange(Hs) - PAD).astype(x.dtype)
            ox = (jnp.arange(Ws) - PAD).astype(x.dtype)
            py = off[:, :, 0] + ky[None, :, None, None] + oy[None, None, :, None]
            px = off[:, :, 1] + kx[None, :, None, None] + ox[None, None, None, :]
            sampled = bilinear_gather(x, py, px)
            out = jnp.einsum('bckhw,ock->bohw', sampled, w.reshape(w.shape[0], Cs, K))
            return out + b[None, :, None, None]
        out = conv2d(x, conv1_w, conv1_b, stride=1, pad=1)
        out = jax.nn.relu(batchnorm(out, bn1_g, bn1_b, bn1_m, bn1_v))
        offset = conv2d(out, off_w, off_b, stride=1, pad=1)
        out = deform_conv(out, offset, dconv_w, dconv_b)
        out = jax.nn.relu(batchnorm(out, bn2_g, bn2_b, bn2_m, bn2_v))
        return out

    def _L2_conv_ref(x, w_d, w_u, w_r, w_l):
        import jax, jax.numpy as jnp
        import numpy as np
        from jax import lax
        ITER = 5
        ALPHA = 2.0
        B, C, H, W = (16, 32, 16, 40)
        WSCALE = 0.02

        def _conv(x, w, pad_h, pad_w):
            return lax.conv_general_dilated(x, w, window_strides=(1, 1), padding=((pad_h, pad_h), (pad_w, pad_w)), dimension_numbers=('NCHW', 'OIHW', 'NCHW'))
        y = x
        h, w = y.shape[-2:]
        for i in range(ITER):
            s = h // 2 ** (ITER - i)
            y = y + ALPHA * jax.nn.relu(_conv(jnp.roll(y, -s, axis=2), w_d[i], 0, 4))
        for i in range(ITER):
            s = h // 2 ** (ITER - i)
            y = y + ALPHA * jax.nn.relu(_conv(jnp.roll(y, s, axis=2), w_u[i], 0, 4))
        for i in range(ITER):
            s = w // 2 ** (ITER - i)
            y = y + ALPHA * jax.nn.relu(_conv(jnp.roll(y, -s, axis=3), w_r[i], 4, 0))
        for i in range(ITER):
            s = w // 2 ** (ITER - i)
            y = y + ALPHA * jax.nn.relu(_conv(jnp.roll(y, s, axis=3), w_l[i], 4, 0))
        return y

    def _L3_conv_ref(x, gn_weight, gn_bias, w1, b1, w2, b2):
        import jax, jax.numpy as jnp
        import numpy as np
        from jax import lax
        EPS_NORM = 1e-12
        KS = 3
        K2 = KS * KS
        MIN_CONN, MAX_CONN = (1, 8)
        NUM_GROUPS = 16
        GN_EPS = 1e-05

        def _unfold3x3_reflect(x):
            B, C, H, W = x.shape
            p = jnp.pad(x, ((0, 0), (0, 0), (1, 1), (1, 1)), mode='reflect')
            pats = [p[:, :, dy:dy + H, dx:dx + W] for dy in range(KS) for dx in range(KS)]
            return jnp.stack(pats, axis=2)

        def _df_counts(x):
            B = x.shape[0]
            avg = jnp.mean(x, axis=1, keepdims=True)
            kern = jnp.array([[0.0, -1.0, 0.0], [-1.0, 4.0, -1.0], [0.0, -1.0, 0.0]], dtype=x.dtype).reshape(1, 1, 3, 3)
            df = jnp.abs(lax.conv_general_dilated(avg, kern, window_strides=(1, 1), padding=((1, 1), (1, 1)), dimension_numbers=('NCHW', 'OIHW', 'NCHW')))
            dmin = df.reshape(B, -1).min(axis=1).reshape(B, 1, 1, 1)
            dmax = df.reshape(B, -1).max(axis=1).reshape(B, 1, 1, 1)
            dn = (df - dmin) / (dmax - dmin + 1e-08)
            return MIN_CONN + jnp.round(dn * (MAX_CONN - MIN_CONN))

        def _group_norm(x, w, b):
            B, C, H, W = x.shape
            g = x.reshape(B, NUM_GROUPS, -1)
            mu = g.mean(-1, keepdims=True)
            var = g.var(-1, keepdims=True)
            g = (g - mu) * lax.rsqrt(var + GN_EPS)
            return g.reshape(B, C, H, W) * w[None, :, None, None] + b[None, :, None, None]
        B, C, H, W = x.shape
        P = H * W
        counts = lax.stop_gradient(_df_counts(x))
        kvals = jnp.minimum(counts, K2).astype(jnp.int32).reshape(B, 1, P)
        patches = _unfold3x3_reflect(x).reshape(B, C, K2, P)
        xc = x.reshape(B, C, P)
        cn = xc / jnp.maximum(jnp.linalg.norm(xc, axis=1, keepdims=True), EPS_NORM)
        pn = patches / jnp.maximum(jnp.linalg.norm(patches, axis=1, keepdims=True), EPS_NORM)
        sim = jnp.einsum('bcp,bckp->bkp', cn, pn)
        order = jnp.argsort(-sim, axis=1)
        top_sim = jnp.take_along_axis(sim, order, axis=1)
        mask = jnp.arange(K2)[None, :, None] < kvals
        wts = jnp.exp(top_sim) * mask
        wts = wts / jnp.sum(wts, axis=1, keepdims=True)
        pat_sorted = jnp.take_along_axis(patches, order[:, None, :, :], axis=2)
        out = jnp.einsum('bckp,bkp->bcp', pat_sorted, wts).reshape(B, C, H, W)
        enhanced = out + _group_norm(x, gn_weight, gn_bias)
        h = jax.nn.relu(jnp.einsum('oi,bihw->bohw', w1, enhanced) + b1[None, :, None, None])
        ffn = jnp.einsum('oi,bihw->bohw', w2, h) + b2[None, :, None, None]
        return enhanced + ffn

    def _gn(v, G=32, eps=1e-05):
        B_, C_, H_, W_ = v.shape
        g = v.reshape(B_, G, C_ // G, H_, W_)
        m = jnp.mean(g, axis=(2, 3, 4), keepdims=True)
        s = jnp.var(g, axis=(2, 3, 4), keepdims=True)
        return ((g - m) / jnp.sqrt(s + eps)).reshape(v.shape)

    def _ln_c(v, eps=1e-06):
        m = jnp.mean(v, axis=1, keepdims=True)
        s = jnp.var(v, axis=1, keepdims=True)
        return (v - m) / jnp.sqrt(s + eps)

    def _ln_t(v, eps=1e-05):
        m = jnp.mean(v, axis=-1, keepdims=True)
        s = jnp.var(v, axis=-1, keepdims=True)
        return (v - m) / jnp.sqrt(s + eps)

    def _to_tokens(v):
        B_, C_, H_, W_ = v.shape
        return v.reshape(B_, C_, H_ * W_).transpose(0, 2, 1)

    def _from_tokens(t, like):
        B_, C_, H_, W_ = like.shape
        return t.transpose(0, 2, 1).reshape(B_, C_, H_, W_)
    x = x + _L0_conv_ref(_gn(x), L0_conv_w1, L0_conv_b1, L0_conv_bn_gamma, L0_conv_bn_beta, L0_conv_bn_mean, L0_conv_bn_var, L0_conv_w2, L0_conv_b2)
    x = x + _L1_conv_ref(_gn(x), L1_conv_conv1_w, L1_conv_conv1_b, L1_conv_bn1_g, L1_conv_bn1_b, L1_conv_bn1_m, L1_conv_bn1_v, L1_conv_off_w, L1_conv_off_b, L1_conv_dconv_w, L1_conv_dconv_b, L1_conv_bn2_g, L1_conv_bn2_b, L1_conv_bn2_m, L1_conv_bn2_v)
    x = x + _L2_conv_ref(_gn(x), L2_conv_w_d, L2_conv_w_u, L2_conv_w_r, L2_conv_w_l)
    x = x + _L3_conv_ref(_gn(x), L3_conv_gn_weight, L3_conv_gn_bias, L3_conv_w1, L3_conv_b1, L3_conv_w2, L3_conv_b2)
    return x

_drawn_inputs = setup_inputs


def setup_inputs(seed=0):
    import zlib

    import numpy as np

    out = dict(_drawn_inputs(seed))
    spreads = {'L0_conv_bn_gamma': (1.0, 0.6),
     'L0_conv_bn_beta': (0.0, 0.8),
     'L0_conv_bn_mean': (0.0, 0.8),
     'L0_conv_bn_var': (1.0, 0.6),
     'L1_conv_off_b': (0.0, 0.8)}
    factors = {'L0_conv_b1': 8.0,
     'L0_conv_b2': 8.0,
     'L1_conv_conv1_w': 7.039,
     'L1_conv_conv1_b': 8.0,
     'L1_conv_bn1_g': 8.0,
     'L1_conv_bn1_b': 8.0,
     'L1_conv_bn1_m': 8.0,
     'L1_conv_bn1_v': 8.0,
     'L1_conv_off_w': 8.0,
     'L1_conv_dconv_w': 6.441,
     'L1_conv_dconv_b': 200.0,
     'L1_conv_bn2_g': 8.0,
     'L1_conv_bn2_b': 64.0,
     'L1_conv_bn2_m': 39.866,
     'L1_conv_bn2_v': 8.0,
     'L3_conv_gn_weight': 8.0,
     'L3_conv_gn_bias': 56.661,
     'L3_conv_w1': 8.0,
     'L3_conv_b1': 200.0,
     'L3_conv_w2': 8.0,
     'L3_conv_b2': 200.0}
    for name, (base, spread) in spreads.items():
        noise = np.random.default_rng([zlib.crc32(name.encode()), seed]).standard_normal(out[name].shape)
        drawn = base * np.exp(spread * noise) if base else spread * noise
        out[name] = jnp.asarray(drawn.astype(out[name].dtype))
    for name, factor in factors.items():
        out[name] = (out[name] * factor).astype(out[name].dtype)
    return out
```

```python
from contextlib import ExitStack

import concourse.bass as bass
from concourse import mybir

F32 = mybir.dt.float32
ALU = mybir.AluOpType
ACT = mybir.ActivationFunctionType
AX = mybir.AxisListType

B, C, H, W = 4, 32, 16, 16
P = B * C
HW = H * W
Q = 32
RANK = 8
K7 = 7
FILTERS = RANK + 1
HALO7 = 8 + K7 - 1
ROWS7 = 11
TAPS = 9
PAD = H + 2
OFFS = 2 * TAPS * B
NB = 10
STEPS = 20
MAXROLL = 8
YW = 4 * H + 2 * 4 * MAXROLL
Y0 = 4 * MAXROLL
MAPS = 5
ROUND = 12582912.0
KNN = 9
LINE = 96
LINES = 3
G = LINES * B
SPAN = LINE * LINES

VAR, GAMMA, BIAS, MEAN, BETA = (NB * i for i in range(5))
W1R = 5 * NB
GN_W, GN_B, FFN_B2, FFN_B1, OFF_B, EPS, EPS4 = (W1R + RANK + i for i in range(7))
NPAR = EPS4 + 1
C_AVG, C_PAIR, C_MAPS, C_BASE, C_IOTA = 0, 128, 256, 256 + MAPS * 20, 256 + MAPS * 20 + 2 * OFFS
NCST = C_IOTA + 16
W_CONV, W_OFF, W_DEF = 0, TAPS * P, TAPS * P + TAPS * OFFS
NW1 = W_DEF + TAPS * P

POOL_UNITS = {(2, 1), (4, 1), (6, 1), (8, 0)}
VECTOR_DRAINS = {3, 11, 19, 27, 33, 35}


def rolls(step):
    s = H // 2 ** (5 - step % 5)
    return 4 * s if step // 5 % 2 == 0 else -4 * s


def build(nc, x_d, par_d, ident_d, taps_d, wa_d, wb_d, wc_d, cst_d, sel_d, out_d):
    with ExitStack() as ctx:
        def sb(name, shape, dt=F32):
            return ctx.enter_context(nc.sbuf_tensor(name, shape, dt))

        def sem(name):
            return ctx.enter_context(nc.semaphore(name))

        def view(ap, *dims):
            return bass.AP(ap.tensor, ap.offset, [list(ap.ap[0])] + [list(d) for d in dims])

        ps = ctx.enter_context(nc.psum_tensor("ps", [P, 8, 512], F32))

        par = sb("par", [P, NPAR])
        ident = sb("ident", [P, P])
        cst = sb("cst", [P, NCST])
        sel = sb("sel", [36, KNN * P])
        taps7 = sb("taps7", [P, FILTERS, HALO7, W])
        w1blk = sb("w1blk", [P, RANK, P])
        w1s = sb("w1s", [P, RANK])
        wa = sb("wa", [P, NW1])
        wband = sb("wband", [P, STEPS, 12, C])
        wc = sb("wc", [P, 4 * P])
        bnstd = sb("bnstd", [P, NB])
        bnscale = sb("bnscale", [P, NB])
        bnrec = sb("bnrec", [P, NB])
        bnshift = sb("bnshift", [P, NB])
        bnt = sb("bnt", [P, NB])
        x0 = sb("x0", [P, HW])
        x1 = sb("x1", [P, HW])
        x2 = sb("x2", [P, HW])
        x3 = sb("x3", [P, HW])
        st6 = sb("st6", [P, 5, 6])
        mv = sb("mv", [P, 5, 2])
        std = sb("std", [P, 5])
        rstd = sb("rstd", [P, 5])
        g0 = sb("g0", [P, HW])
        g0t = sb("g0t", [P, 2, P])
        hid = sb("hid", [P, RANK, HW])
        prod0 = sb("prod0", [P, 4, 2, HW])
        acc0 = sb("acc0", [P, 2, HW])
        xs0 = sb("xs0", [P, HW])
        xf0 = sb("xf0", [P, HW])
        g1p = sb("g1p", [P, PAD, PAD])
        a1p = sb("a1p", [P, PAD, PAD])
        a1 = sb("a1", [P, HW])
        offs = sb("offs", [OFFS, HW])
        pos = sb("pos", [P, 2, OFFS])
        hats = sb("hats", [P, TAPS, 2, 8, 16])
        mixed = sb("mixed", [P, 2, TAPS * P])
        st = sb("st", [P, 2, 2, B, HW])
        s = sb("s", [P, 2, 2, B, HW])
        r1 = sb("r1", [P, HW])
        nmr = sb("nmr", [P, 1])
        yt = sb("yt", [P, 4, YW])
        ytb = sb("ytb", [P, 4, YW])
        yz = sb("yz", [P, 2, P])
        t3 = sb("t3", [P, HW])
        g3p = sb("g3p", [P, PAD * PAD])
        avp = sb("avp", [P, PAD, PAD])
        maps = sb("maps", [P, MAPS, PAD * PAD])
        sims0 = sb("sims0", [MAPS * B, SPAN + 2 * PAD + 2])
        lap = sb("lap", [P, 3, HW])
        df = sb("df", [P, 2, HW])
        mm = sb("mm", [P, 4])
        kn = sb("kn", [P, SPAN])
        nn = sb("nn", [LINE, KNN, G])
        nc_ = sb("nc_", [LINE, KNN, G])
        pr = sb("pr", [LINE, KNN, G])
        rec = sb("rec", [LINE, KNN, G])
        sim = sb("sim", [LINE, KNN, G])
        ex = sb("ex", [LINE, KNN, G])
        cmp = sb("cmp", [LINE, KNN, KNN, G])
        rank = sb("rank", [LINE, KNN, G])
        keep = sb("keep", [LINE, KNN, G])
        wts = sb("wts", [LINE, KNN, G])
        wn = sb("wn", [LINE, LINES, KNN * B])
        den = sb("den", [LINE, G])
        rden = sb("rden", [LINE, G])
        wc36 = sb("wc36", [36, SPAN])
        prod3 = sb("prod3", [P, KNN, HW])
        acc3 = sb("acc3", [P, 3, 2, HW])
        sum3 = sb("sum3", [P, 2, HW])
        gn = sb("gn", [P, 12])
        gnout = sb("gnout", [P, HW])
        enh = sb("enh", [P, HW])
        hff = sb("hff", [P, 2, HW])
        xe = sb("xe", [P, HW])
        y = sb("y", [P, HW])

        x_loaded, par_loaded, ident_loaded = sem("x_loaded"), sem("par_loaded"), sem("ident_loaded")
        taps_zeroed, taps_loaded = sem("taps_zeroed"), sem("taps_loaded")
        wa_loaded, band_zeroed, band_loaded = sem("wa_loaded"), sem("band_zeroed"), sem("band_loaded")
        cst_loaded, wc_loaded, stored = sem("cst_loaded"), sem("wc_loaded"), sem("stored")
        v_step, a_step, g_step = sem("v_step"), sem("a_step"), sem("g_step")
        bn_scaled, bn_std, w1_ready = sem("bn_scaled"), sem("bn_std"), sem("w1_ready")
        bn_ready, borders_zeroed = sem("bn_ready"), sem("borders_zeroed")
        var_ready, std_ready = sem("var_ready"), sem("std_ready")
        g0_ready, g0_turned, g0t_ready = sem("g0_ready"), sem("g0_turned"), sem("g0t_ready")
        hid_done, hid_ready, filt_done = sem("hid_done"), sem("hid_ready"), sem("filt_done")
        g1_ready, conv_done, a1_ready = sem("g1_ready"), sem("conv_done"), sem("a1_ready")
        off_done, offs_ready, off_turned = sem("off_done"), sem("offs_ready"), sem("off_turned")
        a1_packed = sem("a1_packed")
        mixed_done, mixed_ready = sem("mixed_done"), sem("mixed_ready")
        pos_ready, dist_ready = sem("pos_ready"), sem("dist_ready")
        absd_ready, hats_ready = sem("absd_ready"), sem("hats_ready")
        prod_v, prod_g = sem("prod_v"), sem("prod_g")
        turned, drained_a, drained_v = sem("turned"), sem("drained_a"), sem("drained_v")
        sampled, r1_ready, x2_ready = sem("sampled"), sem("r1_ready"), sem("x2_ready")
        norm2_ready, nmr_ready = sem("norm2_ready"), sem("nmr_ready")
        y_laid = sem("y_laid")
        y_turned, yz_a, yz_v = sem("y_turned"), sem("yz_a"), sem("yz_v")
        z_done, y_updated, yt_turned = sem("z_done"), sem("y_updated"), sem("yt_turned")
        yt_main, yt_border = sem("yt_main"), sem("yt_border")
        t_laid = sem("t_laid")
        g3_ready, g3p_ready, sq_ready, map_v, map_g = (
            sem("g3_ready"), sem("g3p_ready"), sem("sq_ready"), sem("map_v"), sem("map_g"))
        avg_done, av_ready, lap_ready = sem("avg_done"), sem("av_ready"), sem("lap_ready")
        maps_done, sims0_ready, sims_turned = sem("maps_done"), sem("sims0_ready"), sem("sims_turned")
        kn_ready, kn_turned = sem("kn_ready"), sem("kn_turned")
        nn_ready, sim_ready, ex_ready = sem("nn_ready"), sem("sim_ready"), sem("ex_ready")
        gn_in, gn_paired, gn_var, gn_std = sem("gn_in"), sem("gn_paired"), sem("gn_var"), sem("gn_std")
        wn_ready, wn_turned, wc36_ready = sem("wn_ready"), sem("wn_turned"), sem("wc36_ready")
        wb_done, p3_ready, s3_ready = sem("wb_done"), sem("p3_ready"), sem("s3_ready")
        enh_ready, h_done, h_a, h_v = sem("enh_ready"), sem("h_done"), sem("h_a"), sem("h_v")
        ffn_done, xe_ready, y_ready = sem("ffn_done"), sem("xe_ready"), sem("y_ready")

        def inner(padded):
            return padded[:, 1:1 + H, 1:1 + W]

        def rows(flat):
            return flat.rearrange("p (h w) -> p h w", w=W)

        g3v = g3p[:, :].rearrange("p (h w) -> p h w", w=PAD)

        def to_columns(b, j):
            return (view(x2[Q * b:Q * b + Q, j:j + 1], (4, 4), (W, H)),
                    view(yt[Q * j:Q * j + Q, 0, Y0 + b:Y0 + b + 1], (YW, 4), (4, H)))

        def to_rows(j, i):
            return (view(yt[Q * j:Q * j + Q, 0, Y0 + 4 * i:Y0 + 4 * i + 1], (YW, 4), (16, 4), (1, 4)),
                    view(ytb[Q * i:Q * i + Q, 0, Y0 + 4 * j:Y0 + 4 * j + 1], (16, 4), (YW, 4), (1, 4)))

        def to_image(i, b):
            return (view(ytb[Q * i:Q * i + Q, 0, Y0 + b:Y0 + b + 1], (YW, 4), (4, W)),
                    view(t3[Q * b:Q * b + Q, W * i:W * i + 1], (4 * W, 4), (1, W)))

        MOVES = [(i, j) for i in range(4) for j in range(4)]
        V_MOVES, A_MOVES, G_MOVES = MOVES[0:7], MOVES[7:11], MOVES[11:16]

        def bands(step):
            return yt if step < STEPS // 2 else ytb

        def mirrored(t, z):
            return view(t[:, z, Y0:Y0 + 1], ((3 - 2 * z) * YW, 2), (1, 4 * H))

        BORDERED = [0]
        for n in range(1, STEPS + 1):
            needed = n < STEPS and rolls(n) != 0
            BORDERED.append(BORDERED[-1] + 2 * needed)

        block = ctx.enter_context(nc.Block())

        @block.sync
        def _(sp):
            sp.dma_start(x0[:, :], x_d).then_inc(x_loaded, 16)
            sp.dma_start(par[:, :], par_d).then_inc(par_loaded, 16)
            sp.wait_ge(taps_zeroed, 1)
            for n in range(8):
                sp.dma_start(taps7[16 * n:16 * n + 16, :, n:n + K7, :], taps_d).then_inc(taps_loaded, 16)
            sp.dma_start(wa[:, 0:W_DEF], wa_d[:, 0:W_DEF]).then_inc(wa_loaded, 16)
            sp.dma_start(wa[:, W_DEF:NW1], wa_d[:, W_DEF:NW1]).then_inc(wa_loaded, 16)
            sp.wait_ge(band_zeroed, 1)
            for a in range(4):
                sp.dma_start(wband[Q * a:Q * a + Q, :, a:a + TAPS, :], wb_d).then_inc(band_loaded, 16)
            sp.dma_start(wc[:, :], wc_d).then_inc(wc_loaded, 16)
            sp.dma_start(sel[:, :], sel_d).then_inc(wc_loaded, 16)
            sp.wait_ge(y_ready, 1)
            sp.dma_start(out_d, y[:, :]).then_inc(stored, 16)
            sp.wait_ge(stored, 16)

        @block.gpsimd
        def _(g):
            own = [0]

            def step(ins):
                own[0] += 1
                ins.then_inc(g_step, 1)
                g.wait_ge(g_step, own[0])

            g.memset(w1blk[:, :, :], 0.0).then_inc(g_step, 1)
            own[0] += 1
            g.wait_ge(bn_scaled, 1)
            g.wait_ge(g_step, own[0])
            for b in range(B):
                part = slice(Q * b, Q * b + Q)
                g.tensor_copy(w1blk[part, :, part], view(w1s[part, :], (1, RANK), (0, Q))).then_inc(w1_ready, 1)
            for a in range(4):
                part = slice(Q * a, Q * a + Q)
                if a > 0:
                    g.memset(wband[part, :, 0:a, :], 0.0).then_inc(g_step, 1)
                    own[0] += 1
                if a < 3:
                    g.memset(wband[part, :, a + TAPS:12, :], 0.0).then_inc(g_step, 1)
                    own[0] += 1
            g.wait_ge(g_step, own[0])
            g.memset(g1p[:, :, :], 0.0).then_inc(band_zeroed, 1)
            g.memset(a1p[:, :, :], 0.0).then_inc(g_step, 1)
            g.memset(avp[:, :, :], 0.0).then_inc(g_step, 1)
            own[0] += 2
            g.wait_ge(g_step, own[0])
            g.memset(kn[:, :], 1.0).then_inc(g_step, 1)
            g.memset(sims0[:, :], 0.0).then_inc(g_step, 1)
            own[0] += 2
            g.wait_ge(g_step, own[0])
            g.memset(view(cmp[:, 0, 0, :], ((KNN + 1) * G, KNN), (1, G)), 0.0).then_inc(borders_zeroed, 1)

            g.wait_ge(a1_ready, 1)
            g.tensor_copy(rows(a1[:, :]), inner(a1p)).then_inc(a1_packed, 1)
            g.wait_ge(cst_loaded, 16)
            g.wait_ge(pos_ready, 1)
            for c in (1, 2):
                for half in range(2):
                    g.tensor_tensor(hats[:, 3 * c:3 * c + 3, half, :, :],
                                    view(pos[:, half, 24 * c:24 * c + 1], (8, 3), (1, 8), (0, 16)),
                                    view(cst[:, C_IOTA:C_IOTA + 1], (0, 3), (0, 8), (1, 16)),
                                    ALU.subtract).then_inc(dist_ready, 1)
            for k, half in sorted(POOL_UNITS):
                g.wait_ge(hats_ready, k // 3 + 1)
                if k >= 2:
                    g.wait_ge(turned, 4 * (k - 1))
                g.tensor_tensor(
                    st[:, k % 2, half, :, :].rearrange("p b (y x) -> p b y x", x=W),
                    view(hats[:, k, half, 0, 0:1], (16, B), (1, H), (0, W)),
                    view(hats[:, k, half, 4, 0:1], (16, B), (0, H), (1, W)), ALU.mult).then_inc(prod_g, 1)

            g.wait_ge(norm2_ready, 1)
            for b, j in G_MOVES:
                src, dst = to_columns(b, j)
                g.tensor_scalar(dst, src, mv[Q * b:Q * b + Q, 2, 0:1], rstd[Q * b:Q * b + Q, 2:3],
                                ALU.subtract, ALU.mult).then_inc(y_laid, 1)
            g.wait_ge(yt_main, 2 * STEPS // 2)
            for i, j in G_MOVES:
                src, dst = to_rows(i, j)
                g.tensor_copy(dst, src).then_inc(y_laid, 1)
            g.wait_ge(yt_main, 2 * STEPS)
            for i, j in G_MOVES:
                src, dst = to_image(i, j)
                g.tensor_copy(dst, src).then_inc(t_laid, 1)

            g.wait_ge(g3p_ready, 1)
            g.tensor_tensor(maps[:, 4, 0:305], g3p[:, 0:305], g3p[:, 19:324], ALU.mult).then_inc(map_g, 1)
            g.wait_ge(av_ready, 1)
            g.tensor_tensor(rows(lap[:, 0, :]), avp[:, 0:H, 1:1 + W], avp[:, 2:2 + H, 1:1 + W],
                            ALU.add).then_inc(g_step, 1)
            g.tensor_tensor(rows(lap[:, 1, :]), avp[:, 1:1 + H, 0:W], avp[:, 1:1 + H, 2:2 + W],
                            ALU.add).then_inc(g_step, 1)
            own[0] += 2
            g.wait_ge(g_step, own[0])
            g.tensor_tensor(lap[:, 2, :], lap[:, 0, :], lap[:, 1, :], ALU.add).then_inc(lap_ready, 1)
            g.wait_ge(p3_ready, 2)
            g.tensor_tensor(acc3[:, 0, :, :], prod3[:, 0:2, :], prod3[:, 2:4, :], ALU.add).then_inc(s3_ready, 1)
            g.wait_ge(enh_ready, 1)
            g.tensor_tensor(xe[:, :], enh[:, :], x3[:, :], ALU.add).then_inc(xe_ready, 1)

        @block.scalar
        def _(a):
            a.dma_start(ident[:, :], ident_d).then_inc(ident_loaded, 16)
            a.dma_start(cst[:, :], cst_d).then_inc(cst_loaded, 16)

            def norm_std(n, eps_col, scale):
                a.wait_ge(var_ready, n + 1)
                a.activation(std[:, n:n + 1], mv[:, n, 1:2], ACT.Sqrt, bias=par[:, eps_col:eps_col + 1],
                             scale=scale).then_inc(std_ready, 1)

            a.wait_ge(par_loaded, 16)
            a.activation(bnstd[:, :], par[:, VAR:VAR + NB], ACT.Sqrt,
                         bias=par[:, EPS:EPS + 1]).then_inc(bn_std, 1)
            norm_std(0, EPS, 1.0)
            a.wait_ge(bn_ready, 1)
            for r in range(RANK):
                a.wait_ge(hid_done, r // 2 + 1)
                a.activation(hid[:, r, :], ps[:, r // 2 % 2, HW * (r % 2):HW * (r % 2) + HW], ACT.Relu,
                             bias=bnshift[:, r:r + 1]).then_inc(hid_ready, 1)
            norm_std(1, EPS, 1.0)
            a.wait_ge(borders_zeroed, 1)
            a.wait_ge(conv_done, 1)
            a.activation(inner(a1p), rows(ps[:, 0, 0:HW]), ACT.Relu, bias=bnshift[:, RANK:RANK + 1],
                         scale=bnscale[:, RANK:RANK + 1]).then_inc(a1_ready, 1)

            def mixed_out(n):
                a.wait_ge(mixed_done, n + 1)
                a.activation(mixed[:, n // 3, 384 * (n % 3):384 * (n % 3) + 384], ps[:, 1 + n, 0:384],
                             ACT.Copy).then_inc(mixed_ready, 1)

            def hat(c):
                a.wait_ge(absd_ready, c + 1)
                a.activation(hats[:, 3 * c:3 * c + 3, :, :, :], hats[:, 3 * c:3 * c + 3, :, :, :],
                             ACT.Relu, bias=1.0).then_inc(hats_ready, 1)

            for n in range(3):
                mixed_out(n)
            hat(0)
            mixed_out(3)
            mixed_out(4)
            hat(1)
            mixed_out(5)
            hat(2)
            for e in range(4 * TAPS):
                if e in VECTOR_DRAINS:
                    continue
                k, kb, pair = e // 4, e // 2 % 2, e % 2
                a.wait_ge(turned, e + 1)
                if k >= 2:
                    a.wait_ge(sampled, 2 * (k - 2) + kb + 1)
                a.activation(s[:, k % 2, kb, 2 * pair:2 * pair + 2, :], ps[:, 1 + e % 6, :],
                             ACT.Copy).then_inc(drained_a, 1)
            a.wait_ge(sampled, 2 * TAPS)
            a.activation(r1[:, :], ps[:, 0, 0:HW], ACT.Relu, bias=bnshift[:, RANK + 1:RANK + 2],
                         scale=bnscale[:, RANK + 1:RANK + 2]).then_inc(r1_ready, 1)

            norm_std(2, EPS4, 0.25)
            a.wait_ge(nmr_ready, 1)
            for b, j in A_MOVES:
                src, dst = to_columns(b, j)
                a.activation(dst, src, ACT.Identity, bias=nmr[Q * b:Q * b + Q, :],
                             scale=rstd[Q * b:Q * b + Q, 2:3]).then_inc(y_laid, 1)
            for n in range(STEPS):
                if n % (STEPS // 2) == 0:
                    a.wait_ge(y_turned, n // (STEPS // 2) * 2 + 1)
                    a.activation(yz[:, 0, :], ps[:, 6, 0:P], ACT.Copy, scale=0.5).then_inc(yz_a, 1)
                for z in range(2):
                    a.wait_ge(yt_turned, 2 * n + z + 1)
                    a.activation(mirrored(bands(n), z),
                                 ps[:, 2 + z, 0:P].rearrange("p (m n) -> p m n", m=2),
                                 ACT.Copy, scale=2.0).then_inc(yt_main, 1)
                if n == STEPS // 2 - 1:
                    a.wait_ge(yt_main, 2 * (n + 1))
                    for i, j in A_MOVES:
                        src, dst = to_rows(i, j)
                        a.activation(dst, src, ACT.Copy).then_inc(y_laid, 1)
            a.wait_ge(yt_main, 2 * STEPS)
            for i, j in A_MOVES:
                src, dst = to_image(i, j)
                a.activation(dst, src, ACT.Copy).then_inc(t_laid, 1)

            norm_std(3, EPS, 1.0)
            a.wait_ge(g3p_ready, 1)
            a.activation(maps[:, 0, :], g3p[:, :], ACT.Square).then_inc(sq_ready, 1)
            a.wait_ge(avg_done, 1)
            a.activation(inner(avp), rows(ps[:, 0, 0:HW]), ACT.Copy).then_inc(av_ready, 1)
            a.wait_ge(gn_var, 1)
            a.activation(gn[:, 5:6], gn[:, 4:5], ACT.Sqrt, bias=par[:, EPS:EPS + 1],
                         scale=-1.0).then_inc(gn_std, 1)
            a.wait_ge(maps_done, 1)
            a.activation(sims0[:, 0:PAD * PAD], ps[0:MAPS * B, 1, 0:PAD * PAD], ACT.Copy).then_inc(sims0_ready, 1)
            a.wait_ge(sims_turned, 1)
            a.activation(nn[:, :, :].rearrange("p k (l b) -> p k l b", b=B),
                         view(ps[0:LINE, 2, 0:1], (20, KNN), (512, LINES), (1, B)), ACT.Sqrt).then_inc(nn_ready, 1)
            a.wait_ge(sim_ready, 2)
            a.activation(ex[:, :, :], sim[:, :, :], ACT.Exp).then_inc(ex_ready, 1)
            a.wait_ge(wn_turned, 1)
            a.activation(wc36[:, :], ps[0:36, 2, 0:SPAN], ACT.Copy).then_inc(wc36_ready, 1)
            a.wait_ge(h_done, 1)
            a.activation(hff[:, 0, :], ps[:, 0, 0:HW], ACT.Relu,
                         bias=par[:, FFN_B1:FFN_B1 + 1]).then_inc(h_a, 1)

        @block.vector
        def _(v):
            own = [0]

            def step(ins):
                own[0] += 1
                ins.then_inc(v_step, 1)
                v.wait_ge(v_step, own[0])

            def stats(n, image):
                step(v.bn_stats(st6[:, n, :], image))
                v.bn_aggr(mv[:, n, :], st6[:, n, :]).then_inc(var_ready, 1)

            def rstd_of(n):
                v.wait_ge(std_ready, n + 1)
                step(v.reciprocal(rstd[:, n:n + 1], std[:, n:n + 1]))

            def normed(n, out, image, signal):
                v.wait_ge(var_ready, n + 1)
                rstd_of(n)
                v.tensor_scalar(out, image, mv[:, n, 0:1], rstd[:, n:n + 1], ALU.subtract,
                                ALU.mult).then_inc(signal, 1)

            v.memset(taps7[:, :, :, :], 0.0).then_inc(taps_zeroed, 1)
            v.wait_ge(x_loaded, 16)
            stats(0, x0[:, :])
            v.wait_ge(par_loaded, 16)
            v.wait_ge(bn_std, 1)
            step(v.reciprocal(bnrec[:, :], bnstd[:, :]))
            step(v.tensor_tensor(bnscale[:, :], bnrec[:, :], par[:, GAMMA:GAMMA + NB], ALU.mult))
            v.tensor_tensor(w1s[:, :], par[:, W1R:W1R + RANK], bnscale[:, 0:RANK], ALU.mult).then_inc(bn_scaled, 1)
            normed(0, g0[:, :], x0[:, :], g0_ready)
            step(v.tensor_tensor(bnt[:, :], par[:, BIAS:BIAS + NB], par[:, MEAN:MEAN + NB], ALU.subtract))
            step(v.tensor_tensor(bnrec[:, :], bnt[:, :], bnscale[:, :], ALU.mult))
            v.tensor_tensor(bnshift[:, :], bnrec[:, :], par[:, BETA:BETA + NB], ALU.add).then_inc(bn_ready, 1)

            v.wait_ge(g0_turned, 1)
            v.tensor_copy(g0t[:, :, :], ps[:, 2, 0:2 * P].rearrange("p (a b) -> p a b", a=2)).then_inc(g0t_ready, 1)
            for i in range(4):
                v.wait_ge(filt_done, i + 1)
                v.wait_ge(hid_ready, 2 * i + 2)
                step(v.tensor_tensor(prod0[:, i, :, :], ps[:, 3 + i, :].rearrange("p (a b) -> p a b", a=2),
                                     hid[:, 2 * i:2 * i + 2, :], ALU.mult))
                if i:
                    first = prod0[:, 0, :, :] if i == 1 else acc0[:, :, :]
                    step(v.tensor_tensor(acc0[:, :, :], first, prod0[:, i, :, :], ALU.add))
                if i == 2:
                    v.wait_ge(filt_done, 5)
                    v.tensor_tensor(xs0[:, :], ps[:, 7, 0:HW], x0[:, :], ALU.add).then_inc(v_step, 1)
                    own[0] += 1
            step(v.tensor_tensor(xf0[:, :], acc0[:, 0, :], acc0[:, 1, :], ALU.add))
            step(v.tensor_tensor(x1[:, :], xf0[:, :], xs0[:, :], ALU.add))

            stats(1, x1[:, :])
            v.wait_ge(borders_zeroed, 1)
            normed(1, inner(g1p), rows(x1[:, :]), g1_ready)
            v.wait_ge(off_done, 1)
            v.tensor_scalar(offs[:, :], ps[0:OFFS, 7, 0:HW], par[0:OFFS, OFF_B:OFF_B + 1], None,
                            ALU.add).then_inc(offs_ready, 1)
            v.wait_ge(off_turned, 1)
            v.wait_ge(cst_loaded, 16)
            v.tensor_tensor(pos[:, :, :], ps[:, 7, 0:2 * OFFS].rearrange("p (a b) -> p a b", a=2),
                            cst[:, C_BASE:C_BASE + 2 * OFFS].rearrange("p (a b) -> p a b", a=2),
                            ALU.add).then_inc(pos_ready, 1)
            v.wait_ge(pos_ready, 1)
            for half in range(2):
                v.tensor_tensor(hats[:, 0:3, half, :, :],
                                view(pos[:, half, 0:1], (8, 3), (1, 8), (0, 16)),
                                view(cst[:, C_IOTA:C_IOTA + 1], (0, 3), (0, 8), (1, 16)),
                                ALU.subtract).then_inc(v_step, 1)
                own[0] += 1
            v.wait_ge(v_step, own[0])

            def minus_abs(c):
                if c:
                    v.wait_ge(dist_ready, 2 * c)
                part = hats[:, 3 * c:3 * c + 3, :, :, :]
                v.scalar_tensor_tensor(out=part, in0=part, scalar=-1.0, in1=part, op0=ALU.mult,
                                       op1=ALU.min).then_inc(absd_ready, 1)

            def drain(e):
                k, kb, pair = e // 4, e // 2 % 2, e % 2
                v.wait_ge(turned, e + 1)
                if k >= 2:
                    v.wait_ge(sampled, 2 * (k - 2) + kb + 1)
                v.tensor_copy(s[:, k % 2, kb, 2 * pair:2 * pair + 2, :],
                              ps[:, 1 + e % 6, :].rearrange("p (a b) -> p a b", a=2)).then_inc(drained_v, 1)

            minus_abs(0)
            for k in range(TAPS):
                for half in range(2):
                    if (k, half) in POOL_UNITS:
                        continue
                    v.wait_ge(hats_ready, k // 3 + 1)
                    if k >= 2:
                        v.wait_ge(turned, 4 * (k - 1))
                    v.tensor_tensor(
                        st[:, k % 2, half, :, :].rearrange("p b (y x) -> p b y x", x=W),
                        view(hats[:, k, half, 0, 0:1], (16, B), (1, H), (0, W)),
                        view(hats[:, k, half, 4, 0:1], (16, B), (0, H), (1, W)), ALU.mult).then_inc(prod_v, 1)
                if k == 0:
                    minus_abs(1)
                if k == 1:
                    minus_abs(2)
                for e in sorted(VECTOR_DRAINS):
                    if e // 4 == k - 1:
                        drain(e)
            for e in sorted(VECTOR_DRAINS):
                if e // 4 == TAPS - 1:
                    drain(e)
            v.wait_ge(r1_ready, 1)
            step(v.tensor_tensor(x2[:, :], x1[:, :], r1[:, :], ALU.add))

            stats(2, x2[:, :])
            v.wait_ge(std_ready, 3)
            v.reciprocal(rstd[:, 2:3], std[:, 2:3]).then_inc(norm2_ready, 1)
            v.wait_ge(norm2_ready, 1)
            v.scalar_tensor_tensor(out=nmr[:, :], in0=mv[:, 2, 0:1], scalar=-1.0, in1=rstd[:, 2:3],
                                   op0=ALU.mult, op1=ALU.mult).then_inc(nmr_ready, 1)
            for b, j in V_MOVES:
                src, dst = to_columns(b, j)
                v.tensor_scalar(dst, src, mv[Q * b:Q * b + Q, 2, 0:1], rstd[Q * b:Q * b + Q, 2:3],
                                ALU.subtract, ALU.mult).then_inc(y_laid, 1)
            for n in range(STEPS):
                if n % (STEPS // 2) == 0:
                    v.wait_ge(y_turned, n // (STEPS // 2) * 2 + 2)
                    v.tensor_scalar(yz[:, 1, :], ps[:, 7, 0:P], 0.5, None, ALU.mult).then_inc(yz_v, 1)
                    v.wait_ge(yz_v, n // (STEPS // 2) + 1)
                    v.wait_ge(yz_a, n // (STEPS // 2) + 1)
                for z in range(2):
                    v.wait_ge(z_done, 2 * n + z + 1)
                    v.scalar_tensor_tensor(out=yz[:, z, :], in0=ps[:, z, 0:P], scalar=0.0, in1=yz[:, z, :],
                                           op0=ALU.max, op1=ALU.add).then_inc(y_updated, 1)
                shift = rolls(n + 1) if n + 1 < STEPS else 0
                if shift:
                    for z in range(2):
                        v.wait_ge(yt_turned, 2 * n + z + 1)
                        width = abs(shift)
                        at = Y0 + 4 * H if shift > 0 else Y0 - width
                        frm = 0 if shift > 0 else 4 * H - width
                        v.tensor_scalar(
                            view(bands(n)[:, z, at:at + 1], ((3 - 2 * z) * YW, 2), (1, width)),
                            view(ps[:, 4 + z, frm:frm + 1], (4 * H, 2), (1, width)), 2.0, None,
                            ALU.mult).then_inc(yt_border, 1)
                if n == STEPS // 2 - 1:
                    v.wait_ge(yt_main, 2 * (n + 1))
                    for i, j in V_MOVES:
                        src, dst = to_rows(i, j)
                        v.tensor_copy(dst, src).then_inc(y_laid, 1)
            v.wait_ge(yt_main, 2 * STEPS)
            for i, j in V_MOVES:
                src, dst = to_image(i, j)
                v.tensor_copy(dst, src).then_inc(t_laid, 1)
            v.wait_ge(t_laid, 16)
            step(v.scalar_tensor_tensor(out=x3[:, :], in0=t3[:, :], scalar=0.5, in1=x2[:, :],
                                        op0=ALU.mult, op1=ALU.add))

            stats(3, x3[:, :])
            normed(3, g3v[:, 1:1 + H, 1:1 + W], rows(x3[:, :]), g3_ready)
            v.wait_ge(g3_ready, 1)
            step(v.tensor_copy(view(g3v[:, 0, 1:2], (17 * PAD, 2), (1, W)),
                               view(g3v[:, 2, 1:2], (13 * PAD, 2), (1, W))))
            v.tensor_copy(view(g3v[:, 0, 0:1], (PAD, PAD), (17, 2)),
                          view(g3v[:, 0, 2:3], (PAD, PAD), (13, 2))).then_inc(g3p_ready, 1)
            v.wait_ge(g3p_ready, 1)
            for m, off in ((1, 1), (2, PAD - 1), (3, PAD)):
                v.tensor_tensor(maps[:, m, 0:324 - off], g3p[:, 0:324 - off], g3p[:, off:324],
                                ALU.mult).then_inc(map_v, 1)
            step(v.bn_stats(st6[:, 4, :], x3[:, :]))
            step(v.bn_aggr(mv[:, 4, :], st6[:, 4, :]))
            step(v.tensor_scalar(gn[:, 0:1], mv[:, 4, 0:1], mv[:, 3, 0:1], rstd[:, 3:4], ALU.subtract, ALU.mult))
            step(v.tensor_scalar(gn[:, 6:7], mv[:, 4, 1:2], rstd[:, 3:4], rstd[:, 3:4], ALU.mult, ALU.mult))
            v.scalar_tensor_tensor(out=gn[:, 1:2], in0=gn[:, 0:1], scalar=gn[:, 0:1], in1=gn[:, 6:7],
                                   op0=ALU.mult, op1=ALU.add).then_inc(gn_in, 1)
            v.wait_ge(gn_paired, 1)
            step(v.tensor_copy(gn[:, 2:4], ps[:, 5, 0:2]))
            v.scalar_tensor_tensor(out=gn[:, 4:5], in0=gn[:, 2:3], scalar=gn[:, 2:3], in1=gn[:, 3:4],
                                   op0=ALU.mult, op1=ALU.subtract).then_inc(gn_var, 1)
            v.wait_ge(lap_ready, 1)
            step(v.scalar_tensor_tensor(out=rows(df[:, 0, :]), in0=inner(avp), scalar=4.0,
                                        in1=rows(lap[:, 2, :]), op0=ALU.mult, op1=ALU.subtract))
            step(v.scalar_tensor_tensor(out=df[:, 1, :], in0=df[:, 0, :], scalar=-1.0, in1=df[:, 0, :],
                                        op0=ALU.mult, op1=ALU.max))
            v.tensor_reduce(mm[:, 0:1], df[:, 1, :], AX.X, ALU.max).then_inc(v_step, 1)
            v.tensor_reduce(mm[:, 1:2], df[:, 1, :], AX.X, ALU.min).then_inc(v_step, 1)
            own[0] += 2
            v.wait_ge(v_step, own[0])
            step(v.tensor_scalar(mm[:, 2:3], mm[:, 0:1], mm[:, 1:2], 1e-8, ALU.subtract, ALU.add))
            step(v.reciprocal(mm[:, 3:4], mm[:, 2:3]))
            step(v.tensor_scalar(df[:, 0, :], df[:, 1, :], mm[:, 1:2], mm[:, 3:4], ALU.subtract, ALU.mult))
            step(v.tensor_scalar(df[:, 1, :], df[:, 0, :], 7.0, ROUND, ALU.mult, ALU.add))
            v.tensor_scalar(view(kn[:, 0:1], (PAD, H), (1, W)), rows(df[:, 1, :]), ROUND - 1.0, float(KNN), ALU.subtract,
                            ALU.min).then_inc(kn_ready, 1)
            v.wait_ge(gn_std, 1)
            step(v.reciprocal(gn[:, 7:8], gn[:, 5:6]))
            step(v.tensor_tensor(gn[:, 8:9], gn[:, 7:8], par[:, GN_W:GN_W + 1], ALU.mult))
            step(v.scalar_tensor_tensor(out=gn[:, 9:10], in0=gn[:, 2:3], scalar=gn[:, 8:9],
                                        in1=par[:, GN_B:GN_B + 1], op0=ALU.mult, op1=ALU.subtract))
            v.tensor_scalar(rows(gnout[:, :]), g3v[:, 1:1 + H, 1:1 + W], gn[:, 8:9], gn[:, 9:10],
                            ALU.mult, ALU.subtract).then_inc(v_step, 1)
            own[0] += 1
            v.wait_ge(nn_ready, 1)
            step(v.tensor_scalar(nc_[:, :, :], nn[:, :, :], 1e-12, None, ALU.max))
            step(v.tensor_tensor(pr[:, :, :], nc_[:, :, :], view(nc_[:, 4, 0:1], (0, KNN), (1, G)), ALU.mult))
            step(v.reciprocal(rec[:, :, :], pr[:, :, :]))
            four = "p k (l b) -> p k l b"
            v.tensor_tensor(sim[:, 4:9, :].rearrange(four, b=B), view(ps[0:LINE, 2, 80:81], (4, 5), (512, LINES), (1, B)),
                            rec[:, 4:9, :].rearrange(four, b=B), ALU.mult).then_inc(sim_ready, 1)
            v.tensor_tensor(sim[:, 0:4, :].rearrange(four, b=B), view(ps[0:LINE, 2, 16:17], (16, 4), (512, LINES), (1, B)),
                            rec[:, 0:4, :].rearrange(four, b=B), ALU.mult).then_inc(sim_ready, 1)
            v.wait_ge(sim_ready, 2)
            v.wait_ge(borders_zeroed, 1)
            for k in range(KNN):
                if k < KNN - 1:
                    v.tensor_tensor(cmp[:, k, k + 1:KNN, :], sim[:, k + 1:KNN, :],
                                    view(sim[:, k, 0:1], (0, KNN - 1 - k), (1, G)), ALU.is_gt).then_inc(v_step, 1)
                    own[0] += 1
                if k:
                    v.tensor_tensor(cmp[:, k, 0:k, :], sim[:, 0:k, :],
                                    view(sim[:, k, 0:1], (0, k), (1, G)), ALU.is_ge).then_inc(v_step, 1)
                    own[0] += 1
            v.wait_ge(v_step, own[0])
            step(v.tensor_reduce(rank[:, :, :], view(cmp[:, 0, 0, 0:1], (KNN * G, KNN), (1, G), (G, KNN)),
                                 AX.X, ALU.add))
            v.wait_ge(kn_turned, 1)
            step(v.tensor_tensor(keep[:, :, :].rearrange(four, b=B), rank[:, :, :].rearrange(four, b=B),
                                 view(ps[0:LINE, 0, 0:1], (0, KNN), (P, LINES), (Q, B)), ALU.is_lt))
            v.wait_ge(ex_ready, 1)
            step(v.tensor_tensor(wts[:, :, :], ex[:, :, :], keep[:, :, :], ALU.mult))
            step(v.tensor_reduce(den[:, :], view(wts[:, 0, 0:1], (1, G), (G, KNN)), AX.X, ALU.add))
            step(v.reciprocal(rden[:, :], den[:, :]))
            v.tensor_tensor(view(wn[:, 0, 0:1], (B, KNN), (KNN * B, LINES), (1, B)),
                            wts[:, :, :].rearrange(four, b=B),
                            view(rden[:, 0:1], (0, KNN), (B, LINES), (1, B)), ALU.mult).then_inc(wn_ready, 1)
            at = [k // 3 * PAD + k % 3 for k in range(KNN)]
            for i in range(4):
                v.wait_ge(wb_done, i + 1)
                k = 2 * i
                v.tensor_tensor(prod3[:, k:k + 2, :].rearrange("p k (h w) -> p k h w", w=W),
                                view(ps[:, 3 + i, 0:1], (HW, 2), (W, H), (1, W)),
                                view(g3p[:, at[k]:at[k] + 1], (at[k + 1] - at[k], 2), (PAD, H), (1, W)),
                                ALU.mult).then_inc(p3_ready, 1)
            v.wait_ge(p3_ready, 4)
            step(v.tensor_tensor(acc3[:, 1, :, :], prod3[:, 4:6, :], prod3[:, 6:8, :], ALU.add))
            v.wait_ge(wb_done, 5)
            step(v.tensor_tensor(rows(prod3[:, 8, :]), rows(ps[:, 7, 0:HW]),
                                 view(g3p[:, at[8]:at[8] + 1], (PAD, H), (1, W)), ALU.mult))
            v.tensor_tensor(sum3[:, 0, :], prod3[:, 8, :], gnout[:, :], ALU.add).then_inc(v_step, 1)
            own[0] += 1
            v.wait_ge(s3_ready, 1)
            step(v.tensor_tensor(acc3[:, 2, :, :], acc3[:, 0, :, :], acc3[:, 1, :, :], ALU.add))
            step(v.tensor_tensor(sum3[:, 1, :], acc3[:, 2, 0, :], acc3[:, 2, 1, :], ALU.add))
            v.tensor_tensor(enh[:, :], sum3[:, 0, :], sum3[:, 1, :], ALU.add).then_inc(enh_ready, 1)
            v.wait_ge(h_done, 2)
            v.tensor_scalar(hff[:, 1, :], ps[:, 1, 0:HW], par[:, FFN_B1:FFN_B1 + 1], 0.0,
                            ALU.add, ALU.max).then_inc(h_v, 1)
            v.wait_ge(xe_ready, 1)
            v.wait_ge(ffn_done, 1)
            v.scalar_tensor_tensor(out=y[:, :], in0=ps[:, 2, 0:HW], scalar=par[:, FFN_B2:FFN_B2 + 1],
                                   in1=xe[:, :], op0=ALU.add, op1=ALU.add).then_inc(y_ready, 1)

        @block.tensor
        def _(t):
            t.wait_ge(ident_loaded, 16)
            t.wait_ge(g0_ready, 1)
            for i in range(2):
                last = t.transpose(ps[:, 2, P * i:P * i + P], g0[:, P * i:P * i + P], ident[:, :])
            last.then_inc(g0_turned, 1)

            def hidden(i):
                if i >= 2:
                    t.wait_ge(hid_ready, 2 * (i - 1))
                for r in (2 * i, 2 * i + 1):
                    last = t.matmul(ps[:, i % 2, HW * (r % 2):HW * (r % 2) + HW], w1blk[:, r, :], g0[:, :],
                                    start=True, stop=True)
                last.then_inc(hid_done, 1)

            def filters(i):
                n = 2 if i < 4 else 1
                out = ps[:, 3 + i, 0:n * HW].rearrange("p (r y x) -> p r y x", r=n, x=W)
                for half in range(2):
                    lo = 3 if half == 0 else 0
                    y0 = 0 if half == 0 else H - ROWS7
                    last = t.matmul(out[:, :, y0:y0 + ROWS7, :], g0t[:, half, :],
                                    taps7[:, 2 * i:2 * i + n, lo:lo + ROWS7, :],
                                    start=(half == 0), stop=(half == 1), skip_group_check=True)
                last.then_inc(filt_done, 1)

            t.wait_ge(w1_ready, 4)
            hidden(0)
            hidden(1)
            t.wait_ge(g0t_ready, 1)
            t.wait_ge(taps_loaded, 16 * 8)
            filters(0)
            hidden(2)
            filters(1)
            hidden(3)
            filters(2)
            filters(3)
            filters(4)

            def conv(out, image, col, width):
                for n in range(TAPS):
                    dy, dx = n // 3, n % 3
                    last = t.matmul(out, wa[:, col + width * n:col + width * n + width],
                                    image[:, dy:dy + H, dx:dx + W], start=(n == 0), stop=(n == TAPS - 1))
                return last

            t.wait_ge(wa_loaded, 32)
            t.wait_ge(g1_ready, 1)
            t.wait_ge(hid_ready, RANK)
            conv(ps[:, 0, 0:HW], g1p, W_CONV, P).then_inc(conv_done, 1)
            t.wait_ge(a1_ready, 1)
            conv(ps[0:OFFS, 7, 0:HW], a1p, W_OFF, OFFS).then_inc(off_done, 1)

            def mix(n):
                half, c = n // 3, n % 3
                t.matmul(ps[:, 1 + n, 0:384], a1[:, P * half:P * half + P],
                         wa[:, W_DEF + 384 * c:W_DEF + 384 * c + 384], start=True, stop=True).then_inc(mixed_done, 1)

            t.wait_ge(a1_packed, 1)
            mix(0)
            mix(1)
            t.wait_ge(offs_ready, 1)
            for half in range(2):
                last = t.transpose(ps[:, 7, OFFS * half:OFFS * half + OFFS], offs[:, P * half:P * half + P],
                                   ident[0:OFFS, 0:OFFS])
            last.then_inc(off_turned, 1)
            for n in range(2, 6):
                mix(n)

            def drained(e):
                v_count = sum(d <= e for d in VECTOR_DRAINS)
                if e in VECTOR_DRAINS:
                    t.wait_ge(drained_v, v_count)
                else:
                    t.wait_ge(drained_a, e + 1 - v_count)

            def turn_hats(k):
                for half in range(2):
                    done = [(i, h) for i in range(k + 1) for h in range(2) if (i, h) <= (k, half)]
                    pool = sum(u in POOL_UNITS for u in done)
                    if (k, half) in POOL_UNITS:
                        t.wait_ge(prod_g, pool)
                    else:
                        t.wait_ge(prod_v, len(done) - pool)
                for kb in range(2):
                    for pair in range(2):
                        e = 4 * k + 2 * kb + pair
                        if e < 6:
                            t.wait_ge(mixed_ready, e + 1)
                        else:
                            drained(e - 6)
                        for i in range(2):
                            for half in range(2):
                                last = t.transpose(ps[:, 1 + e % 6, HW * i + P * half:HW * i + P * half + P],
                                                   st[:, k % 2, half, 2 * pair + i, P * kb:P * kb + P],
                                                   ident[:, :])
                        last.then_inc(turned, 1)

            def sample(k):
                for kb in range(2):
                    for pair in range(2):
                        drained(4 * k + 2 * kb + pair)
                    for b in range(B):
                        col = TAPS * C * b + C * k
                        last = t.matmul(ps[Q * b:Q * b + Q, 0, 0:HW], mixed[:, kb, col:col + C],
                                        s[:, k % 2, kb, b, :], start=(k == 0 and kb == 0),
                                        stop=(k == TAPS - 1 and kb == 1))
                    last.then_inc(sampled, 1)

            for k in range(TAPS):
                turn_hats(k)
                if k:
                    sample(k - 1)
            sample(TAPS - 1)

            def turn_bands(tens, phase):
                t.wait_ge(y_laid, 16 * (phase + 1))
                for z in range(2):
                    for low, band in ((0, z), (64, 3 - z)):
                        last = t.matmul(ps[low:low + 64, 6 + z, 0:P], tens[:, band, Y0:Y0 + 4 * H], ident[:, :],
                                        start=True, stop=True)
                    last.then_inc(y_turned, 1)

            t.wait_ge(r1_ready, 1)
            t.wait_ge(band_loaded, 64)
            for n in range(STEPS):
                src = bands(n)
                if n % (STEPS // 2) == 0:
                    turn_bands(src, n // (STEPS // 2))
                at = Y0 + rolls(n)

                def banded(z, k, n=n, src=src, at=at):
                    for low, band, d in ((0, k, k - z), (64, 3 - k, z - k)):
                        last = t.matmul(ps[low:low + 64, z, 0:P], src[:, band, at:at + 64],
                                        wband[:, n, 4 * (1 - d):4 * (1 - d) + 4, :],
                                        start=(k == 0), stop=(k == z + 1))
                    return last

                if n % (STEPS // 2):
                    t.wait_ge(yt_main, 2 * n - 1)
                    if rolls(n):
                        t.wait_ge(yt_border, BORDERED[n] - 1)
                banded(0, 0)
                banded(1, 0)
                if n % (STEPS // 2):
                    t.wait_ge(yt_main, 2 * n)
                    if rolls(n):
                        t.wait_ge(yt_border, BORDERED[n])
                banded(0, 1).then_inc(z_done, 1)
                banded(1, 1)
                banded(1, 2).then_inc(z_done, 1)
                border = n + 1 < STEPS and rolls(n + 1) != 0
                for z in range(2):
                    t.wait_ge(y_updated, 2 * n + z + 1)
                    last = t.transpose(ps[:, 2 + z, 0:P], yz[:, z, :], ident[:, :])
                    if border:
                        last = t.transpose(ps[:, 4 + z, 0:P], yz[:, z, :], ident[:, :])
                    last.then_inc(yt_turned, 1)

            t.wait_ge(g3_ready, 1)
            t.matmul(ps[:, 0, 0:HW], cst[:, C_AVG:C_AVG + P], g3v[:, 1:1 + H, 1:1 + W],
                     start=True, stop=True).then_inc(avg_done, 1)
            for m, off, ready, count in ((0, 0, sq_ready, 1), (1, 1, map_v, 1), (2, 17, map_v, 2),
                                         (3, 18, map_v, 3), (4, 19, map_g, 1)):
                t.wait_ge(ready, count)
                last = t.matmul(ps[0:20, 1, 0:324 - off], cst[:, C_MAPS + 20 * m:C_MAPS + 20 * m + 20],
                                maps[:, m, 0:324 - off], start=(m == 0), stop=(m == 4), skip_group_check=True)
            last.then_inc(maps_done, 1)
            t.wait_ge(gn_in, 1)
            t.matmul(ps[:, 5, 0:2], cst[:, C_PAIR:C_PAIR + P], gn[:, 0:2], start=True, stop=True).then_inc(gn_paired, 1)
            t.wait_ge(sims0_ready, 1)
            for i in range(LINES):
                for k in range(KNN):
                    at = LINE * i + k // 3 * PAD + k % 3
                    last = t.transpose(ps[0:LINE, 2 + i, 20 * k:20 * k + 20], sims0[:, at:at + LINE],
                                       ident[0:20, 0:20])
            last.then_inc(sims_turned, 1)
            t.wait_ge(kn_ready, 1)
            for i in range(LINES):
                last = t.transpose(ps[0:LINE, 0, P * i:P * i + P], kn[:, LINE * i:LINE * i + LINE], ident[:, :])
            last.then_inc(kn_turned, 1)
            t.wait_ge(wn_ready, 1)
            for i in range(LINES):
                last = t.transpose(ps[0:36, 2, LINE * i:LINE * i + LINE], wn[:, i, :], ident[0:LINE, 0:LINE])
            last.then_inc(wn_turned, 1)
            t.wait_ge(wc36_ready, 1)
            t.wait_ge(wc_loaded, 32)
            for k in range(KNN):
                last = t.matmul(ps[:, 3 + k // 2, HW * (k % 2):HW * (k % 2) + HW], sel[:, P * k:P * k + P],
                                view(wc36[:, 0:1], (PAD, H), (1, W)), start=True, stop=True)
                if k % 2 or k == KNN - 1:
                    last.then_inc(wb_done, 1)
            t.wait_ge(enh_ready, 1)
            for i in range(2):
                t.matmul(ps[:, i, 0:HW], wc[:, P * i:P * i + P], enh[:, :], start=True, stop=True).then_inc(h_done, 1)
            for i, ready in ((0, h_a), (1, h_v)):
                t.wait_ge(ready, 1)
                last = t.matmul(ps[:, 2, 0:HW], wc[:, P * (2 + i):P * (3 + i)], hff[:, i, :],
                                start=(i == 0), stop=(i == 1))
            last.then_inc(ffn_done, 1)


def kernel(**inputs):
    import numpy as np
    import concourse.bacc as bacc
    from concourse.bass_utils import run_bass_kernel_spmd

    f = {k: np.asarray(v) for k, v in inputs.items()}
    f32 = np.float32

    def per_channel(a):
        return np.tile(a, B)[:, None]

    def per_rank(a):
        return np.tile(a[None, :], (P, 1))

    def column(a):
        out = np.zeros((P, 1), f32)
        out[:a.size, 0] = a
        return out

    off_b = np.repeat(f['L1_conv_off_b'], B)
    par = np.concatenate([
        np.concatenate([per_rank(f['L0_conv_' + r]), per_channel(f['L1_conv_' + c1]),
                        per_channel(f['L1_conv_' + c2])], 1)
        for r, c1, c2 in (('bn_var', 'bn1_v', 'bn2_v'), ('bn_gamma', 'bn1_g', 'bn2_g'),
                          ('b1', 'conv1_b', 'dconv_b'), ('bn_mean', 'bn1_m', 'bn2_m'),
                          ('bn_beta', 'bn1_b', 'bn2_b'))
    ] + [np.tile(f['L0_conv_w1'].T, (B, 1)), per_channel(f['L3_conv_gn_weight']),
         per_channel(f['L3_conv_gn_bias']), per_channel(f['L3_conv_b2']),
         np.tile(f['L3_conv_b1'], 2)[:, None], column(off_b),
         np.full((P, 1), 1e-5, f32), np.full((P, 1), 0.25e-5, f32)], 1)

    filt = np.concatenate([f['L0_conv_w2'], f['L0_conv_b2'][:, None]], 1).reshape(K7, K7, FILTERS)
    taps = np.zeros((W, FILTERS, K7, W), f32)
    for x in range(W):
        for xo in range(max(0, x - 3), min(W, x + 4)):
            taps[x, :, :, xo] = filt[::-1, x - xo + 3, :].T

    wa = np.zeros((B, C, NW1), f32)
    conv = wa[:, :, W_CONV:W_OFF].reshape(B, C, TAPS, B, C)
    off = np.zeros((B, C, TAPS, TAPS, 2, B), f32)
    conv = np.zeros((B, C, TAPS, B, C), f32)
    deform = np.zeros((B, C, B, TAPS, C), f32)
    for b in range(B):
        conv[b, :, :, b, :] = f['L1_conv_conv1_w'].reshape(C, C, TAPS).transpose(1, 2, 0)
        off[b, :, :, :, :, b] = f['L1_conv_off_w'].reshape(TAPS, 2, C, TAPS).transpose(2, 3, 0, 1)
        deform[b, :, b, :, :] = f['L1_conv_dconv_w'].reshape(C, C, TAPS).transpose(1, 2, 0)
    wa = np.concatenate([conv.reshape(P, -1), off.reshape(P, -1), deform.reshape(P, -1)], 1)

    wb = np.concatenate([f['L2_conv_' + n].reshape(5, C, C, TAPS) for n in ('w_d', 'w_u', 'w_r', 'w_l')])
    wb = wb[:, :, :, ::-1].transpose(2, 0, 3, 1)

    wc = np.zeros((P, 4, P), f32)
    for b in range(B):
        i, j = b // 2, b % 2
        wc[C * b:C * b + C, i, 64 * j:64 * j + 64] = f['L3_conv_w1'].T
        wc[64 * j:64 * j + 64, 2 + i, C * b:C * b + C] = f['L3_conv_w2'].T

    part = np.arange(P)
    cst = np.zeros((P, NCST), f32)
    cst[:, C_AVG:C_AVG + P] = (part[:, None] // C == part[None, :] // C) / f32(C)
    cst[:, C_PAIR:C_PAIR + P] = (part[:, None] // 2 == part[None, :] // 2) / f32(2)
    for m in range(MAPS):
        cst[part, C_MAPS + 20 * m + 4 * m + part // C] = 1
    base = np.zeros((P, 2, TAPS, 2, B), f32)
    for half in range(2):
        for k in range(TAPS):
            base[:, half, k, 0, :] = (8 * half + part // W - 1 + k // 3)[:, None]
            base[:, half, k, 1, :] = (part % W - 1 + k % 3)[:, None]
    cst[:, C_BASE:C_BASE + 2 * OFFS] = base.reshape(P, -1)
    cst[:, C_IOTA:C_IOTA + 16] = np.arange(16)
    sel = np.zeros((36, KNN, P), f32)
    for k in range(KNN):
        sel[4 * k + part // C, k, part] = 1

    arrays = {'x': f['x'].reshape(P, HW), 'par': par, 'ident': np.eye(P, dtype=f32),
              'taps': taps, 'wa': wa, 'wb': wb, 'wc': wc.reshape(P, -1), 'cst': cst,
              'sel': sel.reshape(36, -1)}
    arrays = {f'in_{k}': np.ascontiguousarray(v, dtype=f32) for k, v in arrays.items()}
    nc = bacc.Bacc("TRN2", target_bir_lowering=False, num_devices=1)
    args = [nc.dram_tensor(k, a.shape, F32, kind="ExternalInput").ap() for k, a in arrays.items()]
    out = nc.dram_tensor("out", (P, HW), F32, kind="ExternalOutput").ap()
    build(nc, *args, out)
    got = run_bass_kernel_spmd(nc, [arrays], core_ids=[0]).results[0]["out"]
    return got.reshape(B, C, H, W)
```

```python
from contextlib import ExitStack

import concourse.bass as bass
from concourse import mybir

F32 = mybir.dt.float32
BF16 = mybir.dt.bfloat16
ALU = mybir.AluOpType
ACT = mybir.ActivationFunctionType
AX = mybir.AxisListType

B, C, H, W = 4, 32, 16, 16
P = B * C
HW = H * W
Q = 32
RANK = 8
K7 = 7
FILTERS = RANK + 1
HALO7 = 8 + K7 - 1
ROWS7 = 11
UNITS7 = 5
HID_BANKS = (1, 2, 0, 1)
TAPS = 9
PAD = H + 2
OFFS = 2 * TAPS * B
NB = 3
STEPS = 20
LANE = 4 * H
MAPS = 5
ROUND = 12582912.0
KNN = 9
LINE = 96
LINES = 3
G = LINES * B
SPAN = LINE * LINES

VAR, GAMMA, BIAS, MEAN, BETA = (NB * i for i in range(5))
W1R = 5 * NB
GN_W, GN_B, FFN_B2, FFN_B1, OFF_B, EPS = (W1R + RANK * B + i for i in range(6))
NPAR = EPS + 1
C_AVG, C_PAIR, C_MAPS, C_BASE, C_IOTA = 0, 128, 256, 256 + MAPS * 20, 256 + MAPS * 20 + 2 * OFFS
NCST = C_IOTA + 16
W_CONV, W_OFF, W_DEF = 0, TAPS * P, TAPS * P + TAPS * OFFS
NW1 = W_DEF + TAPS * P

WARM = (12, 6, 18, 0)

HAT_GROUPS = ((0, 1), (1, 3), (3, 6), (6, 9))
POOL_UNITS = {(0, 1), (3, 1), (5, 1), (7, 1)}
VECTOR_DRAINS = {19, 27, 33, 35}


def pieces(step):
    r = H // 2 ** (5 - step % 5)
    if step // 5 % 2:
        r = (H - r) % H
    return [(r, 0, H - r)] + ([(0, H - r, r)] if r else [])


def updates(steps):
    return sum(len(pieces(n)) for n in range(steps))


def build(nc, x_d, par_d, ident_d, taps_d, wa_d, wb_d, wc_d, cst_d, sel_d, sel0_d, out_d):
    with ExitStack() as ctx:
        def sb(name, shape, dt=F32):
            return ctx.enter_context(nc.sbuf_tensor(name, shape, dt))

        def sem(name):
            return ctx.enter_context(nc.semaphore(name))

        def view(ap, *dims):
            return bass.AP(ap.tensor, ap.offset, [list(ap.ap[0])] + [list(d) for d in dims])

        ps = ctx.enter_context(nc.psum_tensor("ps", [P, 8, 512], F32))

        par = sb("par", [P, NPAR])
        ident = sb("ident", [P, P])
        cst = sb("cst", [P, NCST])
        sel = sb("sel", [36, KNN * P])
        taps7 = sb("taps7", [P, FILTERS, HALO7, W])
        sel0 = sb("sel0", [3 * Q, RANK * P], BF16)
        zeros = sb("zeros", [P, 512], BF16)
        wa = sb("wa", [P, NW1])
        wband = sb("wband", [P, STEPS, 12, C])
        wc = sb("wc", [P, 4 * P])
        bnstd = sb("bnstd", [P, NB])
        bnscale = sb("bnscale", [P, NB])
        bnrec = sb("bnrec", [P, NB])
        bnshift = sb("bnshift", [P, NB])
        bnt = sb("bnt", [P, NB])
        x0 = sb("x0", [P, HW])
        x1 = sb("x1", [P, HW])
        x2 = sb("x2", [P, HW])
        x3 = sb("x3", [P, HW])
        st6 = sb("st6", [P, 5, 6])
        mv = sb("mv", [P, 5, 2])
        std = sb("std", [P, 5])
        rstd = sb("rstd", [P, 5])
        g0 = sb("g0", [P, HW])
        g0t = sb("g0t", [P, 2, P])
        f0 = sb("f0", [Q, HW])
        fr0 = sb("fr0", [Q, 2, HW])
        fparts = sb("fparts", [3 * Q, HW], BF16)
        hid = sb("hid", [P, RANK, HW])
        prod3 = sb("prod3", [P, 2 * UNITS7, HW])
        prod0 = prod3[:, :, :].rearrange("p (u r) n -> p u r n", r=2)
        part0 = sb("part0", [P, 8, HW])
        g1p = sb("g1p", [P, PAD, PAD])
        a1p = sb("a1p", [P, PAD, PAD])
        a1 = sb("a1", [P, HW])
        offs = sb("offs", [OFFS, HW])
        pos = sb("pos", [P, 2, OFFS])
        hats = sb("hats", [P, 2, TAPS, 2 * B, 16])
        mixed = sb("mixed", [P, 2, TAPS * P])
        st = sb("st", [P, 2, 2, B, HW])
        s = sb("s", [P, 2, 2, B, HW])
        r1 = sb("r1", [P, HW])
        nmr = sb("nmr", [P, 1])
        yt = sb("yt", [P, B, LANE])
        ytb = sb("ytb", [P, B, LANE])
        t3 = sb("t3", [P, HW])
        g3p = sb("g3p", [P, PAD * PAD])
        avp = sb("avp", [P, PAD, PAD])
        maps = sb("maps", [P, MAPS, PAD * PAD])
        sims0 = sb("sims0", [MAPS * B, SPAN + 2 * PAD + 2])
        lap = sb("lap", [P, 3, HW])
        df = sb("df", [P, 2, HW])
        mm = sb("mm", [P, 4])
        kn = sb("kn", [P, SPAN])
        nn = sb("nn", [LINE, KNN, G])
        nc_ = sb("nc_", [LINE, KNN, G])
        pr = sb("pr", [LINE, KNN, G])
        rec = sb("rec", [LINE, KNN, G])
        sim = sb("sim", [LINE, KNN, G])
        ex = sb("ex", [LINE, KNN, G])
        cmp = sb("cmp", [LINE, KNN, KNN, G])
        rank = sb("rank", [LINE, KNN, G])
        keep = sb("keep", [LINE, KNN, G])
        wts = sb("wts", [LINE, KNN, G])
        wn = sb("wn", [LINE, LINES, KNN * B])
        den = sb("den", [LINE, G])
        rden = sb("rden", [LINE, G])
        wc36 = sb("wc36", [36, SPAN])
        acc3 = sb("acc3", [P, 3, 2, HW])
        sum3 = sb("sum3", [P, 2, HW])
        gn = sb("gn", [P, 12])
        gnout = sb("gnout", [P, HW])
        enh = sb("enh", [P, HW])
        hff = sb("hff", [P, 2, HW])
        xe = sb("xe", [P, HW])
        y = sb("y", [P, HW])

        x_loaded, par_loaded, ident_loaded = sem("x_loaded"), sem("par_loaded"), sem("ident_loaded")
        taps_loaded, late_taps_loaded, sel0_loaded = sem("taps_loaded"), sem("late_taps_loaded"), sem("sel0_loaded")
        wa_loaded, band_zeroed, band_loaded = sem("wa_loaded"), sem("band_zeroed"), sem("band_loaded")
        cst_loaded, wc_loaded, stored = sem("cst_loaded"), sem("wc_loaded"), sem("stored")
        v_step, a_step, g_step = sem("v_step"), sem("a_step"), sem("g_step")
        bn_std, zeros_ready = sem("bn_std"), sem("zeros_ready")
        bn_ready, borders_zeroed = sem("bn_ready"), sem("borders_zeroed")
        var_ready, std_ready = sem("var_ready"), sem("std_ready")
        g0_ready, g0_turned, g0t_ready = sem("g0_ready"), sem("g0_turned"), sem("g0t_ready")
        f_done, f_ready, fparts_ready = sem("f_done"), sem("f_ready"), sem("fparts_ready")
        hid_done, hid_ready, filt_done = sem("hid_done"), sem("hid_ready"), sem("filt_done")
        prod0_ready, fold0_ready, sum0_ready = sem("prod0_ready"), sem("fold0_ready"), sem("sum0_ready")
        g1_ready, conv_done, a1_ready = sem("g1_ready"), sem("conv_done"), sem("a1_ready")
        off_done, offs_ready, off_turned = sem("off_done"), sem("offs_ready"), sem("off_turned")
        a1_packed = sem("a1_packed")
        mixed_done, mixed_ready = sem("mixed_done"), sem("mixed_ready")
        pos_ready, first_dist_ready, dist_ready = sem("pos_ready"), sem("first_dist_ready"), sem("dist_ready")
        absd_ready, hats_ready = sem("absd_ready"), sem("hats_ready")
        prod_v, prod_g = sem("prod_v"), sem("prod_g")
        turned, drained_a, drained_v = sem("turned"), sem("drained_a"), sem("drained_v")
        sampled, r1_ready, x2_ready = sem("sampled"), sem("r1_ready"), sem("x2_ready")
        norm2_ready, nmr_ready = sem("norm2_ready"), sem("nmr_ready")
        y_laid = sem("y_laid")
        z_done, band_doubled = sem("z_done"), sem("band_doubled")
        pair_updated = (sem("pair0_updated"), sem("pair1_updated"))
        t_laid = sem("t_laid")
        g3_ready, g3p_ready, sq_ready, map_v, map_g = (
            sem("g3_ready"), sem("g3p_ready"), sem("sq_ready"), sem("map_v"), sem("map_g"))
        avg_done, av_ready, lap_ready = sem("avg_done"), sem("av_ready"), sem("lap_ready")
        maps_done, sims0_ready, sims_turned = sem("maps_done"), sem("sims0_ready"), sem("sims_turned")
        kn_ready, kn_turned = sem("kn_ready"), sem("kn_turned")
        nn_ready, sim_ready, ex_ready = sem("nn_ready"), sem("sim_ready"), sem("ex_ready")
        gn_in, gn_paired, gn_var, gn_std = sem("gn_in"), sem("gn_paired"), sem("gn_var"), sem("gn_std")
        wn_ready, wn_turned, wc36_ready = sem("wn_ready"), sem("wn_turned"), sem("wc36_ready")
        wb_done, p3_ready, s3_ready = sem("wb_done"), sem("p3_ready"), sem("s3_ready")
        enh_ready, h_done, h_a, h_v = sem("enh_ready"), sem("h_done"), sem("h_a"), sem("h_v")
        ffn_done, xe_ready, y_ready = sem("ffn_done"), sem("xe_ready"), sem("y_ready")

        def group_of(k):
            return next(c for c, (k0, k1) in enumerate(HAT_GROUPS) if k0 <= k < k1)

        def hat_group(c):
            k0, k1 = HAT_GROUPS[c]
            return view(hats[:, 0, k0, 0, 0:1], (TAPS * 8 * 16, 2), (16, 8 * (k1 - k0)), (1, 16))

        def distances(c):
            k0, k1 = HAT_GROUPS[c]
            return (view(pos[:, 0, 8 * k0:8 * k0 + 1], (OFFS, 2), (1, 8 * (k1 - k0)), (0, 16)),
                    view(cst[:, C_IOTA:C_IOTA + 1], (0, 2), (0, 8 * (k1 - k0)), (1, 16)))

        def flat_group(c):
            k0, k1 = HAT_GROUPS[c]
            return view(hats[:, 0, k0, 0, 0:1], (TAPS * 8 * 16, 2), (1, 128 * (k1 - k0)))

        def inner(padded):
            return padded[:, 1:1 + H, 1:1 + W]

        def rows(flat):
            return flat.rearrange("p (h w) -> p h w", w=W)

        g3v = g3p[:, :].rearrange("p (h w) -> p h w", w=PAD)

        def to_columns(b, j):
            return (view(x2[Q * b:Q * b + Q, j:j + 1], (4, 4), (W, H)),
                    view(yt[Q * j:Q * j + Q, b, 0:1], (H, 4), (1, H)))

        def to_rows(j, i):
            return (view(yt[Q * j:Q * j + Q, 0, i:i + 1], (LANE, B), (H, 4), (4, 4)),
                    view(ytb[Q * i:Q * i + Q, 0, j:j + 1], (LANE, B), (4, 4), (W, 4)))

        def to_image(i, b):
            return (view(ytb[Q * i:Q * i + Q, b, 0:1], (W, 4), (1, W)),
                    view(t3[Q * b:Q * b + Q, W * i:W * i + 1], (4 * W, 4), (1, W)))

        MOVES = [(i, j) for i in range(4) for j in range(4)]
        V_MOVES, A_MOVES, G_MOVES = MOVES[0:8], MOVES[8:14], MOVES[14:16]

        def bands(step):
            return yt if step < STEPS // 2 else ytb

        block = ctx.enter_context(nc.Block())

        @block.sync
        def _(sp):
            sp.dma_start(x0[:, :], x_d).then_inc(x_loaded, 16)
            sp.dma_start(par[:, :], par_d).then_inc(par_loaded, 16)
            sp.dma_start(ident[:, :], ident_d).then_inc(ident_loaded, 16)
            sp.dma_start(taps7[:, 0:4, :, :], taps_d[:, 0:4, :, :]).then_inc(taps_loaded, 16)
            sp.dma_start(sel0[:, :], sel0_d).then_inc(sel0_loaded, 16)
            sp.dma_start(taps7[:, 4:FILTERS, :, :], taps_d[:, 4:FILTERS, :, :]).then_inc(late_taps_loaded, 16)
            sp.dma_start(cst[:, :], cst_d).then_inc(cst_loaded, 16)
            sp.dma_start(wa[:, 0:W_DEF], wa_d[:, 0:W_DEF]).then_inc(wa_loaded, 16)
            sp.dma_start(wa[:, W_DEF:NW1], wa_d[:, W_DEF:NW1]).then_inc(wa_loaded, 16)
            sp.wait_ge(band_zeroed, 1)
            for a in range(4):
                sp.dma_start(wband[Q * a:Q * a + Q, :, a:a + TAPS, :], wb_d).then_inc(band_loaded, 16)
            sp.dma_start(wc[:, :], wc_d).then_inc(wc_loaded, 16)
            sp.dma_start(sel[:, :], sel_d).then_inc(wc_loaded, 16)
            sp.wait_ge(y_ready, 1)
            sp.dma_start(out_d, y[:, :]).then_inc(stored, 16)
            sp.wait_ge(stored, 16)

        @block.gpsimd
        def _(g):
            own = [0]

            def step(ins):
                own[0] += 1
                ins.then_inc(g_step, 1)
                g.wait_ge(g_step, own[0])

            for a in range(4):
                part = slice(Q * a, Q * a + Q)
                if a > 0:
                    g.memset(wband[part, :, 0:a, :], 0.0).then_inc(g_step, 1)
                    own[0] += 1
                if a < 3:
                    g.memset(wband[part, :, a + TAPS:12, :], 0.0).then_inc(g_step, 1)
                    own[0] += 1
            g.wait_ge(g_step, own[0])
            g.memset(g1p[:, :, :], 0.0).then_inc(band_zeroed, 1)
            g.memset(a1p[:, :, :], 0.0).then_inc(g_step, 1)
            g.memset(avp[:, :, :], 0.0).then_inc(g_step, 1)
            own[0] += 2
            g.wait_ge(g_step, own[0])
            g.memset(kn[:, :], 1.0).then_inc(g_step, 1)
            g.memset(sims0[:, :], 0.0).then_inc(g_step, 1)
            own[0] += 2
            g.wait_ge(g_step, own[0])
            g.memset(view(cmp[:, 0, 0, :], ((KNN + 1) * G, KNN), (1, G)), 0.0).then_inc(borders_zeroed, 1)

            g.wait_ge(fold0_ready, 2)
            step(g.tensor_tensor(part0[:, 5, :], part0[:, 1, :], part0[:, 2, :], ALU.add))
            g.wait_ge(fold0_ready, 3)
            g.tensor_tensor(part0[:, 6, :], part0[:, 5, :], part0[:, 3, :], ALU.add).then_inc(sum0_ready, 1)

            g.wait_ge(a1_ready, 1)
            g.tensor_copy(rows(a1[:, :]), inner(a1p)).then_inc(a1_packed, 1)
            g.wait_ge(cst_loaded, 16)
            g.wait_ge(pos_ready, 1)

            def distance(c):
                dist, grid = distances(c)
                g.tensor_tensor(hat_group(c), dist, grid, ALU.subtract).then_inc(dist_ready, 1)

            def multiply(k, half):
                g.wait_ge(hats_ready, group_of(k) + 1)
                if k >= 2:
                    g.wait_ge(turned, 4 * (k - 1))
                g.tensor_tensor(
                    st[:, k % 2, half, :, :].rearrange("p b (y x) -> p b y x", x=W),
                    view(hats[:, half, k, 0, 0:1], (16, B), (1, H), (0, W)),
                    view(hats[:, half, k, B, 0:1], (16, B), (0, H), (1, W)), ALU.mult).then_inc(prod_g, 1)

            distance(1)
            units = sorted(POOL_UNITS)
            multiply(*units[0])
            distance(2)
            distance(3)
            for k, half in units[1:]:
                multiply(k, half)

            g.wait_ge(norm2_ready, 1)
            for b, j in G_MOVES:
                src, dst = to_columns(b, j)
                g.tensor_scalar(dst, src, mv[Q * b:Q * b + Q, 2, 0:1], rstd[Q * b:Q * b + Q, 2:3],
                                ALU.subtract, ALU.mult).then_inc(y_laid, 1)
            for pair in range(2):
                g.wait_ge(pair_updated[pair], updates(STEPS // 2))
            for i, j in G_MOVES:
                src, dst = to_rows(i, j)
                g.tensor_copy(dst, src).then_inc(y_laid, 1)
            for pair in range(2):
                g.wait_ge(pair_updated[pair], updates(STEPS))
            for i, j in G_MOVES:
                src, dst = to_image(i, j)
                g.tensor_copy(dst, src).then_inc(t_laid, 1)

            g.wait_ge(g3p_ready, 1)
            g.tensor_tensor(maps[:, 4, 0:305], g3p[:, 0:305], g3p[:, 19:324], ALU.mult).then_inc(map_g, 1)
            g.wait_ge(av_ready, 1)
            g.tensor_tensor(rows(lap[:, 0, :]), avp[:, 0:H, 1:1 + W], avp[:, 2:2 + H, 1:1 + W],
                            ALU.add).then_inc(g_step, 1)
            g.tensor_tensor(rows(lap[:, 1, :]), avp[:, 1:1 + H, 0:W], avp[:, 1:1 + H, 2:2 + W],
                            ALU.add).then_inc(g_step, 1)
            own[0] += 2
            g.wait_ge(g_step, own[0])
            g.tensor_tensor(lap[:, 2, :], lap[:, 0, :], lap[:, 1, :], ALU.add).then_inc(lap_ready, 1)
            g.wait_ge(p3_ready, 2)
            g.tensor_tensor(acc3[:, 0, :, :], prod3[:, 0:2, :], prod3[:, 2:4, :], ALU.add).then_inc(s3_ready, 1)
            g.wait_ge(enh_ready, 1)
            g.tensor_tensor(xe[:, :], enh[:, :], x3[:, :], ALU.add).then_inc(xe_ready, 1)

        @block.scalar
        def _(a):

            def norm_std(n):
                a.wait_ge(var_ready, n + 1)
                a.activation(std[:, n:n + 1], mv[:, n, 1:2], ACT.Sqrt,
                             bias=par[:, EPS:EPS + 1]).then_inc(std_ready, 1)

            a.wait_ge(par_loaded, 16)
            a.activation(bnstd[:, :], par[:, VAR:VAR + NB], ACT.Sqrt,
                         bias=par[:, EPS:EPS + 1]).then_inc(bn_std, 1)
            norm_std(0)
            a.wait_ge(bn_ready, 1)
            a.wait_ge(f_done, 1)
            a.activation(f0[:, :], ps[0:Q, 0, 0:HW], ACT.Relu, bias=bnshift[0:Q, 0:1],
                         scale=bnscale[0:Q, 0:1]).then_inc(f_ready, 1)
            a.activation(fparts[0:Q, :], ps[0:Q, 0, 0:HW], ACT.Relu, bias=bnshift[0:Q, 0:1],
                         scale=bnscale[0:Q, 0:1]).then_inc(f_ready, 1)
            for i in range(4):
                a.wait_ge(hid_done, i + 1)
                a.activation(hid[:, 2 * i:2 * i + 2, :].rearrange("p r n -> p (r n)"), ps[:, HID_BANKS[i], :],
                             ACT.Copy).then_inc(hid_ready, 1)
            norm_std(1)
            a.wait_ge(borders_zeroed, 1)
            a.wait_ge(conv_done, 1)
            a.activation(inner(a1p), rows(ps[:, 0, 0:HW]), ACT.Relu, bias=bnshift[:, 1:2],
                         scale=bnscale[:, 1:2]).then_inc(a1_ready, 1)

            def mixed_out(n):
                a.wait_ge(mixed_done, n + 1)
                a.activation(mixed[:, n // 3, 384 * (n % 3):384 * (n % 3) + 384], ps[:, 1 + n, 0:384],
                             ACT.Copy).then_inc(mixed_ready, 1)

            def hat(c):
                a.wait_ge(absd_ready, c + 1)
                a.activation(flat_group(c), flat_group(c), ACT.Relu, bias=1.0).then_inc(hats_ready, 1)

            mixed_out(0)
            mixed_out(1)
            hat(0)
            mixed_out(2)
            hat(1)
            for n in range(3, 6):
                mixed_out(n)
            for e in range(4 * TAPS):
                if e == 4:
                    hat(2)
                if e == 12:
                    hat(3)
                if e in VECTOR_DRAINS:
                    continue
                k, kb, pair = e // 4, e // 2 % 2, e % 2
                a.wait_ge(turned, e + 1)
                if k >= 2:
                    a.wait_ge(sampled, 2 * (k - 2) + kb + 1)
                a.activation(s[:, k % 2, kb, 2 * pair:2 * pair + 2, :], ps[:, 1 + e % 6, :],
                             ACT.Copy).then_inc(drained_a, 1)
            a.wait_ge(sampled, 2 * TAPS)
            a.activation(r1[:, :], ps[:, 0, 0:HW], ACT.Relu, bias=bnshift[:, 2:3],
                         scale=bnscale[:, 2:3]).then_inc(r1_ready, 1)

            norm_std(2)
            a.wait_ge(nmr_ready, 1)
            for b, j in A_MOVES:
                src, dst = to_columns(b, j)
                a.activation(dst, src, ACT.Identity, bias=nmr[Q * b:Q * b + Q, :],
                             scale=rstd[Q * b:Q * b + Q, 2:3]).then_inc(y_laid, 1)
            for pair in range(2):
                a.wait_ge(pair_updated[pair], updates(STEPS // 2))
            for i, j in A_MOVES:
                src, dst = to_rows(i, j)
                a.activation(dst, src, ACT.Copy).then_inc(y_laid, 1)
            for pair in range(2):
                a.wait_ge(pair_updated[pair], updates(STEPS))
            for i, j in A_MOVES:
                src, dst = to_image(i, j)
                a.activation(dst, src, ACT.Copy).then_inc(t_laid, 1)

            norm_std(3)
            a.wait_ge(g3p_ready, 1)
            a.activation(maps[:, 0, :], g3p[:, :], ACT.Square).then_inc(sq_ready, 1)
            a.wait_ge(avg_done, 1)
            a.activation(inner(avp), rows(ps[:, 0, 0:HW]), ACT.Copy).then_inc(av_ready, 1)
            a.wait_ge(gn_var, 1)
            a.activation(gn[:, 5:6], gn[:, 4:5], ACT.Sqrt, bias=par[:, EPS:EPS + 1],
                         scale=-1.0).then_inc(gn_std, 1)
            a.wait_ge(maps_done, 1)
            a.activation(sims0[:, 0:PAD * PAD], ps[0:MAPS * B, 1, 0:PAD * PAD], ACT.Copy).then_inc(sims0_ready, 1)
            a.wait_ge(sims_turned, 1)
            a.activation(nn[:, :, :].rearrange("p k (l b) -> p k l b", b=B),
                         view(ps[0:LINE, 2, 0:1], (20, KNN), (512, LINES), (1, B)), ACT.Sqrt).then_inc(nn_ready, 1)
            a.wait_ge(sim_ready, 2)
            a.activation(ex[:, :, :], sim[:, :, :], ACT.Exp).then_inc(ex_ready, 1)
            a.wait_ge(wn_turned, 1)
            a.activation(wc36[:, :], ps[0:36, 2, 0:SPAN], ACT.Copy).then_inc(wc36_ready, 1)
            a.wait_ge(h_done, 1)
            a.activation(hff[:, 0, :], ps[:, 0, 0:HW], ACT.Relu,
                         bias=par[:, FFN_B1:FFN_B1 + 1]).then_inc(h_a, 1)

        @block.vector
        def _(v):
            own = [0]

            def step(ins):
                own[0] += 1
                ins.then_inc(v_step, 1)
                v.wait_ge(v_step, own[0])

            def stats(n, image):
                step(v.bn_stats(st6[:, n, :], image))
                v.bn_aggr(mv[:, n, :], st6[:, n, :]).then_inc(var_ready, 1)

            def rstd_of(n):
                v.wait_ge(std_ready, n + 1)
                step(v.reciprocal(rstd[:, n:n + 1], std[:, n:n + 1]))

            def normed(n, out, image, signal):
                v.wait_ge(var_ready, n + 1)
                rstd_of(n)
                v.tensor_scalar(out, image, mv[:, n, 0:1], rstd[:, n:n + 1], ALU.subtract,
                                ALU.mult).then_inc(signal, 1)

            v.memset(zeros[:, :], 0.0).then_inc(zeros_ready, 1)
            v.wait_ge(x_loaded, 16)
            stats(0, x0[:, :])
            v.wait_ge(par_loaded, 16)
            v.wait_ge(bn_std, 1)
            step(v.reciprocal(bnrec[:, :], bnstd[:, :]))
            step(v.tensor_tensor(bnscale[:, :], bnrec[:, :], par[:, GAMMA:GAMMA + NB], ALU.mult))
            normed(0, g0[:, :], x0[:, :], g0_ready)
            step(v.tensor_tensor(bnt[:, :], par[:, BIAS:BIAS + NB], par[:, MEAN:MEAN + NB], ALU.subtract))
            step(v.tensor_tensor(bnrec[:, :], bnt[:, :], bnscale[:, :], ALU.mult))
            v.tensor_tensor(bnshift[:, :], bnrec[:, :], par[:, BETA:BETA + NB], ALU.add).then_inc(bn_ready, 1)

            v.wait_ge(g0_turned, 1)
            v.tensor_copy(g0t[:, :, :], ps[:, 2, 0:2 * P].rearrange("p (a b) -> p a b", a=2)).then_inc(g0t_ready, 1)
            v.wait_ge(f_ready, 2)
            step(v.tensor_tensor(fr0[:, 0, :], f0[:, :], fparts[0:Q, :], ALU.subtract))
            step(v.tensor_copy(fparts[Q:2 * Q, :], fr0[:, 0, :]))
            step(v.tensor_copy(fr0[:, 1, :], fparts[Q:2 * Q, :]))
            v.tensor_tensor(fparts[2 * Q:3 * Q, :], fr0[:, 0, :], fr0[:, 1, :],
                            ALU.subtract).then_inc(fparts_ready, 1)
            v.wait_ge(filt_done, 1)
            step(v.tensor_tensor(part0[:, 0, :], ps[:, 3, 0:HW], x0[:, :], ALU.add))
            v.wait_ge(hid_ready, 1)
            v.tensor_tensor(prod0[:, 0, 0, :], ps[:, 3, HW:2 * HW], hid[:, 0, :], ALU.mult).then_inc(prod0_ready, 1)
            v.wait_ge(prod0_ready, 1)
            v.tensor_tensor(part0[:, 1, :], part0[:, 0, :], prod0[:, 0, 0, :], ALU.add).then_inc(fold0_ready, 1)
            for i in range(1, UNITS7):
                n = 2 if i < UNITS7 - 1 else 1
                v.wait_ge(filt_done, i + 1)
                v.wait_ge(hid_ready, min(i + 1, 4))
                v.tensor_tensor(prod0[:, i, 0:n, :], ps[:, 3 + i, 0:n * HW].rearrange("p (a b) -> p a b", a=n),
                                hid[:, 2 * i - 1:2 * i - 1 + n, :], ALU.mult).then_inc(prod0_ready, 1)
                if n == 2:
                    v.wait_ge(prod0_ready, i + 1)
                    v.tensor_tensor(part0[:, 1 + i, :], prod0[:, i, 0, :], prod0[:, i, 1, :],
                                    ALU.add).then_inc(fold0_ready, 1)
            v.wait_ge(fold0_ready, 4)
            v.wait_ge(sum0_ready, 1)
            step(v.tensor_tensor(part0[:, 7, :], part0[:, 6, :], part0[:, 4, :], ALU.add))
            v.wait_ge(prod0_ready, UNITS7)
            step(v.tensor_tensor(x1[:, :], part0[:, 7, :], prod0[:, 4, 0, :], ALU.add))

            stats(1, x1[:, :])
            v.wait_ge(borders_zeroed, 1)
            normed(1, inner(g1p), rows(x1[:, :]), g1_ready)
            v.wait_ge(band_loaded, 64)
            for n in range(0, STEPS, 5):
                v.tensor_scalar(wband[:, n:n + 5, :, :], wband[:, n:n + 5, :, :], 2.0, None,
                                ALU.mult).then_inc(band_doubled, 1)
            v.wait_ge(off_done, 1)
            v.tensor_scalar(offs[:, :], ps[0:OFFS, 7, 0:HW], par[0:OFFS, OFF_B:OFF_B + 1], None,
                            ALU.add).then_inc(offs_ready, 1)
            v.wait_ge(off_turned, 1)
            v.wait_ge(cst_loaded, 16)
            v.tensor_tensor(pos[:, :, :], ps[:, 7, 0:2 * OFFS].rearrange("p (a b) -> p a b", a=2),
                            cst[:, C_BASE:C_BASE + 2 * OFFS].rearrange("p (a b) -> p a b", a=2),
                            ALU.add).then_inc(pos_ready, 1)
            v.wait_ge(pos_ready, 1)
            dist, grid = distances(0)
            v.tensor_tensor(hat_group(0), dist, grid, ALU.subtract).then_inc(first_dist_ready, 1)
            v.wait_ge(first_dist_ready, 1)

            def minus_abs(c):
                if c:
                    v.wait_ge(dist_ready, c)
                v.scalar_tensor_tensor(out=flat_group(c), in0=flat_group(c), scalar=-1.0, in1=flat_group(c), op0=ALU.mult,
                                       op1=ALU.min).then_inc(absd_ready, 1)

            def drain(e):
                k, kb, pair = e // 4, e // 2 % 2, e % 2
                v.wait_ge(turned, e + 1)
                if k >= 2:
                    v.wait_ge(sampled, 2 * (k - 2) + kb + 1)
                v.tensor_copy(s[:, k % 2, kb, 2 * pair:2 * pair + 2, :],
                              ps[:, 1 + e % 6, :].rearrange("p (a b) -> p a b", a=2)).then_inc(drained_v, 1)

            minus_abs(0)
            minus_abs(1)
            for k in range(TAPS):
                for half in range(2):
                    if (k, half) in POOL_UNITS:
                        continue
                    v.wait_ge(hats_ready, group_of(k) + 1)
                    if k >= 2:
                        v.wait_ge(turned, 4 * (k - 1))
                    v.tensor_tensor(
                        st[:, k % 2, half, :, :].rearrange("p b (y x) -> p b y x", x=W),
                        view(hats[:, half, k, 0, 0:1], (16, B), (1, H), (0, W)),
                        view(hats[:, half, k, B, 0:1], (16, B), (0, H), (1, W)), ALU.mult).then_inc(prod_v, 1)
                if k == 1 or k == 3:
                    minus_abs(k // 2 + 2)
                for e in sorted(VECTOR_DRAINS):
                    if e // 4 == k - 1:
                        drain(e)
            for e in sorted(VECTOR_DRAINS):
                if e // 4 == TAPS - 1:
                    drain(e)
            v.wait_ge(r1_ready, 1)
            step(v.tensor_tensor(x2[:, :], x1[:, :], r1[:, :], ALU.add))

            stats(2, x2[:, :])
            v.wait_ge(std_ready, 3)
            v.reciprocal(rstd[:, 2:3], std[:, 2:3]).then_inc(norm2_ready, 1)
            v.wait_ge(norm2_ready, 1)
            v.scalar_tensor_tensor(out=nmr[:, :], in0=mv[:, 2, 0:1], scalar=-1.0, in1=rstd[:, 2:3],
                                   op0=ALU.mult, op1=ALU.mult).then_inc(nmr_ready, 1)
            for b, j in V_MOVES:
                src, dst = to_columns(b, j)
                v.tensor_scalar(dst, src, mv[Q * b:Q * b + Q, 2, 0:1], rstd[Q * b:Q * b + Q, 2:3],
                                ALU.subtract, ALU.mult).then_inc(y_laid, 1)
            for n in range(STEPS):
                tens = yt if n < STEPS // 2 else ytb
                for pair in range(2):
                    v.wait_ge(z_done, 2 * n + pair + 1)
                    for frm, to, count in pieces(n):
                        lanes = view(tens[:, 2 * pair, to:to + 1], (H, 8), (1, count))
                        v.scalar_tensor_tensor(out=lanes, in0=view(ps[:, pair, frm:frm + 1], (H, 8), (1, count)),
                                               scalar=0.0, in1=lanes, op0=ALU.max,
                                               op1=ALU.add).then_inc(pair_updated[pair], 1)
                if n == STEPS // 2 - 1:
                    for pair in range(2):
                        v.wait_ge(pair_updated[pair], updates(STEPS // 2))
                    for i, j in V_MOVES:
                        src, dst = to_rows(i, j)
                        v.tensor_copy(dst, src).then_inc(y_laid, 1)
            for pair in range(2):
                v.wait_ge(pair_updated[pair], updates(STEPS))
            for i, j in V_MOVES:
                src, dst = to_image(i, j)
                v.tensor_copy(dst, src).then_inc(t_laid, 1)
            v.wait_ge(t_laid, 16)
            step(v.tensor_tensor(x3[:, :], t3[:, :], x2[:, :], ALU.add))

            stats(3, x3[:, :])
            normed(3, g3v[:, 1:1 + H, 1:1 + W], rows(x3[:, :]), g3_ready)
            v.wait_ge(g3_ready, 1)
            step(v.tensor_copy(view(g3v[:, 0, 1:2], (17 * PAD, 2), (1, W)),
                               view(g3v[:, 2, 1:2], (13 * PAD, 2), (1, W))))
            v.tensor_copy(view(g3v[:, 0, 0:1], (PAD, PAD), (17, 2)),
                          view(g3v[:, 0, 2:3], (PAD, PAD), (13, 2))).then_inc(g3p_ready, 1)
            v.wait_ge(g3p_ready, 1)
            for m, off in ((1, 1), (2, PAD - 1), (3, PAD)):
                v.tensor_tensor(maps[:, m, 0:324 - off], g3p[:, 0:324 - off], g3p[:, off:324],
                                ALU.mult).then_inc(map_v, 1)
            step(v.bn_stats(st6[:, 4, :], x3[:, :]))
            step(v.bn_aggr(mv[:, 4, :], st6[:, 4, :]))
            step(v.tensor_scalar(gn[:, 0:1], mv[:, 4, 0:1], mv[:, 3, 0:1], rstd[:, 3:4], ALU.subtract, ALU.mult))
            step(v.tensor_scalar(gn[:, 6:7], mv[:, 4, 1:2], rstd[:, 3:4], rstd[:, 3:4], ALU.mult, ALU.mult))
            v.scalar_tensor_tensor(out=gn[:, 1:2], in0=gn[:, 0:1], scalar=gn[:, 0:1], in1=gn[:, 6:7],
                                   op0=ALU.mult, op1=ALU.add).then_inc(gn_in, 1)
            v.wait_ge(gn_paired, 1)
            step(v.tensor_copy(gn[:, 2:4], ps[:, 5, 0:2]))
            v.scalar_tensor_tensor(out=gn[:, 4:5], in0=gn[:, 2:3], scalar=gn[:, 2:3], in1=gn[:, 3:4],
                                   op0=ALU.mult, op1=ALU.subtract).then_inc(gn_var, 1)
            v.wait_ge(lap_ready, 1)
            step(v.scalar_tensor_tensor(out=rows(df[:, 0, :]), in0=inner(avp), scalar=4.0,
                                        in1=rows(lap[:, 2, :]), op0=ALU.mult, op1=ALU.subtract))
            step(v.scalar_tensor_tensor(out=df[:, 1, :], in0=df[:, 0, :], scalar=-1.0, in1=df[:, 0, :],
                                        op0=ALU.mult, op1=ALU.max))
            v.tensor_reduce(mm[:, 0:1], df[:, 1, :], AX.X, ALU.max).then_inc(v_step, 1)
            v.tensor_reduce(mm[:, 1:2], df[:, 1, :], AX.X, ALU.min).then_inc(v_step, 1)
            own[0] += 2
            v.wait_ge(v_step, own[0])
            step(v.tensor_scalar(mm[:, 2:3], mm[:, 0:1], mm[:, 1:2], 1e-8, ALU.subtract, ALU.add))
            step(v.reciprocal(mm[:, 3:4], mm[:, 2:3]))
            step(v.tensor_scalar(df[:, 0, :], df[:, 1, :], mm[:, 1:2], mm[:, 3:4], ALU.subtract, ALU.mult))
            step(v.tensor_scalar(df[:, 1, :], df[:, 0, :], 7.0, ROUND, ALU.mult, ALU.add))
            v.tensor_scalar(view(kn[:, 0:1], (PAD, H), (1, W)), rows(df[:, 1, :]), ROUND - 1.0, float(KNN), ALU.subtract,
                            ALU.min).then_inc(kn_ready, 1)
            v.wait_ge(gn_std, 1)
            step(v.reciprocal(gn[:, 7:8], gn[:, 5:6]))
            step(v.tensor_tensor(gn[:, 8:9], gn[:, 7:8], par[:, GN_W:GN_W + 1], ALU.mult))
            step(v.scalar_tensor_tensor(out=gn[:, 9:10], in0=gn[:, 2:3], scalar=gn[:, 8:9],
                                        in1=par[:, GN_B:GN_B + 1], op0=ALU.mult, op1=ALU.subtract))
            v.tensor_scalar(rows(gnout[:, :]), g3v[:, 1:1 + H, 1:1 + W], gn[:, 8:9], gn[:, 9:10],
                            ALU.mult, ALU.subtract).then_inc(v_step, 1)
            own[0] += 1
            v.wait_ge(nn_ready, 1)
            step(v.tensor_scalar(nc_[:, :, :], nn[:, :, :], 1e-12, None, ALU.max))
            step(v.tensor_tensor(pr[:, :, :], nc_[:, :, :], view(nc_[:, 4, 0:1], (0, KNN), (1, G)), ALU.mult))
            step(v.reciprocal(rec[:, :, :], pr[:, :, :]))
            four = "p k (l b) -> p k l b"
            v.tensor_tensor(sim[:, 4:9, :].rearrange(four, b=B), view(ps[0:LINE, 2, 80:81], (4, 5), (512, LINES), (1, B)),
                            rec[:, 4:9, :].rearrange(four, b=B), ALU.mult).then_inc(sim_ready, 1)
            v.tensor_tensor(sim[:, 0:4, :].rearrange(four, b=B), view(ps[0:LINE, 2, 16:17], (16, 4), (512, LINES), (1, B)),
                            rec[:, 0:4, :].rearrange(four, b=B), ALU.mult).then_inc(sim_ready, 1)
            v.wait_ge(sim_ready, 2)
            v.wait_ge(borders_zeroed, 1)
            for k in range(KNN):
                if k < KNN - 1:
                    v.tensor_tensor(cmp[:, k, k + 1:KNN, :], sim[:, k + 1:KNN, :],
                                    view(sim[:, k, 0:1], (0, KNN - 1 - k), (1, G)), ALU.is_gt).then_inc(v_step, 1)
                    own[0] += 1
                if k:
                    v.tensor_tensor(cmp[:, k, 0:k, :], sim[:, 0:k, :],
                                    view(sim[:, k, 0:1], (0, k), (1, G)), ALU.is_ge).then_inc(v_step, 1)
                    own[0] += 1
            v.wait_ge(v_step, own[0])
            step(v.tensor_reduce(rank[:, :, :], view(cmp[:, 0, 0, 0:1], (KNN * G, KNN), (1, G), (G, KNN)),
                                 AX.X, ALU.add))
            v.wait_ge(kn_turned, 1)
            step(v.tensor_tensor(keep[:, :, :].rearrange(four, b=B), rank[:, :, :].rearrange(four, b=B),
                                 view(ps[0:LINE, 0, 0:1], (0, KNN), (P, LINES), (Q, B)), ALU.is_lt))
            v.wait_ge(ex_ready, 1)
            step(v.tensor_tensor(wts[:, :, :], ex[:, :, :], keep[:, :, :], ALU.mult))
            step(v.tensor_reduce(den[:, :], view(wts[:, 0, 0:1], (1, G), (G, KNN)), AX.X, ALU.add))
            step(v.reciprocal(rden[:, :], den[:, :]))
            v.tensor_tensor(view(wn[:, 0, 0:1], (B, KNN), (KNN * B, LINES), (1, B)),
                            wts[:, :, :].rearrange(four, b=B),
                            view(rden[:, 0:1], (0, KNN), (B, LINES), (1, B)), ALU.mult).then_inc(wn_ready, 1)
            at = [k // 3 * PAD + k % 3 for k in range(KNN)]
            for i in range(4):
                v.wait_ge(wb_done, i + 1)
                k = 2 * i
                v.tensor_tensor(prod3[:, k:k + 2, :].rearrange("p k (h w) -> p k h w", w=W),
                                view(ps[:, 3 + i, 0:1], (HW, 2), (W, H), (1, W)),
                                view(g3p[:, at[k]:at[k] + 1], (at[k + 1] - at[k], 2), (PAD, H), (1, W)),
                                ALU.mult).then_inc(p3_ready, 1)
            v.wait_ge(p3_ready, 4)
            step(v.tensor_tensor(acc3[:, 1, :, :], prod3[:, 4:6, :], prod3[:, 6:8, :], ALU.add))
            v.wait_ge(wb_done, 5)
            step(v.tensor_tensor(rows(prod3[:, 8, :]), rows(ps[:, 7, 0:HW]),
                                 view(g3p[:, at[8]:at[8] + 1], (PAD, H), (1, W)), ALU.mult))
            v.tensor_tensor(sum3[:, 0, :], prod3[:, 8, :], gnout[:, :], ALU.add).then_inc(v_step, 1)
            own[0] += 1
            v.wait_ge(s3_ready, 1)
            step(v.tensor_tensor(acc3[:, 2, :, :], acc3[:, 0, :, :], acc3[:, 1, :, :], ALU.add))
            step(v.tensor_tensor(sum3[:, 1, :], acc3[:, 2, 0, :], acc3[:, 2, 1, :], ALU.add))
            v.tensor_tensor(enh[:, :], sum3[:, 0, :], sum3[:, 1, :], ALU.add).then_inc(enh_ready, 1)
            v.wait_ge(h_done, 2)
            v.tensor_scalar(hff[:, 1, :], ps[:, 1, 0:HW], par[:, FFN_B1:FFN_B1 + 1], 0.0,
                            ALU.add, ALU.max).then_inc(h_v, 1)
            v.wait_ge(xe_ready, 1)
            v.wait_ge(ffn_done, 1)
            v.scalar_tensor_tensor(out=y[:, :], in0=ps[:, 2, 0:HW], scalar=par[:, FFN_B2:FFN_B2 + 1],
                                   in1=xe[:, :], op0=ALU.add, op1=ALU.add).then_inc(y_ready, 1)

        @block.tensor
        def _(t):
            def keep_warm(count, bank):
                for _ in range(count):
                    t.matmul(ps[:, bank, :], zeros[:, 0:P], zeros[:, :], start=True, stop=True)

            t.wait_ge(zeros_ready, 1)
            keep_warm(WARM[0], 7)
            t.wait_ge(ident_loaded, 16)
            t.wait_ge(par_loaded, 16)
            t.wait_ge(g0_ready, 1)
            for i in range(2):
                last = t.transpose(ps[:, 2, P * i:P * i + P], g0[:, P * i:P * i + P], ident[:, :])
            last.then_inc(g0_turned, 1)
            t.matmul(ps[0:Q, 0, 0:HW], par[:, W1R:W1R + RANK * B], g0[:, :], start=True, stop=True).then_inc(f_done, 1)

            def filters(i):
                n = 2 if i < UNITS7 - 1 else 1
                out = ps[:, 3 + i, 0:n * HW].rearrange("p (r y x) -> p r y x", r=n, x=W)
                for half in range(2):
                    lo = 3 if half == 0 else 0
                    y0 = 0 if half == 0 else H - ROWS7
                    last = t.matmul(out[:, :, y0:y0 + ROWS7, :], g0t[:, half, :],
                                    taps7[:, 2 * i:2 * i + n, lo:lo + ROWS7, :],
                                    start=(half == 0), stop=(half == 1), skip_group_check=True)
                last.then_inc(filt_done, 1)

            def spread(i):
                if i == 3:
                    t.wait_ge(hid_ready, 1)
                for j in range(2):
                    r = 2 * i + j
                    last = t.matmul(ps[:, HID_BANKS[i], HW * j:HW * j + HW], sel0[:, P * r:P * r + P], fparts[:, :],
                                    start=True, stop=True)
                last.then_inc(hid_done, 1)

            t.wait_ge(g0t_ready, 1)
            t.wait_ge(taps_loaded, 16)
            filters(0)
            filters(1)
            t.wait_ge(fparts_ready, 1)
            t.wait_ge(sel0_loaded, 16)
            for i in range(4):
                spread(i)
            t.wait_ge(late_taps_loaded, 16)
            for i in range(2, UNITS7):
                filters(i)

            def conv(out, image, col, width):
                for n in range(TAPS):
                    dy, dx = n // 3, n % 3
                    last = t.matmul(out, wa[:, col + width * n:col + width * n + width],
                                    image[:, dy:dy + H, dx:dx + W], start=(n == 0), stop=(n == TAPS - 1))
                return last

            t.wait_ge(hid_ready, 4)
            keep_warm(WARM[1], 1)
            t.wait_ge(wa_loaded, 32)
            t.wait_ge(g1_ready, 1)
            conv(ps[:, 0, 0:HW], g1p, W_CONV, P).then_inc(conv_done, 1)
            t.wait_ge(a1_ready, 1)
            conv(ps[0:OFFS, 7, 0:HW], a1p, W_OFF, OFFS).then_inc(off_done, 1)

            def mix(n):
                half, c = n // 3, n % 3
                t.matmul(ps[:, 1 + n, 0:384], a1[:, P * half:P * half + P],
                         wa[:, W_DEF + 384 * c:W_DEF + 384 * c + 384], start=True, stop=True).then_inc(mixed_done, 1)

            t.wait_ge(a1_packed, 1)
            mix(0)
            t.wait_ge(offs_ready, 1)
            for half in range(2):
                last = t.transpose(ps[:, 7, OFFS * half:OFFS * half + OFFS], offs[:, P * half:P * half + P],
                                   ident[0:OFFS, 0:OFFS])
            last.then_inc(off_turned, 1)
            for n in range(1, 6):
                mix(n)

            def drained(e):
                v_count = sum(d <= e for d in VECTOR_DRAINS)
                if e in VECTOR_DRAINS:
                    t.wait_ge(drained_v, v_count)
                else:
                    t.wait_ge(drained_a, e + 1 - v_count)

            def products_of(k, half):
                done = [(i, h) for i in range(k + 1) for h in range(2) if (i, h) <= (k, half)]
                pool = sum(u in POOL_UNITS for u in done)
                if (k, half) in POOL_UNITS:
                    t.wait_ge(prod_g, pool)
                else:
                    t.wait_ge(prod_v, len(done) - pool)

            def turn_hats(k, kb, pair, halves):
                e = 4 * k + 2 * kb + pair
                for i in range(2):
                    for half in halves:
                        last = t.transpose(ps[:, 1 + e % 6, HW * i + P * half:HW * i + P * half + P],
                                           st[:, k % 2, half, 2 * pair + i, P * kb:P * kb + P], ident[:, :])
                if 1 in halves:
                    last.then_inc(turned, 1)

            def sample(k):
                for kb in range(2):
                    for pair in range(2):
                        drained(4 * k + 2 * kb + pair)
                    for b in range(B):
                        col = TAPS * C * b + C * k
                        last = t.matmul(ps[Q * b:Q * b + Q, 0, 0:HW], mixed[:, kb, col:col + C],
                                        s[:, k % 2, kb, b, :], start=(k == 0 and kb == 0),
                                        stop=(k == TAPS - 1 and kb == 1))
                    last.then_inc(sampled, 1)

            t.wait_ge(mixed_ready, 4)
            for half in range(2):
                products_of(0, half)
                for kb in range(2):
                    for pair in range(2):
                        turn_hats(0, kb, pair, (half,))
            for k in range(1, TAPS):
                products_of(k, 0)
                products_of(k, 1)
                for kb in range(2):
                    for pair in range(2):
                        e = 4 * k + 2 * kb + pair
                        if e < 6:
                            t.wait_ge(mixed_ready, e + 1)
                        else:
                            drained(e - 6)
                        turn_hats(k, kb, pair, (0, 1))
                sample(k - 1)
            sample(TAPS - 1)

            t.wait_ge(r1_ready, 1)
            keep_warm(WARM[2], 7)
            t.wait_ge(band_doubled, STEPS // 5)
            for n in range(STEPS):
                tens = yt if n < STEPS // 2 else ytb
                for pair in range(2):
                    if n % (STEPS // 2) == 0:
                        t.wait_ge(y_laid, 16 if n == 0 else 32)
                    else:
                        t.wait_ge(pair_updated[pair], updates(n))
                    for d in (0, -1, 1):
                        frm, to, count = max(d, 0), max(-d, 0), 4 - abs(d)
                        for low in (0, 64):
                            at = 4 * (1 - d) + low // Q
                            last = t.matmul(
                                ps[low:low + 64, pair, 0:2 * LANE].rearrange(
                                    "p (b n) -> p b n", b=2)[:, :, H * to:H * (to + count)],
                                wband[:, n, at:at + 2, :].rearrange("p a c -> p (a c)"),
                                tens[:, 2 * pair:2 * pair + 2, H * frm:H * (frm + count)],
                                start=(d == 0), stop=(d == 1), skip_group_check=True)
                    last.then_inc(z_done, 1)

            t.wait_ge(g3_ready, 1)
            t.matmul(ps[:, 0, 0:HW], cst[:, C_AVG:C_AVG + P], g3v[:, 1:1 + H, 1:1 + W],
                     start=True, stop=True).then_inc(avg_done, 1)
            for m, off, ready, count in ((0, 0, sq_ready, 1), (1, 1, map_v, 1), (2, 17, map_v, 2),
                                         (3, 18, map_v, 3), (4, 19, map_g, 1)):
                t.wait_ge(ready, count)
                last = t.matmul(ps[0:20, 1, 0:324 - off], cst[:, C_MAPS + 20 * m:C_MAPS + 20 * m + 20],
                                maps[:, m, 0:324 - off], start=(m == 0), stop=(m == 4), skip_group_check=True)
            last.then_inc(maps_done, 1)
            t.wait_ge(gn_in, 1)
            t.matmul(ps[:, 5, 0:2], cst[:, C_PAIR:C_PAIR + P], gn[:, 0:2], start=True, stop=True).then_inc(gn_paired, 1)
            t.wait_ge(sims0_ready, 1)
            for i in range(LINES):
                for k in range(KNN):
                    at = LINE * i + k // 3 * PAD + k % 3
                    last = t.transpose(ps[0:LINE, 2 + i, 20 * k:20 * k + 20], sims0[:, at:at + LINE],
                                       ident[0:20, 0:20])
            last.then_inc(sims_turned, 1)
            t.wait_ge(kn_ready, 1)
            for i in range(LINES):
                last = t.transpose(ps[0:LINE, 0, P * i:P * i + P], kn[:, LINE * i:LINE * i + LINE], ident[:, :])
            last.then_inc(kn_turned, 1)
            t.wait_ge(wn_ready, 1)
            for i in range(LINES):
                last = t.transpose(ps[0:36, 2, LINE * i:LINE * i + LINE], wn[:, i, :], ident[0:LINE, 0:LINE])
            last.then_inc(wn_turned, 1)
            t.wait_ge(wc36_ready, 1)
            t.wait_ge(wc_loaded, 32)
            for k in range(KNN):
                last = t.matmul(ps[:, 3 + k // 2, HW * (k % 2):HW * (k % 2) + HW], sel[:, P * k:P * k + P],
                                view(wc36[:, 0:1], (PAD, H), (1, W)), start=True, stop=True)
                if k % 2 or k == KNN - 1:
                    last.then_inc(wb_done, 1)
            t.wait_ge(enh_ready, 1)
            for i in range(2):
                t.matmul(ps[:, i, 0:HW], wc[:, P * i:P * i + P], enh[:, :], start=True, stop=True).then_inc(h_done, 1)
            for i, ready in ((0, h_a), (1, h_v)):
                t.wait_ge(ready, 1)
                last = t.matmul(ps[:, 2, 0:HW], wc[:, P * (2 + i):P * (3 + i)], hff[:, i, :],
                                start=(i == 0), stop=(i == 1))
            last.then_inc(ffn_done, 1)


def kernel(**inputs):
    import ml_dtypes
    import numpy as np
    import concourse.bacc as bacc
    from concourse.bass_utils import run_bass_kernel_spmd

    f = {k: np.asarray(v) for k, v in inputs.items()}
    f32 = np.float32

    def per_channel(a):
        return np.tile(a, B)[:, None]

    def per_map(a):
        return np.concatenate([np.repeat(a, B), np.ones(P - RANK * B, f32)])[:, None]

    def column(a):
        out = np.zeros((P, 1), f32)
        out[:a.size, 0] = a
        return out

    w1 = np.zeros((B, C, RANK, B), f32)
    for b in range(B):
        w1[b, :, :, b] = f['L0_conv_w1'].T
    off_b = np.repeat(f['L1_conv_off_b'], B)
    par = np.concatenate([
        np.concatenate([per_map(f['L0_conv_' + r]), per_channel(f['L1_conv_' + c1]),
                        per_channel(f['L1_conv_' + c2])], 1)
        for r, c1, c2 in (('bn_var', 'bn1_v', 'bn2_v'), ('bn_gamma', 'bn1_g', 'bn2_g'),
                          ('b1', 'conv1_b', 'dconv_b'), ('bn_mean', 'bn1_m', 'bn2_m'),
                          ('bn_beta', 'bn1_b', 'bn2_b'))
    ] + [w1.reshape(P, RANK * B), per_channel(f['L3_conv_gn_weight']),
         per_channel(f['L3_conv_gn_bias']), per_channel(f['L3_conv_b2']),
         np.tile(f['L3_conv_b1'], 2)[:, None], column(off_b),
         np.full((P, 1), 1e-5, f32)], 1)

    filt = np.concatenate([f['L0_conv_b2'][:, None], f['L0_conv_w2']], 1).reshape(K7, K7, FILTERS)
    taps = np.zeros((8, W, FILTERS, HALO7, W), f32)
    for n in range(8):
        for x in range(W):
            for xo in range(max(0, x - 3), min(W, x + 4)):
                taps[n, x, :, n:n + K7, xo] = filt[::-1, x - xo + 3, :].T

    wa = np.zeros((B, C, NW1), f32)
    conv = wa[:, :, W_CONV:W_OFF].reshape(B, C, TAPS, B, C)
    off = np.zeros((B, C, TAPS, TAPS, 2, B), f32)
    conv = np.zeros((B, C, TAPS, B, C), f32)
    deform = np.zeros((B, C, B, TAPS, C), f32)
    for b in range(B):
        conv[b, :, :, b, :] = f['L1_conv_conv1_w'].reshape(C, C, TAPS).transpose(1, 2, 0)
        off[b, :, :, :, :, b] = f['L1_conv_off_w'].reshape(TAPS, 2, C, TAPS).transpose(2, 3, 0, 1)
        deform[b, :, b, :, :] = f['L1_conv_dconv_w'].reshape(C, C, TAPS).transpose(1, 2, 0)
    wa = np.concatenate([conv.reshape(P, -1), off.reshape(P, -1), deform.reshape(P, -1)], 1)

    wb = np.concatenate([f['L2_conv_' + n].reshape(5, C, C, TAPS) for n in ('w_d', 'w_u', 'w_r', 'w_l')])
    wb = wb[:, :, :, ::-1].transpose(2, 0, 3, 1)

    wc = np.zeros((P, 4, P), f32)
    for b in range(B):
        i, j = b // 2, b % 2
        wc[C * b:C * b + C, i, 64 * j:64 * j + 64] = f['L3_conv_w1'].T
        wc[64 * j:64 * j + 64, 2 + i, C * b:C * b + C] = f['L3_conv_w2'].T

    part = np.arange(P)
    cst = np.zeros((P, NCST), f32)
    cst[:, C_AVG:C_AVG + P] = (part[:, None] // C == part[None, :] // C) / f32(C)
    cst[:, C_PAIR:C_PAIR + P] = (part[:, None] // 2 == part[None, :] // 2) / f32(2)
    for m in range(MAPS):
        cst[part, C_MAPS + 20 * m + 4 * m + part // C] = 1
    base = np.zeros((P, 2, TAPS, 2, B), f32)
    for half in range(2):
        for k in range(TAPS):
            base[:, half, k, 0, :] = (8 * half + part // W - 1 + k // 3)[:, None]
            base[:, half, k, 1, :] = (part % W - 1 + k % 3)[:, None]
    cst[:, C_BASE:C_BASE + 2 * OFFS] = base.reshape(P, -1)
    cst[:, C_IOTA:C_IOTA + 16] = np.arange(16)
    sel = np.zeros((36, KNN, P), f32)
    for k in range(KNN):
        sel[4 * k + part // C, k, part] = 1

    sel0 = np.zeros((3, RANK * B, RANK, P), f32)
    for r in range(RANK):
        sel0[:, B * r + part // C, r, part] = 1

    arrays = {'x': f['x'].reshape(P, HW), 'par': par, 'ident': np.eye(P, dtype=f32),
              'taps': taps.reshape(P, FILTERS, HALO7, W), 'wa': wa, 'wb': wb, 'wc': wc.reshape(P, -1), 'cst': cst,
              'sel': sel.reshape(36, -1)}
    arrays = {f'in_{k}': np.ascontiguousarray(v, dtype=f32) for k, v in arrays.items()}
    arrays['in_sel0'] = sel0.reshape(3 * Q, -1).astype(ml_dtypes.bfloat16)
    nc = bacc.Bacc("TRN2", target_bir_lowering=False, num_devices=1)
    args = [nc.dram_tensor(k, a.shape, F32 if a.dtype == f32 else BF16, kind="ExternalInput").ap()
            for k, a in arrays.items()]
    out = nc.dram_tensor("out", (P, HW), F32, kind="ExternalOutput").ap()
    build(nc, *args, out)
    got = run_bass_kernel_spmd(nc, [arrays], core_ids=[0]).results[0]["out"]
    return got.reshape(B, C, H, W)
```

```python
from contextlib import ExitStack

import concourse.bass as bass
from concourse import mybir

F32 = mybir.dt.float32
BF16 = mybir.dt.bfloat16
ALU = mybir.AluOpType
ACT = mybir.ActivationFunctionType
AX = mybir.AxisListType

B, C, H, W = 4, 32, 16, 16
P = B * C
HW = H * W
Q = 32
RANK = 8
K7 = 7
FILTERS = RANK + 1
HALO7 = 8 + K7 - 1
ROWS7 = 11
UNITS7 = 5
HID_BANKS = (1, 2, 0, 1)
TAPS = 9
PAD = H + 2
OFFS = 2 * TAPS * B
NB = 3
STEPS = 20
LANE = 4 * H
DOTS = 4
ROUND = 12582912.0
KNN = 9
LINE = 96
LINES = 3
G = LINES * B
PARTS3 = 3 * KNN * B
SPAN = LINE * LINES

VAR, GAMMA, BIAS, MEAN, BETA = (NB * i for i in range(5))
W1R = 5 * NB
GN_W, GN_B, FFN_B2, FFN_B1, EPS, OFF_B = (W1R + RANK * B + i for i in range(6))
NPAR = OFF_B + OFFS
C_AVG, C_PAIR, C_NORM, C_DOTS = 0, P, 2 * P, 2 * P + B
C_BASE = C_DOTS + DOTS * DOTS * B
C_IOTA = C_BASE + 2 * OFFS
NCST = C_IOTA + 16
CB_EYE, CB_NEG, CB_COUNT, CB_TAP, CB_ONE = 0, LINE, 2 * LINE, 2 * LINE + KNN * B, 2 * LINE + KNN * (B + G)
NCB = CB_ONE + LINE
W_OFF, W_DEF = 0, TAPS * OFFS
NW1 = W_DEF + TAPS * P

WARM = (9, 23, 12, 14, 9, 4)

IMAGE_SHARE = {"vector": (0, 7), "scalar": (7, 11), "gpsimd": (11, 12)}
HAT_GROUPS = ((0, 1), (1, 3), (3, 6), (6, 9))
POOL_UNITS = {(0, 1), (1, 1), (5, 1), (7, 1)}
ABS_AT = (1, 3)
VECTOR_DRAINS = {19, 27, 33, 35}

SPREAD3 = ((3, 0), (7, 8), (4, 2), (5, 4), (6, 6))
DOTS_FIRST = 2
HALVES = (slice(0, P), slice(P, HW))
H_BANKS, Y_BANKS = ((0, 2), (4, 5)), (3, 6)


def pieces(step):
    r = H // 2 ** (5 - step % 5)
    if step // 5 % 2:
        r = (H - r) % H
    return [(r, 0, H - r)] + ([(0, H - r, r)] if r else [])


def updates(steps):
    return sum(len(pieces(n)) for n in range(steps))


def build(nc, x_d, par_d, ident_d, taps_d, wconv_d, wa_d, wb_d, wc_d, cst_d, sel_d, sel0_d, cb_d, out_d):
    with ExitStack() as ctx:
        def sb(name, shape, dt=F32):
            return ctx.enter_context(nc.sbuf_tensor(name, shape, dt))

        def sem(name):
            return ctx.enter_context(nc.semaphore(name))

        def view(ap, *dims):
            return bass.AP(ap.tensor, ap.offset, [list(ap.ap[0])] + [list(d) for d in dims])

        ps = ctx.enter_context(nc.psum_tensor("ps", [P, 8, 512], F32))

        par = sb("par", [P, NPAR])
        ident = sb("ident", [P, P])
        cst = sb("cst", [P, NCST])
        sel = sb("sel", [PARTS3, KNN * P], BF16)
        cb = sb("cb", [P, NCB], BF16)
        taps7 = sb("taps7", [P, FILTERS, HALO7, W])
        sel0 = sb("sel0", [3 * Q, RANK * P], BF16)
        zeros = sb("zeros", [P, 512], BF16)
        wa = sb("wa", [P, NW1])
        wconv = sb("wconv", [3 * C, 3 * C])
        wband = sb("wband", [P, STEPS, 12, C])
        wc = sb("wc", [P, 4 * P])
        bnstd = sb("bnstd", [P, NB])
        bnscale = sb("bnscale", [P, NB])
        bnrec = sb("bnrec", [P, NB])
        bnshift = sb("bnshift", [P, NB])
        bnt = sb("bnt", [P, NB])
        x0 = sb("x0", [P, HW])
        x1 = sb("x1", [P, HW])
        x2 = sb("x2", [P, HW])
        x3 = sb("x3", [P, HW])
        st6 = sb("st6", [P, 5, 6])
        mv = sb("mv", [P, 5, 2])
        std = sb("std", [P, 5])
        rstd = sb("rstd", [P, 5])
        g0 = sb("g0", [P, HW])
        g0t = sb("g0t", [P, 2, P])
        f0 = sb("f0", [Q, HW])
        fr0 = sb("fr0", [Q, 2, HW])
        fparts = sb("fparts", [3 * Q, HW], BF16)
        hid = sb("hid", [P, RANK, HW])
        prod3 = sb("prod3", [P, 2 * UNITS7, HW])
        prod0 = prod3[:, :, :].rearrange("p (u r) n -> p u r n", r=2)
        part0 = sb("part0", [P, 8, HW])
        g1x = sb("g1x", [3 * C, B, PAD * W])
        g1 = sb("g1", [P, HW])
        a1x = sb("a1x", [P, 3, PAD * W])
        base = sb("base", [P, 2, OFFS])
        base0 = sb("base0", [P, 2, 2 * B, 16])
        pos = sb("pos", [P, 2, OFFS])
        hats = sb("hats", [P, 2, TAPS, 2 * B, 16])
        mixed = sb("mixed", [P, 2, TAPS * P])
        st = sb("st", [P, 2, 2, B, HW])
        s = sb("s", [P, 2, 2, B, HW])
        r1 = sb("r1", [P, HW])
        g2 = sb("g2", [P, HW])
        yt = sb("yt", [P, B, LANE])
        ytb = sb("ytb", [P, B, LANE])
        t3 = sb("t3", [P, HW])
        g3p = sb("g3p", [P, PAD * PAD])
        avp = sb("avp", [P, PAD, PAD])
        maps = sb("maps", [P, 1 + DOTS, PAD * PAD])
        norms0 = sb("norms0", [B, SPAN + 2 * PAD + 2])
        dots0 = sb("dots0", [DOTS * B, SPAN + 2 * PAD + 2])
        lap = sb("lap", [P, 3, HW])
        df = sb("df", [P, 2, HW])
        mm = sb("mm", [P, 4])
        kn = sb("kn", [P, SPAN], BF16)
        nn = sb("nn", [LINE, KNN, G])
        nc_ = sb("nc_", [LINE, KNN, G])
        pr = sb("pr", [LINE, KNN, G])
        rec = sb("rec", [LINE, KNN, G])
        sim = sb("sim", [LINE, KNN, G])
        ex = sb("ex", [LINE, KNN, G])
        above = sb("above", [LINE, KNN - 1, KNN, G], BF16)
        wts = sb("wts", [LINE, KNN, G])
        den = sb("den", [LINE, G])
        rden = sb("rden", [LINE, G])
        wf = sb("wf", [LINE, KNN, G])
        wrest = sb("wrest", [LINE, KNN, G])
        wparts = sb("wparts", [LINE, LINES, 3, KNN * B], BF16)
        wrows = sb("wrows", [PARTS3, SPAN], BF16)
        sum3 = sb("sum3", [P, 3, HW])
        gn = sb("gn", [P, 12])
        gnout = sb("gnout", [P, HW])
        enh = sb("enh", [P, HW])
        hff = sb("hff", [P, 2, HW])
        xe = sb("xe", [P, HW])
        y = sb("y", [P, HW])

        x_loaded, par_loaded, ident_loaded = sem("x_loaded"), sem("par_loaded"), sem("ident_loaded")
        taps_loaded, late_taps_loaded, sel0_loaded = sem("taps_loaded"), sem("late_taps_loaded"), sem("sel0_loaded")
        wa_loaded, band_zeroed, band_loaded = sem("wa_loaded"), sem("band_zeroed"), sem("band_loaded")
        cst_loaded, wc_loaded, stored = sem("cst_loaded"), sem("wc_loaded"), sem("stored")
        v_step, a_step, g_step = sem("v_step"), sem("a_step"), sem("g_step")
        bn_std, zeros_ready = sem("bn_std"), sem("zeros_ready")
        bn_ready, borders_zeroed = sem("bn_ready"), sem("borders_zeroed")
        var_ready, std_ready = sem("var_ready"), sem("std_ready")
        g0_ready, g0_turned, g0t_ready = sem("g0_ready"), sem("g0_turned"), sem("g0t_ready")
        f_done, f_ready, fparts_ready = sem("f_done"), sem("f_ready"), sem("fparts_ready")
        hid_done, hid_ready, filt_done = sem("hid_done"), sem("hid_ready"), sem("filt_done")
        prod0_ready, fold0_ready, sum0_ready = sem("prod0_ready"), sem("fold0_ready"), sem("sum0_ready")
        g1_ready, g1_laid = sem("g1_ready"), sem("g1_laid")
        conv_done, a1_ready = sem("conv_done"), sem("a1_ready")
        a1_left, a1_right, off_done = sem("a1_left"), sem("a1_right"), sem("off_done")
        base_ready = sem("base_ready")
        mixed_done, mixed_ready = sem("mixed_done"), sem("mixed_ready")
        pos_ready, own_dist_ready, dist_ready = sem("pos_ready"), sem("own_dist_ready"), sem("dist_ready")
        absd_ready, hats_ready = sem("absd_ready"), sem("hats_ready")
        prod_v, prod_g = sem("prod_v"), sem("prod_g")
        turned, drained_a, drained_v = sem("turned"), sem("drained_a"), sem("drained_v")
        sampled, r1_ready = sem("sampled"), sem("r1_ready")
        g2_ready = sem("g2_ready")
        y_laid = (sem("pair0_laid"), sem("pair1_laid"))
        z_done, band_doubled = sem("z_done"), sem("band_doubled")
        pair_updated = (sem("pair0_updated"), sem("pair1_updated"))
        t_laid = sem("t_laid")
        g3_ready, g3p_ready, sq_ready, map_v, map_g = (
            sem("g3_ready"), sem("g3p_ready"), sem("sq_ready"), sem("map_v"), sem("map_g"))
        avg_done, av_ready, lap_ready = sem("avg_done"), sem("av_ready"), sem("lap_ready")
        norms_done, norms0_ready, norms_turned = sem("norms_done"), sem("norms0_ready"), sem("norms_turned")
        dots_done, dots0_ready, dots_turned = sem("dots_done"), sem("dots0_ready"), sem("dots_turned")
        mm_ready, df_ready = sem("mm_ready"), sem("df_ready")
        nc_ready, pr_ready, rec_ready = sem("nc_ready"), sem("pr_ready"), sem("rec_ready")
        kn_ready, above_ready, rank_done = sem("kn_ready"), sem("above_ready"), sem("rank_done")
        nn_ready, sim_ready, ex_ready = sem("nn_ready"), sem("sim_ready"), sem("ex_ready")
        gn_in, gn_paired, gn_std = sem("gn_in"), sem("gn_paired"), sem("gn_std")
        gn_ready, gnout_ready = sem("gn_ready"), sem("gnout_ready")
        wparts_ready, wparts_turned = sem("wparts_ready"), sem("wparts_turned")
        wrows_ready, wb_done, p3_ready = sem("wrows_ready"), sem("wb_done"), sem("p3_ready")
        s3_ready, acc3_done = sem("s3_ready"), sem("acc3_done")
        enh_ready, h_done, h_a, h_v = sem("enh_ready"), sem("h_done"), sem("h_a"), sem("h_v")
        ffn_done, xe_ready, y_ready = sem("ffn_done"), sem("xe_ready"), sem("y_ready")

        def group_of(k):
            return next(c for c, (k0, k1) in enumerate(HAT_GROUPS) if k0 <= k < k1)

        def hat_group(c):
            k0, k1 = HAT_GROUPS[c]
            return view(hats[:, 0, k0, 0, 0:1], (TAPS * 8 * 16, 2), (16, 8 * (k1 - k0)), (1, 16))

        def distances(c):
            k0, k1 = HAT_GROUPS[c]
            return (view(pos[:, 0, 8 * k0:8 * k0 + 1], (OFFS, 2), (1, 8 * (k1 - k0)), (0, 16)),
                    view(cst[:, C_IOTA:C_IOTA + 1], (0, 2), (0, 8 * (k1 - k0)), (1, 16)))

        def flat_group(c):
            k0, k1 = HAT_GROUPS[c]
            return view(hats[:, 0, k0, 0, 0:1], (TAPS * 8 * 16, 2), (1, 128 * (k1 - k0)))

        def inner(padded):
            return padded[:, 1:1 + H, 1:1 + W]

        def rows(flat):
            return flat.rearrange("p (h w) -> p h w", w=W)

        g3v = g3p[:, :].rearrange("p (h w) -> p h w", w=PAD)

        def to_columns(b, j):
            return (view(g2[Q * b:Q * b + Q, j:j + 1], (4, 4), (W, H)),
                    view(yt[Q * j:Q * j + Q, b, 0:1], (H, 4), (1, H)))

        def to_rows(pair, j, i):
            return (view(yt[Q * j:Q * j + Q, 2 * pair, i:i + 1], (LANE, 2), (H, 4), (4, 4)),
                    view(ytb[Q * i:Q * i + Q, 2 * pair, j:j + 1], (LANE, 2), (4, 4), (W, 4)))

        def to_image(b, i):
            return (view(ytb[Q * i:Q * i + Q, b, 0:1], (W, 4), (1, W)),
                    view(t3[Q * b:Q * b + Q, W * i:W * i + 1], (4 * W, 4), (1, W)))

        def to_taps(b, dx):
            frm, to = max(dx - 1, 0), max(1 - dx, 0)
            n = W - abs(dx - 1)
            return (rows(g1[Q * b:Q * b + Q, :])[:, :, frm:frm + n],
                    rows(g1x[C * dx:C * dx + C, b, W:W + HW])[:, :, to:to + n])

        def images(engine):
            share = IMAGE_SHARE[engine]
            return [(n // 3, n % 3) for n in range(*share)]

        def moves(pair, engine):
            share = {"vector": (0, 4), "scalar": (4, 7), "gpsimd": (7, 8)}[engine]
            return [(2 * pair + n // 4, n % 4) for n in range(*share)]

        def turns(pair, engine):
            share = {"vector": (0, 9), "scalar": (9, 14), "gpsimd": (14, 16)}[engine]
            return [(pair, n // 4, n % 4) for n in range(*share)]

        block = ctx.enter_context(nc.Block())

        @block.sync
        def _(sp):
            sp.dma_start(x0[:, :], x_d).then_inc(x_loaded, 16)
            sp.dma_start(par[:, :], par_d).then_inc(par_loaded, 16)
            sp.dma_start(ident[:, :], ident_d).then_inc(ident_loaded, 16)
            sp.dma_start(taps7[:, 0:4, :, :], taps_d[:, 0:4, :, :]).then_inc(taps_loaded, 16)
            sp.dma_start(sel0[:, :], sel0_d).then_inc(sel0_loaded, 16)
            sp.dma_start(taps7[:, 4:FILTERS, :, :], taps_d[:, 4:FILTERS, :, :]).then_inc(late_taps_loaded, 16)
            sp.dma_start(cst[:, :], cst_d).then_inc(cst_loaded, 16)
            sp.dma_start(wconv[:, :], wconv_d).then_inc(wa_loaded, 16)
            sp.dma_start(wa[:, 0:W_DEF], wa_d[:, 0:W_DEF]).then_inc(wa_loaded, 16)
            sp.dma_start(wa[:, W_DEF:NW1], wa_d[:, W_DEF:NW1]).then_inc(wa_loaded, 16)
            sp.wait_ge(band_zeroed, 1)
            for a in range(4):
                sp.dma_start(wband[Q * a:Q * a + Q, :, a:a + TAPS, :], wb_d).then_inc(band_loaded, 16)
            sp.dma_start(wc[:, :], wc_d).then_inc(wc_loaded, 16)
            sp.dma_start(sel[:, :], sel_d).then_inc(wc_loaded, 16)
            sp.dma_start(cb[:, :], cb_d).then_inc(wc_loaded, 16)
            for n, pixels in enumerate(HALVES):
                sp.wait_ge(y_ready, n + 1)
                sp.dma_start(out_d[:, pixels], y[:, pixels]).then_inc(stored, 16)
            sp.wait_ge(stored, 32)

        @block.gpsimd
        def _(g):
            own = [0]

            def step(ins):
                own[0] += 1
                ins.then_inc(g_step, 1)
                g.wait_ge(g_step, own[0])

            for a in range(4):
                part = slice(Q * a, Q * a + Q)
                if a > 0:
                    g.memset(wband[part, :, 0:a, :], 0.0).then_inc(g_step, 1)
                    own[0] += 1
                if a < 3:
                    g.memset(wband[part, :, a + TAPS:12, :], 0.0).then_inc(g_step, 1)
                    own[0] += 1
            g.wait_ge(g_step, own[0])
            g.memset(g1x[:, :, :], 0.0).then_inc(band_zeroed, 1)
            g.memset(a1x[:, :, :], 0.0).then_inc(g_step, 1)
            g.memset(avp[:, :, :], 0.0).then_inc(g_step, 1)
            own[0] += 2
            g.wait_ge(g_step, own[0])
            g.memset(kn[:, :], 1.0).then_inc(g_step, 1)
            g.memset(norms0[:, :], 0.0).then_inc(g_step, 1)
            own[0] += 2
            g.wait_ge(g_step, own[0])
            g.memset(dots0[:, :], 0.0).then_inc(borders_zeroed, 1)

            g.wait_ge(prod0_ready, 1)
            step(g.tensor_tensor(part0[:, 1, :], part0[:, 0, :], prod0[:, 0, 0, :], ALU.add))
            g.wait_ge(prod0_ready, 2)
            step(g.tensor_tensor(part0[:, 2, :], part0[:, 1, :], prod0[:, 1, 0, :], ALU.add))
            step(g.tensor_tensor(part0[:, 3, :], part0[:, 2, :], prod0[:, 1, 1, :], ALU.add))
            g.wait_ge(fold0_ready, 1)
            g.tensor_tensor(part0[:, 5, :], part0[:, 3, :], part0[:, 4, :], ALU.add).then_inc(sum0_ready, 1)

            g.wait_ge(borders_zeroed, 1)
            g.wait_ge(g1_ready, 1)
            for b, dx in images("gpsimd"):
                src, dst = to_taps(b, dx)
                g.tensor_copy(dst, src).then_inc(g1_laid, 1)
            g.wait_ge(g1_laid, 3 * B)
            g.wait_ge(cst_loaded, 16)
            g.wait_ge(par_loaded, 16)
            step(g.tensor_tensor(base[:, :, :], cst[:, C_BASE:C_BASE + 2 * OFFS].rearrange("p (a b) -> p a b", a=2),
                                 view(par[:, OFF_B:OFF_B + 1], (0, 2), (1, OFFS)), ALU.add))
            g.tensor_tensor(base0[:, :, :, :], view(base[:, 0, 0:1], (OFFS, 2), (1, 2 * B), (0, 16)),
                            view(cst[:, C_IOTA:C_IOTA + 1], (0, 2), (0, 2 * B), (1, 16)),
                            ALU.subtract).then_inc(base_ready, 1)
            g.wait_ge(pos_ready, 1)

            def distance(c):
                dist, grid = distances(c)
                g.tensor_tensor(hat_group(c), dist, grid, ALU.subtract).then_inc(dist_ready, 1)

            def multiply(k, half):
                g.wait_ge(hats_ready, group_of(k) + 1)
                if k >= 2:
                    g.wait_ge(turned, 4 * (k - 1))
                g.tensor_tensor(
                    st[:, k % 2, half, :, :].rearrange("p b (y x) -> p b y x", x=W),
                    view(hats[:, half, k, 0, 0:1], (16, B), (1, H), (0, W)),
                    view(hats[:, half, k, B, 0:1], (16, B), (0, H), (1, W)), ALU.mult).then_inc(prod_g, 1)

            distance(1)
            units = sorted(POOL_UNITS)
            multiply(*units[0])
            multiply(*units[1])
            distance(3)
            for k, half in units[2:]:
                multiply(k, half)

            g.wait_ge(g2_ready, 1)
            for pair in range(2):
                for b, j in moves(pair, "gpsimd"):
                    src, dst = to_columns(b, j)
                    g.tensor_copy(dst, src).then_inc(y_laid[pair], 1)
            for pair in range(2):
                g.wait_ge(pair_updated[pair], updates(STEPS // 2))
                for turn in turns(pair, "gpsimd"):
                    src, dst = to_rows(*turn)
                    g.tensor_copy(dst, src).then_inc(y_laid[pair], 1)
            for pair in range(2):
                g.wait_ge(pair_updated[pair], updates(STEPS))
                for b, i in moves(pair, "gpsimd"):
                    src, dst = to_image(b, i)
                    g.tensor_copy(dst, src).then_inc(t_laid, 1)

            g.wait_ge(g3_ready, 1)
            g.wait_ge(g3p_ready, 3)
            g.tensor_tensor(maps[:, 4, 0:305], g3p[:, 0:305], g3p[:, 19:324], ALU.mult).then_inc(map_g, 1)
            g.wait_ge(av_ready, 1)
            g.tensor_tensor(rows(lap[:, 1, :]), avp[:, 1:1 + H, 0:W], avp[:, 1:1 + H, 2:2 + W],
                            ALU.add).then_inc(lap_ready, 1)
            g.wait_ge(gn_ready, 1)
            g.tensor_scalar(rows(gnout[:, :]), g3v[:, 1:1 + H, 1:1 + W], gn[:, 3:4], par[:, GN_B:GN_B + 1],
                            ALU.mult, ALU.add).then_inc(gnout_ready, 1)
            g.wait_ge(df_ready, 1)
            step(g.tensor_scalar(df[:, 1, :], df[:, 0, :], 7.0, ROUND, ALU.mult, ALU.add))
            g.tensor_scalar(view(kn[:, 0:1], (PAD, H), (1, W)), rows(df[:, 1, :]), ROUND - 1.0, float(KNN),
                            ALU.subtract, ALU.min).then_inc(kn_ready, 1)
            g.wait_ge(gnout_ready, 1)
            g.wait_ge(p3_ready, 2)
            g.tensor_tensor(sum3[:, 0, :], prod3[:, 8, :], gnout[:, :], ALU.add).then_inc(s3_ready, 1)
            g.wait_ge(enh_ready, 2)
            g.tensor_tensor(xe[:, :], enh[:, :], x3[:, :], ALU.add).then_inc(xe_ready, 1)

        @block.scalar
        def _(a):

            def norm_std(n):
                a.wait_ge(var_ready, n + 1)
                a.activation(std[:, n:n + 1], mv[:, n, 1:2], ACT.Sqrt,
                             bias=par[:, EPS:EPS + 1]).then_inc(std_ready, 1)

            a.wait_ge(zeros_ready, 1)
            a.activation(std[:, 4:5], zeros[:, 0:1], ACT.Sqrt).then_inc(a_step, 1)
            a.wait_ge(par_loaded, 16)
            norm_std(0)
            a.activation(bnstd[:, :], par[:, VAR:VAR + NB], ACT.Sqrt,
                         bias=par[:, EPS:EPS + 1]).then_inc(bn_std, 1)
            a.wait_ge(bn_ready, 1)
            a.wait_ge(f_done, 1)
            a.activation(f0[:, :], ps[0:Q, 0, 0:HW], ACT.Relu, bias=bnshift[0:Q, 0:1],
                         scale=bnscale[0:Q, 0:1]).then_inc(f_ready, 1)
            a.activation(fparts[0:Q, :], ps[0:Q, 0, 0:HW], ACT.Relu, bias=bnshift[0:Q, 0:1],
                         scale=bnscale[0:Q, 0:1]).then_inc(f_ready, 1)
            for i in range(4):
                a.wait_ge(hid_done, i + 1)
                a.activation(hid[:, 2 * i:2 * i + 2, :].rearrange("p r n -> p (r n)"), ps[:, HID_BANKS[i], :],
                             ACT.Copy).then_inc(hid_ready, 1)
            norm_std(1)
            a.wait_ge(borders_zeroed, 1)
            a.wait_ge(g1_ready, 1)
            for b, dx in images("scalar"):
                src, dst = to_taps(b, dx)
                a.activation(dst, src, ACT.Copy).then_inc(g1_laid, 1)
            a.wait_ge(conv_done, 1)
            a.activation(a1x[:, 1, W:W + HW], ps[:, 0, 0:HW], ACT.Relu, bias=bnshift[:, 1:2],
                         scale=bnscale[:, 1:2]).then_inc(a1_ready, 1)
            a.wait_ge(a1_ready, 1)
            a.activation(rows(a1x[:, 2, W:W + HW])[:, :, 0:W - 1], rows(a1x[:, 1, W:W + HW])[:, :, 1:W],
                         ACT.Copy).then_inc(a1_left, 1)

            def mixed_out(n):
                a.wait_ge(mixed_done, n + 1)
                a.activation(mixed[:, n // 3, 384 * (n % 3):384 * (n % 3) + 384], ps[:, 1 + n, 0:384],
                             ACT.Copy).then_inc(mixed_ready, 1)

            def hat(c):
                a.wait_ge(absd_ready, c + 1)
                a.activation(flat_group(c), flat_group(c), ACT.Relu, bias=1.0).then_inc(hats_ready, 1)

            mixed_out(0)
            hat(0)
            mixed_out(1)
            mixed_out(2)
            hat(1)
            for n in range(3, 6):
                mixed_out(n)
            for e in range(4 * TAPS):
                if e == 4:
                    hat(2)
                if e == 12:
                    hat(3)
                if e in VECTOR_DRAINS:
                    continue
                k, kb, pair = e // 4, e // 2 % 2, e % 2
                a.wait_ge(turned, e + 1)
                if k >= 2:
                    a.wait_ge(sampled, 2 * (k - 2) + kb + 1)
                a.activation(s[:, k % 2, kb, 2 * pair:2 * pair + 2, :], ps[:, 1 + e % 6, :],
                             ACT.Copy).then_inc(drained_a, 1)
            a.wait_ge(sampled, 2 * TAPS)
            a.activation(r1[:, :], ps[:, 0, 0:HW], ACT.Relu, bias=bnshift[:, 2:3],
                         scale=bnscale[:, 2:3]).then_inc(r1_ready, 1)

            norm_std(2)
            a.wait_ge(g2_ready, 1)
            for pair in range(2):
                for b, j in moves(pair, "scalar"):
                    src, dst = to_columns(b, j)
                    a.activation(dst, src, ACT.Copy).then_inc(y_laid[pair], 1)
            for pair in range(2):
                a.wait_ge(pair_updated[pair], updates(STEPS // 2))
                for turn in turns(pair, "scalar"):
                    src, dst = to_rows(*turn)
                    a.activation(dst, src, ACT.Copy).then_inc(y_laid[pair], 1)
            for pair in range(2):
                a.wait_ge(pair_updated[pair], updates(STEPS))
                for b, i in moves(pair, "scalar"):
                    src, dst = to_image(b, i)
                    a.activation(dst, src, ACT.Copy).then_inc(t_laid, 1)

            norm_std(3)
            a.wait_ge(g3_ready, 1)
            a.wait_ge(g3p_ready, 3)
            a.activation(maps[:, 0, :], g3p[:, :], ACT.Square).then_inc(sq_ready, 1)
            a.wait_ge(avg_done, 1)
            a.activation(inner(avp), rows(ps[:, 0, 0:HW]), ACT.Copy).then_inc(av_ready, 1)
            a.wait_ge(norms_done, 1)
            a.activation(norms0[:, 0:PAD * PAD], ps[0:B, 7, 0:PAD * PAD], ACT.Copy).then_inc(norms0_ready, 1)
            a.wait_ge(gn_paired, 1)
            a.activation(gn[:, 1:2], ps[:, 5, 0:1], ACT.Sqrt, bias=par[:, EPS:EPS + 1]).then_inc(gn_std, 1)
            a.wait_ge(norms_turned, 1)
            a.activation(nn[:, :, :].rearrange("p k g -> p (k g)"), ps[0:LINE, 0, 0:KNN * G],
                         ACT.Sqrt).then_inc(nn_ready, 1)
            a.wait_ge(dots_done, 1)
            a.activation(dots0[:, 0:PAD * PAD], ps[0:DOTS * B, 1, 0:PAD * PAD], ACT.Copy).then_inc(dots0_ready, 1)
            a.wait_ge(sim_ready, 3)
            a.activation(ex[:, :, :], sim[:, :, :], ACT.Exp).then_inc(ex_ready, 1)
            a.wait_ge(wparts_turned, 1)
            a.activation(wrows[:, :], ps[0:PARTS3, 0, 0:SPAN], ACT.Copy).then_inc(wrows_ready, 1)
            for n, pixels in enumerate(HALVES):
                a.wait_ge(h_done, 2 * n + 1)
                a.activation(hff[:, 0, pixels], ps[:, H_BANKS[n][0], 0:P], ACT.Relu,
                             bias=par[:, FFN_B1:FFN_B1 + 1]).then_inc(h_a, 1)

        @block.vector
        def _(v):
            own = [0]

            def step(ins):
                own[0] += 1
                ins.then_inc(v_step, 1)
                v.wait_ge(v_step, own[0])

            def stats(n, image):
                step(v.bn_stats(st6[:, n, :], image))
                v.bn_aggr(mv[:, n, :], st6[:, n, :]).then_inc(var_ready, 1)

            def rstd_of(n):
                v.wait_ge(std_ready, n + 1)
                step(v.reciprocal(rstd[:, n:n + 1], std[:, n:n + 1]))

            def normed(n, out, image, signal):
                v.wait_ge(var_ready, n + 1)
                rstd_of(n)
                v.tensor_scalar(out, image, mv[:, n, 0:1], rstd[:, n:n + 1], ALU.subtract,
                                ALU.mult).then_inc(signal, 1)

            v.memset(zeros[:, :], 0.0).then_inc(zeros_ready, 1)
            v.wait_ge(x_loaded, 16)
            stats(0, x0[:, :])
            normed(0, g0[:, :], x0[:, :], g0_ready)
            v.wait_ge(par_loaded, 16)
            v.wait_ge(bn_std, 1)
            step(v.reciprocal(bnrec[:, :], bnstd[:, :]))
            step(v.tensor_tensor(bnscale[:, :], bnrec[:, :], par[:, GAMMA:GAMMA + NB], ALU.mult))
            step(v.tensor_tensor(bnt[:, :], par[:, BIAS:BIAS + NB], par[:, MEAN:MEAN + NB], ALU.subtract))
            step(v.tensor_tensor(bnrec[:, :], bnt[:, :], bnscale[:, :], ALU.mult))
            v.tensor_tensor(bnshift[:, :], bnrec[:, :], par[:, BETA:BETA + NB], ALU.add).then_inc(bn_ready, 1)

            v.wait_ge(g0_turned, 1)
            v.tensor_copy(g0t[:, :, :], ps[:, 2, 0:2 * P].rearrange("p (a b) -> p a b", a=2)).then_inc(g0t_ready, 1)
            v.wait_ge(f_ready, 2)
            step(v.tensor_tensor(fr0[:, 0, :], f0[:, :], fparts[0:Q, :], ALU.subtract))
            step(v.tensor_copy(fparts[Q:2 * Q, :], fr0[:, 0, :]))
            step(v.tensor_copy(fr0[:, 1, :], fparts[Q:2 * Q, :]))
            v.tensor_tensor(fparts[2 * Q:3 * Q, :], fr0[:, 0, :], fr0[:, 1, :],
                            ALU.subtract).then_inc(fparts_ready, 1)
            v.wait_ge(filt_done, 1)
            step(v.tensor_tensor(part0[:, 0, :], ps[:, 3, 0:HW], x0[:, :], ALU.add))
            v.wait_ge(hid_ready, 1)
            v.tensor_tensor(prod0[:, 0, 0, :], ps[:, 3, HW:2 * HW], hid[:, 0, :], ALU.mult).then_inc(prod0_ready, 1)
            for i in range(1, UNITS7):
                n = 2 if i < UNITS7 - 1 else 1
                v.wait_ge(filt_done, i + 1)
                v.wait_ge(hid_ready, min(i + 1, 4))
                v.tensor_tensor(prod0[:, i, 0:n, :], ps[:, 3 + i, 0:n * HW].rearrange("p (a b) -> p a b", a=n),
                                hid[:, 2 * i - 1:2 * i - 1 + n, :], ALU.mult).then_inc(prod0_ready, 1)
                if i == 2:
                    v.wait_ge(prod0_ready, 3)
                    v.tensor_tensor(part0[:, 4, :], prod0[:, 2, 0, :], prod0[:, 2, 1, :],
                                    ALU.add).then_inc(fold0_ready, 1)
            v.wait_ge(prod0_ready, UNITS7 - 1)
            step(v.tensor_tensor(part0[:, 6, :], prod0[:, 3, 0, :], prod0[:, 3, 1, :], ALU.add))
            v.wait_ge(prod0_ready, UNITS7)
            step(v.tensor_tensor(part0[:, 7, :], part0[:, 6, :], prod0[:, 4, 0, :], ALU.add))
            v.wait_ge(sum0_ready, 1)
            step(v.tensor_tensor(x1[:, :], part0[:, 7, :], part0[:, 5, :], ALU.add))

            stats(1, x1[:, :])
            v.wait_ge(borders_zeroed, 1)
            normed(1, g1[:, :], x1[:, :], g1_ready)
            v.wait_ge(g1_ready, 1)
            for b, dx in images("vector"):
                src, dst = to_taps(b, dx)
                v.tensor_copy(dst, src).then_inc(g1_laid, 1)
            v.wait_ge(band_loaded, 64)
            for n in range(0, STEPS, 5):
                v.tensor_scalar(wband[:, n:n + 5, :, :], wband[:, n:n + 5, :, :], 2.0, None,
                                ALU.mult).then_inc(band_doubled, 1)
                if n == 0:
                    v.wait_ge(a1_ready, 1)
                    v.tensor_copy(rows(a1x[:, 0, W:W + HW])[:, :, 1:W],
                                  rows(a1x[:, 1, W:W + HW])[:, :, 0:W - 1]).then_inc(a1_right, 1)
            v.wait_ge(off_done, 1)
            v.wait_ge(base_ready, 1)
            v.tensor_tensor(hat_group(0), view(ps[:, 7, 0:1], (OFFS, 2), (1, 2 * B), (0, 16)),
                            base0[:, :, :, :], ALU.add).then_inc(own_dist_ready, 1)
            v.tensor_tensor(pos[:, :, :], ps[:, 7, 0:2 * OFFS].rearrange("p (a b) -> p a b", a=2),
                            base[:, :, :], ALU.add).then_inc(pos_ready, 1)

            def minus_abs(c):
                if c in (0, 2):
                    v.wait_ge(own_dist_ready, c // 2 + 1)
                else:
                    v.wait_ge(dist_ready, c // 2 + 1)
                v.scalar_tensor_tensor(out=flat_group(c), in0=flat_group(c), scalar=-1.0, in1=flat_group(c),
                                       op0=ALU.mult, op1=ALU.min).then_inc(absd_ready, 1)

            def drain(e):
                k, kb, pair = e // 4, e // 2 % 2, e % 2
                v.wait_ge(turned, e + 1)
                if k >= 2:
                    v.wait_ge(sampled, 2 * (k - 2) + kb + 1)
                v.tensor_copy(s[:, k % 2, kb, 2 * pair:2 * pair + 2, :],
                              ps[:, 1 + e % 6, :].rearrange("p (a b) -> p a b", a=2)).then_inc(drained_v, 1)

            minus_abs(0)
            minus_abs(1)
            for k in range(TAPS):
                for half in range(2):
                    if (k, half) in POOL_UNITS:
                        continue
                    v.wait_ge(hats_ready, group_of(k) + 1)
                    if k >= 2:
                        v.wait_ge(turned, 4 * (k - 1))
                    v.tensor_tensor(
                        st[:, k % 2, half, :, :].rearrange("p b (y x) -> p b y x", x=W),
                        view(hats[:, half, k, 0, 0:1], (16, B), (1, H), (0, W)),
                        view(hats[:, half, k, B, 0:1], (16, B), (0, H), (1, W)), ALU.mult).then_inc(prod_v, 1)
                if k == 1:
                    v.wait_ge(pos_ready, 1)
                    dist, grid = distances(2)
                    v.tensor_tensor(hat_group(2), dist, grid, ALU.subtract).then_inc(own_dist_ready, 1)
                if k == ABS_AT[0] or k == ABS_AT[1]:
                    minus_abs(2 if k == ABS_AT[0] else 3)
                for e in sorted(VECTOR_DRAINS):
                    if e // 4 == k - 1:
                        drain(e)
            for e in sorted(VECTOR_DRAINS):
                if e // 4 == TAPS - 1:
                    drain(e)
            v.wait_ge(r1_ready, 1)
            step(v.tensor_tensor(x2[:, :], x1[:, :], r1[:, :], ALU.add))

            stats(2, x2[:, :])
            normed(2, g2[:, :], x2[:, :], g2_ready)
            v.wait_ge(g2_ready, 1)
            for pair in range(2):
                for b, j in moves(pair, "vector"):
                    src, dst = to_columns(b, j)
                    v.tensor_copy(dst, src).then_inc(y_laid[pair], 1)
            for n in range(STEPS):
                tens = yt if n < STEPS // 2 else ytb
                for pair in range(2):
                    v.wait_ge(z_done, 2 * n + pair + 1)
                    for frm, to, count in pieces(n):
                        lanes = view(tens[:, 2 * pair, to:to + 1], (H, 8), (1, count))
                        v.scalar_tensor_tensor(out=lanes, in0=view(ps[:, pair, frm:frm + 1], (H, 8), (1, count)),
                                               scalar=0.0, in1=lanes, op0=ALU.max,
                                               op1=ALU.add).then_inc(pair_updated[pair], 1)
                    if n == STEPS // 2 - 1:
                        v.wait_ge(pair_updated[pair], updates(STEPS // 2))
                        for turn in turns(pair, "vector"):
                            src, dst = to_rows(*turn)
                            v.tensor_copy(dst, src).then_inc(y_laid[pair], 1)
                    if n == STEPS - 1:
                        v.wait_ge(pair_updated[pair], updates(STEPS))
                        for b, i in moves(pair, "vector"):
                            src, dst = to_image(b, i)
                            v.tensor_copy(dst, src).then_inc(t_laid, 1)
            v.wait_ge(t_laid, 16)
            step(v.tensor_tensor(x3[:, :], t3[:, :], x2[:, :], ALU.add))

            stats(3, x3[:, :])
            normed(3, g3v[:, 1:1 + H, 1:1 + W], rows(x3[:, :]), g3_ready)
            v.wait_ge(g3_ready, 1)
            v.tensor_copy(view(g3v[:, 0, 1:2], (17 * PAD, 2), (1, W)),
                          view(g3v[:, 2, 1:2], (13 * PAD, 2), (1, W))).then_inc(g3p_ready, 1)
            v.tensor_copy(view(g3v[:, 1, 0:1], (PAD, H), (17, 2)),
                          view(g3v[:, 1, 2:3], (PAD, H), (13, 2))).then_inc(g3p_ready, 1)
            v.tensor_copy(view(g3v[:, 0, 0:1], (17 * PAD, 2), (17, 2)),
                          view(g3v[:, 2, 2:3], (13 * PAD, 2), (13, 2))).then_inc(g3p_ready, 1)
            v.wait_ge(g3p_ready, 3)
            for m, off in ((1, 1), (2, PAD - 1), (3, PAD)):
                v.tensor_tensor(maps[:, m, 0:324 - off], g3p[:, 0:324 - off], g3p[:, off:324],
                                ALU.mult).then_inc(map_v, 1)
            v.tensor_scalar(gn[:, 0:1], mv[:, 3, 1:2], rstd[:, 3:4], rstd[:, 3:4], ALU.mult,
                            ALU.mult).then_inc(gn_in, 1)
            v.wait_ge(av_ready, 1)
            step(v.tensor_tensor(rows(lap[:, 0, :]), avp[:, 0:H, 1:1 + W], avp[:, 2:2 + H, 1:1 + W], ALU.add))
            step(v.scalar_tensor_tensor(out=rows(lap[:, 2, :]), in0=inner(avp), scalar=4.0,
                                        in1=rows(lap[:, 0, :]), op0=ALU.mult, op1=ALU.subtract))
            v.wait_ge(lap_ready, 1)
            step(v.tensor_tensor(df[:, 0, :], lap[:, 2, :], lap[:, 1, :], ALU.subtract))
            step(v.scalar_tensor_tensor(out=df[:, 1, :], in0=df[:, 0, :], scalar=-1.0, in1=df[:, 0, :],
                                        op0=ALU.mult, op1=ALU.max))
            v.tensor_reduce(mm[:, 0:1], df[:, 1, :], AX.X, ALU.max).then_inc(mm_ready, 1)
            v.tensor_reduce(mm[:, 1:2], df[:, 1, :], AX.X, ALU.min).then_inc(mm_ready, 1)
            v.wait_ge(gn_std, 1)
            step(v.reciprocal(gn[:, 2:3], gn[:, 1:2]))
            v.tensor_tensor(gn[:, 3:4], gn[:, 2:3], par[:, GN_W:GN_W + 1], ALU.mult).then_inc(gn_ready, 1)
            v.wait_ge(mm_ready, 2)
            v.tensor_scalar(mm[:, 2:3], mm[:, 0:1], mm[:, 1:2], 1e-8, ALU.subtract, ALU.add).then_inc(mm_ready, 1)
            v.wait_ge(nn_ready, 1)
            v.tensor_scalar(nc_[:, :, :], nn[:, :, :], 1e-12, None, ALU.max).then_inc(nc_ready, 1)
            v.wait_ge(mm_ready, 3)
            v.reciprocal(mm[:, 3:4], mm[:, 2:3]).then_inc(mm_ready, 1)
            v.wait_ge(nc_ready, 1)
            v.tensor_tensor(pr[:, :, :], nc_[:, :, :], view(nc_[:, 4, 0:1], (0, KNN), (1, G)),
                            ALU.mult).then_inc(pr_ready, 1)
            v.wait_ge(mm_ready, 4)
            v.tensor_scalar(df[:, 0, :], df[:, 1, :], mm[:, 1:2], mm[:, 3:4], ALU.subtract,
                            ALU.mult).then_inc(df_ready, 1)
            v.wait_ge(pr_ready, 1)
            v.reciprocal(rec[:, :, :], pr[:, :, :]).then_inc(rec_ready, 1)
            v.wait_ge(rec_ready, 1)
            four = "p k (l b) -> p k l b"
            v.tensor_tensor(sim[:, 4, :], ps[0:LINE, 0, 4 * G:5 * G], rec[:, 4, :], ALU.mult).then_inc(sim_ready, 1)
            v.wait_ge(dots_turned, 1)
            v.tensor_tensor(sim[:, 5:9, :].rearrange(four, b=B),
                            view(ps[0:LINE, 2, 192:193], (B, DOTS), (16, LINES), (1, B)),
                            rec[:, 5:9, :].rearrange(four, b=B), ALU.mult).then_inc(sim_ready, 1)
            v.tensor_tensor(sim[:, 0:4, :].rearrange(four, b=B),
                            view(ps[0:LINE, 2, 12:13], (48 - B, DOTS), (16, LINES), (1, B)),
                            rec[:, 0:4, :].rearrange(four, b=B), ALU.mult).then_inc(sim_ready, 1)
            v.wait_ge(sim_ready, 3)
            for o in range(1, KNN):
                v.tensor_tensor(above[:, o - 1, 0:KNN - o, :], sim[:, o:KNN, :], sim[:, 0:KNN - o, :],
                                ALU.is_gt).then_inc(above_ready, 1)
            v.wait_ge(ex_ready, 1)
            v.wait_ge(rank_done, 1)
            step(v.scalar_tensor_tensor(out=wts[:, :, :].rearrange("p k g -> p (k g)"), in0=ps[0:LINE, 6, 0:KNN * G],
                                        scalar=0.0, in1=ex[:, :, :].rearrange("p k g -> p (k g)"),
                                        op0=ALU.is_lt, op1=ALU.mult))
            step(v.tensor_reduce(den[:, :], view(wts[:, 0, 0:1], (1, G), (G, KNN)), AX.X, ALU.add))
            step(v.reciprocal(rden[:, :], den[:, :]))
            every = view(rden[:, 0:1], (0, KNN), (B, LINES), (1, B))

            def part(n):
                return view(wparts[:, 0, n, 0:1], (B, KNN), (PARTS3, LINES), (1, B))

            v.tensor_tensor(wf[:, :, :].rearrange(four, b=B), wts[:, :, :].rearrange(four, b=B), every,
                            ALU.mult).then_inc(v_step, 1)
            own[0] += 1
            step(v.tensor_tensor(part(0), wts[:, :, :].rearrange(four, b=B), every, ALU.mult))
            step(v.tensor_tensor(wrest[:, :, :].rearrange(four, b=B), wf[:, :, :].rearrange(four, b=B), part(0),
                                 ALU.subtract))
            step(v.tensor_copy(part(1), wrest[:, :, :].rearrange(four, b=B)))
            v.tensor_tensor(part(2), wrest[:, :, :].rearrange(four, b=B), part(1),
                            ALU.subtract).then_inc(wparts_ready, 1)
            at = [k // 3 * PAD + k % 3 for k in range(KNN)]
            for n, (bank, k) in enumerate(SPREAD3):
                v.wait_ge(wb_done, n + 1)
                if k == 8:
                    v.tensor_tensor(rows(prod3[:, 8, :]), rows(ps[:, bank, 0:HW]),
                                    view(g3p[:, at[8]:at[8] + 1], (PAD, H), (1, W)), ALU.mult).then_inc(p3_ready, 1)
                else:
                    v.tensor_tensor(prod3[:, k:k + 2, :].rearrange("p k (h w) -> p k h w", w=W),
                                    view(ps[:, bank, 0:1], (HW, 2), (W, H), (1, W)),
                                    view(g3p[:, at[k]:at[k] + 1], (at[k + 1] - at[k], 2), (PAD, H), (1, W)),
                                    ALU.mult).then_inc(p3_ready, 1)
            v.wait_ge(p3_ready, 5)
            step(v.tensor_tensor(sum3[:, 1, :], prod3[:, 6, :], prod3[:, 7, :], ALU.add))
            v.wait_ge(s3_ready, 1)
            step(v.tensor_tensor(sum3[:, 2, :], sum3[:, 1, :], sum3[:, 0, :], ALU.add))
            v.wait_ge(acc3_done, 1)
            for pixels in HALVES:
                v.tensor_tensor(enh[:, pixels], ps[:, 1, pixels], sum3[:, 2, pixels], ALU.add).then_inc(enh_ready, 1)
            for n, pixels in enumerate(HALVES):
                v.wait_ge(h_done, 2 * n + 2)
                v.tensor_scalar(hff[:, 1, pixels], ps[:, H_BANKS[n][1], 0:P], par[:, FFN_B1:FFN_B1 + 1], 0.0,
                                ALU.add, ALU.max).then_inc(h_v, 1)
            v.wait_ge(xe_ready, 1)
            for n, pixels in enumerate(HALVES):
                v.wait_ge(ffn_done, n + 1)
                v.scalar_tensor_tensor(out=y[:, pixels], in0=ps[:, Y_BANKS[n], 0:P], scalar=par[:, FFN_B2:FFN_B2 + 1],
                                       in1=xe[:, pixels], op0=ALU.add, op1=ALU.add).then_inc(y_ready, 1)

        @block.tensor
        def _(t):
            def keep_warm(count, bank):
                for _ in range(count):
                    t.matmul(ps[:, bank, :], zeros[:, 0:P], zeros[:, :], start=True, stop=True)

            t.wait_ge(zeros_ready, 1)
            keep_warm(WARM[0], 7)
            t.wait_ge(ident_loaded, 16)
            t.wait_ge(par_loaded, 16)
            t.wait_ge(g0_ready, 1)
            for i in range(2):
                last = t.transpose(ps[:, 2, P * i:P * i + P], g0[:, P * i:P * i + P], ident[:, :])
            last.then_inc(g0_turned, 1)
            t.matmul(ps[0:Q, 0, 0:HW], par[:, W1R:W1R + RANK * B], g0[:, :], start=True,
                     stop=True).then_inc(f_done, 1)

            def filters(i):
                n = 2 if i < UNITS7 - 1 else 1
                out = ps[:, 3 + i, 0:n * HW].rearrange("p (r y x) -> p r y x", r=n, x=W)
                for half in range(2):
                    lo = 3 if half == 0 else 0
                    y0 = 0 if half == 0 else H - ROWS7
                    last = t.matmul(out[:, :, y0:y0 + ROWS7, :], g0t[:, half, :],
                                    taps7[:, 2 * i:2 * i + n, lo:lo + ROWS7, :],
                                    start=(half == 0), stop=(half == 1), skip_group_check=True)
                last.then_inc(filt_done, 1)

            def spread(i):
                if i == 3:
                    t.wait_ge(hid_ready, 1)
                for j in range(2):
                    r = 2 * i + j
                    last = t.matmul(ps[:, HID_BANKS[i], HW * j:HW * j + HW], sel0[:, P * r:P * r + P], fparts[:, :],
                                    start=True, stop=True)
                last.then_inc(hid_done, 1)

            t.wait_ge(g0t_ready, 1)
            t.wait_ge(taps_loaded, 16)
            filters(0)
            filters(1)
            t.wait_ge(fparts_ready, 1)
            t.wait_ge(sel0_loaded, 16)
            for i in range(3):
                spread(i)
            t.wait_ge(late_taps_loaded, 16)
            filters(2)
            spread(3)
            filters(3)
            filters(4)

            t.wait_ge(hid_ready, 4)
            keep_warm(WARM[1], 1)
            t.wait_ge(wa_loaded, 48)
            t.wait_ge(g1_laid, 3 * B)
            for dy in range(3):
                for b in range(B):
                    last = t.matmul(ps[Q * b:Q * b + Q, 0, 0:HW], wconv[:, C * dy:C * dy + C],
                                    g1x[:, b, W * dy:W * dy + HW], start=(dy == 0), stop=(dy == 2))
            last.then_inc(conv_done, 1)
            t.wait_ge(a1_ready, 1)
            for dx in (1, 0, 2):
                if dx == 0:
                    t.wait_ge(a1_right, 1)
                if dx == 2:
                    t.wait_ge(a1_left, 1)
                for dy in range(3):
                    col = W_OFF + OFFS * (3 * dy + dx)
                    for half in range(2):
                        at = (8 * half + dy) * W
                        for low in (0, 64):
                            last = t.matmul(ps[low:low + 64, 7, OFFS * half:OFFS * half + OFFS],
                                            a1x[:, dx, at + low:at + low + 64], wa[:, col:col + OFFS],
                                            start=(dx == 1 and dy == half == 0),
                                            stop=(dx == 2 and dy == 2), skip_group_check=True)
            last.then_inc(off_done, 1)

            def mix(n):
                half, c = n // 3, n % 3
                at = W + P * half
                t.matmul(ps[:, 1 + n, 0:384], a1x[:, 1, at:at + P],
                         wa[:, W_DEF + 384 * c:W_DEF + 384 * c + 384], start=True, stop=True).then_inc(mixed_done, 1)

            for n in range(6):
                mix(n)

            def drained(e):
                v_count = sum(d <= e for d in VECTOR_DRAINS)
                if e in VECTOR_DRAINS:
                    t.wait_ge(drained_v, v_count)
                else:
                    t.wait_ge(drained_a, e + 1 - v_count)

            def products_of(k, half):
                done = [(i, h) for i in range(k + 1) for h in range(2) if (i, h) <= (k, half)]
                pool = sum(u in POOL_UNITS for u in done)
                if (k, half) in POOL_UNITS:
                    t.wait_ge(prod_g, pool)
                else:
                    t.wait_ge(prod_v, len(done) - pool)

            def turn_hats(k, kb, pair, halves):
                e = 4 * k + 2 * kb + pair
                for i in range(2):
                    for half in halves:
                        last = t.transpose(ps[:, 1 + e % 6, HW * i + P * half:HW * i + P * half + P],
                                           st[:, k % 2, half, 2 * pair + i, P * kb:P * kb + P], ident[:, :])
                if 1 in halves:
                    last.then_inc(turned, 1)

            def sample(k):
                for kb in range(2):
                    for pair in range(2):
                        drained(4 * k + 2 * kb + pair)
                    for b in range(B):
                        col = TAPS * C * b + C * k
                        last = t.matmul(ps[Q * b:Q * b + Q, 0, 0:HW], mixed[:, kb, col:col + C],
                                        s[:, k % 2, kb, b, :], start=(k == 0 and kb == 0),
                                        stop=(k == TAPS - 1 and kb == 1))
                    last.then_inc(sampled, 1)

            t.wait_ge(mixed_ready, 4)
            for half in range(2):
                products_of(0, half)
                for kb in range(2):
                    for pair in range(2):
                        turn_hats(0, kb, pair, (half,))
            for k in range(1, TAPS):
                products_of(k, 0)
                products_of(k, 1)
                for kb in range(2):
                    for pair in range(2):
                        e = 4 * k + 2 * kb + pair
                        if e < 6:
                            t.wait_ge(mixed_ready, e + 1)
                        else:
                            drained(e - 6)
                        turn_hats(k, kb, pair, (0, 1))
                sample(k - 1)
            sample(TAPS - 1)

            t.wait_ge(r1_ready, 1)
            keep_warm(WARM[2], 7)
            t.wait_ge(band_doubled, STEPS // 5)
            for n in range(STEPS):
                tens = yt if n < STEPS // 2 else ytb
                for pair in range(2):
                    if n % (STEPS // 2) == 0:
                        t.wait_ge(y_laid[pair], 8 if n == 0 else 8 + 16)
                    else:
                        t.wait_ge(pair_updated[pair], updates(n))
                    for d in (0, -1, 1):
                        frm, to, count = max(d, 0), max(-d, 0), 4 - abs(d)
                        for low in (0, 64):
                            at = 4 * (1 - d) + low // Q
                            last = t.matmul(
                                ps[low:low + 64, pair, 0:2 * LANE].rearrange(
                                    "p (b n) -> p b n", b=2)[:, :, H * to:H * (to + count)],
                                wband[:, n, at:at + 2, :].rearrange("p a c -> p (a c)"),
                                tens[:, 2 * pair:2 * pair + 2, H * frm:H * (frm + count)],
                                start=(d == 0), stop=(d == 1), skip_group_check=True)
                    last.then_inc(z_done, 1)

            keep_warm(WARM[3], 7)
            t.wait_ge(g3_ready, 1)
            t.matmul(ps[:, 0, 0:HW], cst[:, C_AVG:C_AVG + P], g3v[:, 1:1 + H, 1:1 + W],
                     start=True, stop=True).then_inc(avg_done, 1)
            t.wait_ge(sq_ready, 1)
            t.matmul(ps[0:B, 7, 0:324], cst[:, C_NORM:C_NORM + B], maps[:, 0, :], start=True,
                     stop=True).then_inc(norms_done, 1)

            def dots(m):
                t.wait_ge(*((map_v, m + 1) if m < 3 else (map_g, 1)))
                off = (1, PAD - 1, PAD, PAD + 1)[m]
                return t.matmul(ps[0:DOTS * B, 1, 0:324 - off],
                                cst[:, C_DOTS + DOTS * B * m:C_DOTS + DOTS * B * (m + 1)],
                                maps[:, 1 + m, 0:324 - off], start=(m == 0), stop=(m == DOTS - 1),
                                skip_group_check=True)

            for m in range(DOTS_FIRST):
                dots(m)
            t.wait_ge(gn_in, 1)
            t.matmul(ps[:, 5, 0:1], cst[:, C_PAIR:C_PAIR + P], gn[:, 0:1], start=True,
                     stop=True).then_inc(gn_paired, 1)
            t.wait_ge(norms0_ready, 1)
            t.wait_ge(av_ready, 1)
            for k in range(KNN):
                for i in range(LINES):
                    at = LINE * i + k // 3 * PAD + k % 3
                    last = t.transpose(ps[0:LINE, 0, G * k + B * i:G * k + B * i + B], norms0[:, at:at + LINE],
                                       ident[0:B, 0:B])
            last.then_inc(norms_turned, 1)
            for m in range(DOTS_FIRST, DOTS):
                last = dots(m)
            last.then_inc(dots_done, 1)
            t.wait_ge(wc_loaded, 48)
            t.matmul(ps[0:LINE, 6, 0:KNN * G], cb[0:1, CB_ONE:CB_ONE + LINE], cb[0:1, CB_TAP:CB_TAP + KNN * G],
                     start=True, stop=False, skip_group_check=True)
            t.wait_ge(dots0_ready, 1)
            for k in range(DOTS + 1):
                for i in range(LINES):
                    at = LINE * i + k // 3 * PAD + k % 3
                    last = t.transpose(ps[0:LINE, 2, 48 * k + 16 * i:48 * k + 16 * i + 16], dots0[:, at:at + LINE],
                                       ident[0:DOTS * B, 0:DOTS * B])
            last.then_inc(dots_turned, 1)
            keep_warm(WARM[5], 7)
            for o in range(1, KNN):
                if o == 5:
                    t.wait_ge(kn_ready, 1)
                    for i in range(LINES):
                        t.matmul(view(ps[0:LINE, 6, B * i:B * i + 1], (G, KNN), (1, B)),
                                 kn[:, LINE * i:LINE * i + LINE], cb[:, CB_COUNT:CB_COUNT + KNN * B],
                                 start=False, stop=False, skip_group_check=True)
                t.wait_ge(above_ready, o)
                n = (KNN - o) * G
                for out, sign in ((0, CB_EYE), (o * G, CB_NEG)):
                    last = t.matmul(ps[0:LINE, 6, out:out + n], cb[0:LINE, sign:sign + LINE],
                                    above[:, o - 1, 0:KNN - o, :].rearrange("p k g -> p (k g)"),
                                    start=False, stop=(o == KNN - 1), skip_group_check=True)
            last.then_inc(rank_done, 1)
            keep_warm(WARM[4], 7)
            t.wait_ge(sim_ready, 1)
            t.wait_ge(wparts_ready, 1)
            for i in range(LINES):
                last = t.matmul(ps[0:PARTS3, 0, LINE * i:LINE * i + LINE],
                                wparts[:, i, :, :].rearrange("p a k -> p (a k)"), cb[0:LINE, CB_EYE:CB_EYE + LINE],
                                start=True, stop=True)
            last.then_inc(wparts_turned, 1)
            t.wait_ge(wrows_ready, 1)
            for bank, first in SPREAD3:
                for j in range(1 if first == 8 else 2):
                    at = P * (first + j)
                    last = t.matmul(ps[:, bank, HW * j:HW * j + HW], sel[:, at:at + P],
                                    view(wrows[:, 0:1], (PAD, H), (1, W)), start=True, stop=True)
                last.then_inc(wb_done, 1)
            for k in range(6):
                t.wait_ge(p3_ready, (1, 3, 4)[k // 2])
                last = t.matmul(ps[:, 1, 0:HW], ident[:, :], prod3[:, k, :], start=(k == 0), stop=(k == 5))
            last.then_inc(acc3_done, 1)
            for n, pixels in enumerate(HALVES):
                t.wait_ge(enh_ready, n + 1)
                for i in range(2):
                    t.matmul(ps[:, H_BANKS[n][i], 0:P], wc[:, P * i:P * i + P], enh[:, pixels], start=True,
                             stop=True).then_inc(h_done, 1)
            for n, pixels in enumerate(HALVES):
                for i, ready in ((0, h_a), (1, h_v)):
                    t.wait_ge(ready, n + 1)
                    last = t.matmul(ps[:, Y_BANKS[n], 0:P], wc[:, P * (2 + i):P * (3 + i)], hff[:, i, pixels],
                                    start=(i == 0), stop=(i == 1))
                last.then_inc(ffn_done, 1)


def kernel(**inputs):
    import ml_dtypes
    import numpy as np
    import concourse.bacc as bacc
    from concourse.bass_utils import run_bass_kernel_spmd

    f = {k: np.asarray(v) for k, v in inputs.items()}
    f32 = np.float32

    def per_channel(a):
        return np.tile(a, B)[:, None]

    def per_map(a):
        return np.concatenate([np.repeat(a, B), np.ones(P - RANK * B, f32)])[:, None]

    w1 = np.zeros((B, C, RANK, B), f32)
    for b in range(B):
        w1[b, :, :, b] = f['L0_conv_w1'].T
    off_b = np.repeat(f['L1_conv_off_b'], B)
    par = np.concatenate([
        np.concatenate([per_map(f['L0_conv_' + r]), per_channel(f['L1_conv_' + c1]),
                        per_channel(f['L1_conv_' + c2])], 1)
        for r, c1, c2 in (('bn_var', 'bn1_v', 'bn2_v'), ('bn_gamma', 'bn1_g', 'bn2_g'),
                          ('b1', 'conv1_b', 'dconv_b'), ('bn_mean', 'bn1_m', 'bn2_m'),
                          ('bn_beta', 'bn1_b', 'bn2_b'))
    ] + [w1.reshape(P, RANK * B), per_channel(f['L3_conv_gn_weight']),
         per_channel(f['L3_conv_gn_bias']), per_channel(f['L3_conv_b2']),
         np.tile(f['L3_conv_b1'], 2)[:, None],
         np.full((P, 1), 1e-5, f32), np.tile(off_b, (P, 1))], 1)

    filt = np.concatenate([f['L0_conv_b2'][:, None], f['L0_conv_w2']], 1).reshape(K7, K7, FILTERS)
    taps = np.zeros((8, W, FILTERS, HALO7, W), f32)
    for n in range(8):
        for x in range(W):
            for xo in range(max(0, x - 3), min(W, x + 4)):
                taps[n, x, :, n:n + K7, xo] = filt[::-1, x - xo + 3, :].T

    off = np.zeros((B, C, TAPS, TAPS, 2, B), f32)
    deform = np.zeros((B, C, B, TAPS, C), f32)
    for b in range(B):
        off[b, :, :, :, :, b] = f['L1_conv_off_w'].reshape(TAPS, 2, C, TAPS).transpose(2, 3, 0, 1)
        deform[b, :, b, :, :] = f['L1_conv_dconv_w'].reshape(C, C, TAPS).transpose(1, 2, 0)
    wa = np.concatenate([off.reshape(P, -1), deform.reshape(P, -1)], 1)
    wconv = f['L1_conv_conv1_w'].transpose(3, 1, 2, 0).reshape(3 * C, 3 * C)

    wb = np.concatenate([f['L2_conv_' + n].reshape(5, C, C, TAPS) for n in ('w_d', 'w_u', 'w_r', 'w_l')])
    wb = wb[:, :, :, ::-1].transpose(2, 0, 3, 1)

    wc = np.zeros((P, 4, P), f32)
    for b in range(B):
        i, j = b // 2, b % 2
        wc[C * b:C * b + C, i, 64 * j:64 * j + 64] = f['L3_conv_w1'].T
        wc[64 * j:64 * j + 64, 2 + i, C * b:C * b + C] = f['L3_conv_w2'].T

    part = np.arange(P)
    cst = np.zeros((P, NCST), f32)
    cst[:, C_AVG:C_AVG + P] = (part[:, None] // C == part[None, :] // C) / f32(C)
    cst[:, C_PAIR:C_PAIR + P] = (part[:, None] // 2 == part[None, :] // 2) / f32(2)
    cst[part, C_NORM + part // C] = 1
    for m in range(DOTS):
        cst[part, C_DOTS + DOTS * B * m + B * m + part // C] = 1
    base = np.zeros((P, 2, TAPS, 2, B), f32)
    for half in range(2):
        for k in range(TAPS):
            base[:, half, k, 0, :] = (8 * half + part // W - 1 + k // 3)[:, None]
            base[:, half, k, 1, :] = (part % W - 1 + k % 3)[:, None]
    cst[:, C_BASE:C_BASE + 2 * OFFS] = base.reshape(P, -1)
    cst[:, C_IOTA:C_IOTA + 16] = np.arange(16)
    sel = np.zeros((3, KNN, B, KNN, P), f32)
    for k in range(KNN):
        sel[:, k, part // C, k, part] = 1
    cb = np.zeros((P, NCB), f32)
    cb[:LINE, CB_EYE:CB_EYE + LINE] = np.eye(LINE)
    cb[:LINE, CB_NEG:CB_NEG + LINE] = -np.eye(LINE)
    for b in range(B):
        cb[C * b, CB_COUNT + b:CB_COUNT + KNN * B:B] = -1
    cb[0, CB_TAP:CB_TAP + KNN * G] = np.repeat(np.arange(KNN), G)
    cb[0, CB_ONE:CB_ONE + LINE] = 1

    sel0 = np.zeros((3, RANK * B, RANK, P), f32)
    for r in range(RANK):
        sel0[:, B * r + part // C, r, part] = 1

    arrays = {'x': f['x'].reshape(P, HW), 'par': par, 'ident': np.eye(P, dtype=f32),
              'taps': taps.reshape(P, FILTERS, HALO7, W), 'wconv': wconv, 'wa': wa, 'wb': wb,
              'wc': wc.reshape(P, -1), 'cst': cst}
    arrays = {f'in_{k}': np.ascontiguousarray(v, dtype=f32) for k, v in arrays.items()}
    for k, v in (('sel', sel.reshape(PARTS3, -1)), ('sel0', sel0.reshape(3 * Q, -1)), ('cb', cb)):
        arrays['in_' + k] = v.astype(ml_dtypes.bfloat16)
    nc = bacc.Bacc("TRN2", target_bir_lowering=False, num_devices=1)
    args = [nc.dram_tensor(k, a.shape, F32 if a.dtype == f32 else BF16, kind="ExternalInput").ap()
            for k, a in arrays.items()]
    out = nc.dram_tensor("out", (P, HW), F32, kind="ExternalOutput").ap()
    build(nc, *args, out)
    got = run_bass_kernel_spmd(nc, [arrays], core_ids=[0]).results[0]["out"]
    return got.reshape(B, C, H, W)
```
